# Optimizing a Trainium2 kernel written in Bass

```python
import numpy as np
import jax
import jax.numpy as jnp

def _softmax(x, axis=-1):
    return jax.nn.softmax(x, axis=axis)

def _gelu(x):
    return jax.nn.gelu(x, approximate=True)

def _silu(x):
    return jax.nn.silu(x)

def _sigmoid(x):
    return jax.nn.sigmoid(x)

def _layernorm(x, axis=-1, eps=1e-05):
    m = jnp.mean(x, axis=axis, keepdims=True)
    v = jnp.var(x, axis=axis, keepdims=True)
    return (x - m) / jnp.sqrt(v + eps)

def _scatter_add(tgt, idx, src, axis=0):
    return tgt.at[idx].add(src)

def _segment_sum(src, seg, n):
    return jax.ops.segment_sum(src, seg, n)
kernel_name = 'mk_hybrid_d2_jaxref_r8_7b93b3'

def setup_inputs(seed: int=0):
    np.random.seed(seed)
    _w = jnp.asarray

    def _L0_attn_a_setup():
        import jax, jax.numpy as jnp
        import numpy as np
        B, S, D, H, MLP = (2, 256, 128, 16, 512)
        DH = D // H
        EPS_LN = 1e-06
        KERNEL_EPS = 0.001

        def layer_norm(x, scale, bias):
            m = jnp.mean(x, axis=-1, keepdims=True)
            v = jnp.mean(jnp.square(x - m), axis=-1, keepdims=True)
            return (x - m) * jax.lax.rsqrt(v + EPS_LN) * scale + bias

        def performer_causal_attention(q, k, v):
            phi_q = jax.nn.relu(q) + KERNEL_EPS
            phi_k = jax.nn.relu(k) + KERNEL_EPS
            kv = jnp.cumsum(jnp.einsum('bshm,bshd->bshmd', phi_k, v), axis=1)
            num = jnp.einsum('bshm,bshmd->bshd', phi_q, kv)
            den = jnp.einsum('bshm,bshm->bsh', phi_q, jnp.cumsum(phi_k, axis=1))
            return num / den[..., None]
        key = jax.random.key(seed)
        ks = jax.random.split(key, 7)

        def w(k, shape, scale):
            return jax.random.normal(k, shape, jnp.float32) * scale
        s_in = 1.0 / np.sqrt(D)
        return {'inputs': jax.random.normal(ks[0], (B, S, D), jnp.float32), 'ln1_scale': jnp.ones((D,), jnp.float32), 'ln1_bias': jnp.zeros((D,), jnp.float32), 'wq': w(ks[1], (D, H, DH), s_in), 'wk': w(ks[2], (D, H, DH), s_in), 'wv': w(ks[3], (D, H, DH), s_in), 'wo': w(ks[4], (H, DH, D), s_in), 'ln2_scale': jnp.ones((D,), jnp.float32), 'ln2_bias': jnp.zeros((D,), jnp.float32), 'w1': w(ks[5], (D, MLP), s_in), 'b1': jnp.zeros((MLP,), jnp.float32), 'w2': w(ks[6], (MLP, D), 1.0 / np.sqrt(MLP)), 'b2': jnp.zeros((D,), jnp.float32)}
    _L0_attn_a_in = _L0_attn_a_setup()

    def _L0_attn_b_setup():
        import math
        import jax, jax.numpy as jnp
        import numpy as np
        D_MODEL = 128
        HEADS = 16
        DH = D_MODEL // HEADS
        MAX_REL = 128
        LN_EPS = 1e-05

        def _layernorm(x, gamma, beta):
            mu = jnp.mean(x, axis=-1, keepdims=True)
            var = jnp.mean(jnp.square(x - mu), axis=-1, keepdims=True)
            return (x - mu) * jax.lax.rsqrt(var + LN_EPS) * gamma + beta
        key = jax.random.key(seed)
        ks = jax.random.split(key, 6)
        B, T = (4, 256)
        scale = 1.0 / math.sqrt(D_MODEL)
        x = jax.random.normal(ks[0], (B, T, D_MODEL), dtype=jnp.float32)
        Wq = jax.random.normal(ks[1], (D_MODEL, D_MODEL), dtype=jnp.float32) * scale
        Wk = jax.random.normal(ks[2], (D_MODEL, D_MODEL), dtype=jnp.float32) * scale
        Wv = jax.random.normal(ks[3], (D_MODEL, D_MODEL), dtype=jnp.float32) * scale
        Wo = jax.random.normal(ks[4], (D_MODEL, D_MODEL), dtype=jnp.float32) * scale
        rel = jnp.tile(jnp.linspace(0.0, -2.0, MAX_REL + 1, dtype=jnp.float32)[None, :], (HEADS, 1))
        ln_gamma = jnp.ones((D_MODEL,), dtype=jnp.float32)
        ln_beta = jnp.zeros((D_MODEL,), dtype=jnp.float32)
        return {'x': x, 'Wq': Wq, 'Wk': Wk, 'Wv': Wv, 'Wo': Wo, 'rel': rel, 'ln_gamma': ln_gamma, 'ln_beta': ln_beta}
    _L0_attn_b_in = _L0_attn_b_setup()

    def _L0_ffn_setup():
        import jax, jax.numpy as jnp
        import numpy as np
        HIDDEN = 128
        N_ROUTED = 16
        N_SHARED = 2
        TOP_K = 2
        MID_R = HIDDEN // 4
        MID_S = HIDDEN // 2
        key = jax.random.key(seed)
        ks = jax.random.split(key, 8)
        s = 0.02
        return {'x': jax.random.normal(ks[0], (2, 128, HIDDEN), dtype=jnp.float32), 'router_w': jax.random.normal(ks[1], (HIDDEN, N_ROUTED), dtype=jnp.float32) * s, 'wg_r': jax.random.normal(ks[2], (N_ROUTED, HIDDEN, MID_R), dtype=jnp.float32) * s, 'wu_r': jax.random.normal(ks[3], (N_ROUTED, HIDDEN, MID_R), dtype=jnp.float32) * s, 'wd_r': jax.random.normal(ks[4], (N_ROUTED, MID_R, HIDDEN), dtype=jnp.float32) * s, 'wg_s': jax.random.normal(ks[5], (N_SHARED, HIDDEN, MID_S), dtype=jnp.float32) * s, 'wu_s': jax.random.normal(ks[6], (N_SHARED, HIDDEN, MID_S), dtype=jnp.float32) * s, 'wd_s': jax.random.normal(ks[7], (N_SHARED, MID_S, HIDDEN), dtype=jnp.float32) * s}
    _L0_ffn_in = _L0_ffn_setup()

    def _L1_attn_a_setup():
        import jax, jax.numpy as jnp
        import numpy as np
        B, S, E, H = (2, 256, 128, 16)
        D = E // H
        LN_EPS = 1e-05
        NORM_EPS = 1e-12
        ROPE_BASE = 10000.0

        def _rope(x, sin, cos):
            x1 = x[..., :-1:2]
            x2 = x[..., 1::2]
            x_rot = jnp.concatenate((-x2, x1), axis=-1)
            return x * cos + x_rot * sin

        def _l2norm(t):
            n = jnp.linalg.norm(t, axis=-1, keepdims=True)
            return t / jnp.maximum(n, NORM_EPS)

        def _forward(x, ln_gamma, ln_beta, w_qkv, w_out, qkscale):
            b, s, e = x.shape
            mu = jnp.mean(x, axis=-1, keepdims=True)
            var = jnp.mean((x - mu) ** 2, axis=-1, keepdims=True)
            h = (x - mu) / jnp.sqrt(var + LN_EPS) * ln_gamma + ln_beta
            qkv = h @ w_qkv
            q, k, v = jnp.split(qkv, 3, axis=-1)
            inv = ROPE_BASE ** (-(jnp.arange(0, e, 2, dtype=jnp.float32) / e))
            emb = jnp.repeat(inv, 2)
            sin, cos = (jnp.sin(s * emb), jnp.cos(s * emb))
            q = _rope(q, sin, cos)
            k = _rope(k, sin, cos)

            def split(t):
                return t.reshape(b, s, H, D).transpose(0, 2, 1, 3)
            q, k, v = (split(q), split(k), split(v))
            qn = _l2norm(q)
            kn = _l2norm(k)
            scores = jnp.einsum('bhqd,bhkd->bhqk', qn, kn) * qkscale
            causal = jnp.tril(jnp.ones((s, s), bool))
            scores = jnp.where(causal, scores, jnp.finfo(scores.dtype).min)
            attn = jax.nn.softmax(scores, axis=-1)
            o = jnp.einsum('bhqk,bhkd->bhqd', attn, v)
            o = o.transpose(0, 2, 1, 3).reshape(b, s, e)
            return o @ w_out
        key = jax.random.key(seed)
        k0, k1, k2 = jax.random.split(key, 3)
        x = jax.random.normal(k0, (B, S, E), jnp.float32)
        w_qkv = jax.random.normal(k1, (E, 3 * E), jnp.float32) * 0.02
        w_out = jax.random.normal(k2, (E, E), jnp.float32) * 0.02
        return {'x': x, 'ln_gamma': jnp.ones((E,), jnp.float32), 'ln_beta': jnp.zeros((E,), jnp.float32), 'w_qkv': w_qkv, 'w_out': w_out, 'qkscale': jnp.asarray(E ** (-0.5), jnp.float32)}
    _L1_attn_a_in = _L1_attn_a_setup()

    def _L1_attn_b_setup():
        import jax, jax.numpy as jnp
        import numpy as np
        D_MODEL = 128
        NUM_HEADS = 16
        HEAD_DIM = D_MODEL // NUM_HEADS
        ROPE_THETA = 10000.0

        def apply_rope(x):
            S, d_k = (x.shape[-2], x.shape[-1])
            inv_freq = ROPE_THETA ** (jnp.arange(0, d_k, 2, dtype=jnp.float32) / d_k)
            ang = jnp.arange(S, dtype=jnp.float32)[:, None] / inv_freq[None, :]
            cos, sin = (jnp.cos(ang), jnp.sin(ang))
            xp = x.reshape(x.shape[:-1] + (d_k // 2, 2))
            x0, x1 = (xp[..., 0], xp[..., 1])
            out = jnp.stack([x0 * cos - x1 * sin, x0 * sin + x1 * cos], axis=-1)
            return out.reshape(x.shape)
        key = jax.random.key(seed)
        k1, k2, k3 = jax.random.split(key, 3)
        B, S = (2, 256)
        std = 2.0 / (D_MODEL + 3 * D_MODEL)
        std_o = 2.0 / (D_MODEL + D_MODEL)
        return {'x': jax.random.normal(k1, (B, S, D_MODEL), dtype=jnp.float32), 'W_qkv': jax.random.normal(k2, (3 * D_MODEL, D_MODEL), dtype=jnp.float32) * std, 'W_o': jax.random.normal(k3, (D_MODEL, D_MODEL), dtype=jnp.float32) * std_o}
    _L1_attn_b_in = _L1_attn_b_setup()

    def _L1_ffn_setup():
        import jax, jax.numpy as jnp
        import numpy as np
        DIM = 128
        DEPTH = 6
        HEADS = 16
        DIM_HEAD = 64
        WINDOW = 32
        INNER = HEADS * DIM_HEAD
        DIM_INNER = int(DIM * 4 * 2 / 3)
        QK_SCALE = 8.0

        def shift_tokens(t):
            a, s = jnp.split(t, 2, -1)
            s = jnp.pad(s, ((0, 0), (1, 0), (0, 0)))[:, :-1]
            return jnp.concatenate([a, s], -1)

        def l2norm(t):
            return t / jnp.maximum(jnp.linalg.norm(t, axis=-1, keepdims=True), 1e-12)

        def rotate_half(x):
            x1, x2 = jnp.split(x, 2, -1)
            return jnp.concatenate([-x2, x1], -1)

        def rotary_tables(n):
            half = jnp.arange(0, DIM_HEAD, 2, dtype=jnp.float32)
            inv_freq = 1.0 / 10000.0 ** (half / DIM_HEAD)
            t = jnp.arange(n, dtype=jnp.float32)
            freqs = t[:, None] * inv_freq[None, :]
            freqs = jnp.concatenate([freqs, freqs], -1)
            base_scale = (half + 0.4 * DIM_HEAD) / (1.4 * DIM_HEAD)
            power = (t - n // 2) / (WINDOW // 2)
            scale = base_scale[None, :] ** power[:, None]
            scale = jnp.concatenate([scale, scale], -1)
            return (freqs, scale)

        def local_attention(q, k, v):
            b, h, n, d = q.shape
            w = WINDOW
            nw = n // w
            bq = q.reshape(b, h, nw, w, d)
            bk = k.reshape(b, h, nw, w, d)
            bv = v.reshape(b, h, nw, w, d)

            def look(t):
                p = jnp.pad(t, ((0, 0), (0, 0), (1, 0), (0, 0), (0, 0)))
                return jnp.concatenate([p[:, :, :nw], p[:, :, 1:]], axis=3)
            bk2, bv2 = (look(bk), look(bv))
            seq = jnp.arange(n).reshape(nw, w)
            seq_p = jnp.pad(seq, ((1, 0), (0, 0)), constant_values=-1)
            jt = jnp.concatenate([seq_p[:nw], seq_p[1:]], axis=1)
            it = seq[:, :, None]
            jb = jt[:, None, :]
            mask = (it < jb) | (it > jb + w) | (jb == -1)
            sim = jnp.einsum('bhwie,bhwje->bhwij', bq, bk2) * QK_SCALE
            sim = jnp.where(mask, -jnp.finfo(sim.dtype).max, sim)
            attn = jax.nn.softmax(sim, -1)
            out = jnp.einsum('bhwij,bhwje->bhwie', attn, bv2)
            return out.reshape(b, h, n, d)

        def attn_layer(x, Wqkv, qs, ksc, Wo):
            b, n, _ = x.shape
            qkv = x @ Wqkv
            q, k, v = jnp.split(qkv, 3, -1)
            sh = lambda t: t.reshape(b, n, HEADS, DIM_HEAD).transpose(0, 2, 1, 3)
            q, k, v = (sh(q), sh(k), sh(v))
            q = l2norm(q) * qs
            k = l2norm(k) * ksc
            freqs, scale = rotary_tables(n)
            cos, sin = (jnp.cos(freqs), jnp.sin(freqs))
            q = q * cos * scale + rotate_half(q) * sin * scale
            inv = 1.0 / scale
            k = k * cos * inv + rotate_half(k) * sin * inv
            out = local_attention(q, k, v)
            out = out.transpose(0, 2, 1, 3).reshape(b, n, INNER)
            return out @ Wo

        def ffn_layer(x, g, bln, W1, b1, W2, b2):
            mu = x.mean(-1, keepdims=True)
            var = ((x - mu) ** 2).mean(-1, keepdims=True)
            xn = (x - mu) / jnp.sqrt(var + 1e-05) * g + bln
            hg = xn @ W1 + b1
            a, gate = jnp.split(hg, 2, -1)
            return a * jax.nn.gelu(gate, approximate=False) @ W2 + b2
        key = jax.random.key(seed)
        ks = jax.random.split(key, 8)
        B, N = (2, 256)
        init = lambda k, shape: jax.random.normal(k, shape, jnp.float32) * 0.02
        return {'x': jax.random.normal(ks[0], (B, N, DIM), jnp.float32), 'Wqkv': init(ks[1], (DEPTH, DIM, 3 * INNER)), 'q_scale': jnp.ones((DEPTH, DIM_HEAD), jnp.float32), 'k_scale': jnp.ones((DEPTH, DIM_HEAD), jnp.float32), 'Wo': init(ks[2], (DEPTH, INNER, DIM)), 'ln_g': jnp.ones((DEPTH, DIM), jnp.float32), 'ln_b': jnp.zeros((DEPTH, DIM), jnp.float32), 'W1': init(ks[3], (DEPTH, DIM, 2 * DIM_INNER)), 'b1': jnp.zeros((DEPTH, 2 * DIM_INNER), jnp.float32), 'W2': init(ks[4], (DEPTH, DIM_INNER, DIM)), 'b2': jnp.zeros((DEPTH, DIM), jnp.float32)}
    _L1_ffn_in = _L1_ffn_setup()
    _d = {'L0_attn_a_inputs': _L0_attn_a_in['inputs'], 'L0_attn_a_ln1_scale': _L0_attn_a_in['ln1_scale'], 'L0_attn_a_ln1_bias': _L0_attn_a_in['ln1_bias'], 'L0_attn_a_wq': _L0_attn_a_in['wq'], 'L0_attn_a_wk': _L0_attn_a_in['wk'], 'L0_attn_a_wv': _L0_attn_a_in['wv'], 'L0_attn_a_wo': _L0_attn_a_in['wo'], 'L0_attn_a_ln2_scale': _L0_attn_a_in['ln2_scale'], 'L0_attn_a_ln2_bias': _L0_attn_a_in['ln2_bias'], 'L0_attn_a_w1': _L0_attn_a_in['w1'], 'L0_attn_a_b1': _L0_attn_a_in['b1'], 'L0_attn_a_w2': _L0_attn_a_in['w2'], 'L0_attn_a_b2': _L0_attn_a_in['b2'], 'L0_attn_b_Wq': _L0_attn_b_in['Wq'], 'L0_attn_b_Wk': _L0_attn_b_in['Wk'], 'L0_attn_b_Wv': _L0_attn_b_in['Wv'], 'L0_attn_b_Wo': _L0_attn_b_in['Wo'], 'L0_attn_b_rel': _L0_attn_b_in['rel'], 'L0_attn_b_ln_gamma': _L0_attn_b_in['ln_gamma'], 'L0_attn_b_ln_beta': _L0_attn_b_in['ln_beta'], 'L0_ffn_router_w': _L0_ffn_in['router_w'], 'L0_ffn_wg_r': _L0_ffn_in['wg_r'], 'L0_ffn_wu_r': _L0_ffn_in['wu_r'], 'L0_ffn_wd_r': _L0_ffn_in['wd_r'], 'L0_ffn_wg_s': _L0_ffn_in['wg_s'], 'L0_ffn_wu_s': _L0_ffn_in['wu_s'], 'L0_ffn_wd_s': _L0_ffn_in['wd_s'], 'L1_attn_a_ln_gamma': _L1_attn_a_in['ln_gamma'], 'L1_attn_a_ln_beta': _L1_attn_a_in['ln_beta'], 'L1_attn_a_w_qkv': _L1_attn_a_in['w_qkv'], 'L1_attn_a_w_out': _L1_attn_a_in['w_out'], 'L1_attn_a_qkscale': _L1_attn_a_in['qkscale'], 'L1_attn_b_W_qkv': _L1_attn_b_in['W_qkv'], 'L1_attn_b_W_o': _L1_attn_b_in['W_o'], 'L1_ffn_Wqkv': _L1_ffn_in['Wqkv'], 'L1_ffn_q_scale': _L1_ffn_in['q_scale'], 'L1_ffn_k_scale': _L1_ffn_in['k_scale'], 'L1_ffn_Wo': _L1_ffn_in['Wo'], 'L1_ffn_ln_g': _L1_ffn_in['ln_g'], 'L1_ffn_ln_b': _L1_ffn_in['ln_b'], 'L1_ffn_W1': _L1_ffn_in['W1'], 'L1_ffn_b1': _L1_ffn_in['b1'], 'L1_ffn_W2': _L1_ffn_in['W2'], 'L1_ffn_b2': _L1_ffn_in['b2']}
    _x0 = _d['L0_attn_a_inputs']
    _d['L0_attn_a_inputs'] = jax.random.normal(jax.random.fold_in(jax.random.key(seed), 1), (1, 2048, 128), dtype=_x0.dtype)
    del _x0
    return _d

def reference(L0_attn_a_inputs, L0_attn_a_ln1_scale, L0_attn_a_ln1_bias, L0_attn_a_wq, L0_attn_a_wk, L0_attn_a_wv, L0_attn_a_wo, L0_attn_a_ln2_scale, L0_attn_a_ln2_bias, L0_attn_a_w1, L0_attn_a_b1, L0_attn_a_w2, L0_attn_a_b2, L0_attn_b_Wq, L0_attn_b_Wk, L0_attn_b_Wv, L0_attn_b_Wo, L0_attn_b_rel, L0_attn_b_ln_gamma, L0_attn_b_ln_beta, L0_ffn_router_w, L0_ffn_wg_r, L0_ffn_wu_r, L0_ffn_wd_r, L0_ffn_wg_s, L0_ffn_wu_s, L0_ffn_wd_s, L1_attn_a_ln_gamma, L1_attn_a_ln_beta, L1_attn_a_w_qkv, L1_attn_a_w_out, L1_attn_a_qkscale, L1_attn_b_W_qkv, L1_attn_b_W_o, L1_ffn_Wqkv, L1_ffn_q_scale, L1_ffn_k_scale, L1_ffn_Wo, L1_ffn_ln_g, L1_ffn_ln_b, L1_ffn_W1, L1_ffn_b1, L1_ffn_W2, L1_ffn_b2):

    def _L0_attn_a_ref(inputs, ln1_scale, ln1_bias, wq, wk, wv, wo, ln2_scale, ln2_bias, w1, b1, w2, b2):
        import jax, jax.numpy as jnp
        import numpy as np
        B, S, D, H, MLP = (2, 256, 128, 16, 512)
        DH = D // H
        EPS_LN = 1e-06
        KERNEL_EPS = 0.001

        def layer_norm(x, scale, bias):
            m = jnp.mean(x, axis=-1, keepdims=True)
            v = jnp.mean(jnp.square(x - m), axis=-1, keepdims=True)
            return (x - m) * jax.lax.rsqrt(v + EPS_LN) * scale + bias

        def performer_causal_attention(q, k, v):
            phi_q = jax.nn.relu(q) + KERNEL_EPS
            phi_k = jax.nn.relu(k) + KERNEL_EPS
            kv = jnp.cumsum(jnp.einsum('bshm,bshd->bshmd', phi_k, v), axis=1)
            num = jnp.einsum('bshm,bshmd->bshd', phi_q, kv)
            den = jnp.einsum('bshm,bshm->bsh', phi_q, jnp.cumsum(phi_k, axis=1))
            return num / den[..., None]
        x = layer_norm(inputs, ln1_scale, ln1_bias)
        q = jnp.einsum('bsd,dhm->bshm', x, wq)
        k = jnp.einsum('bsd,dhm->bshm', x, wk)
        v = jnp.einsum('bsd,dhm->bshm', x, wv)
        attn = performer_causal_attention(q, k, v)
        attn_out = jnp.einsum('bshm,hmd->bsd', attn, wo)
        x = attn_out + inputs
        y = layer_norm(x, ln2_scale, ln2_bias)
        y = jax.nn.gelu(y @ w1 + b1) @ w2 + b2
        return x + y

    def _L0_attn_b_ref(x, Wq, Wk, Wv, Wo, rel, ln_gamma, ln_beta):
        import math
        import jax, jax.numpy as jnp
        import numpy as np
        D_MODEL = 128
        HEADS = 16
        DH = D_MODEL // HEADS
        MAX_REL = 128
        LN_EPS = 1e-05

        def _layernorm(x, gamma, beta):
            mu = jnp.mean(x, axis=-1, keepdims=True)
            var = jnp.mean(jnp.square(x - mu), axis=-1, keepdims=True)
            return (x - mu) * jax.lax.rsqrt(var + LN_EPS) * gamma + beta
        B, T, D = x.shape
        x0 = x
        xn = _layernorm(x, ln_gamma, ln_beta)

        def proj(W):
            return (xn @ W.T).reshape(B, T, HEADS, DH).transpose(0, 2, 1, 3)
        q = proj(Wq) / math.sqrt(DH)
        k = proj(Wk)
        v = proj(Wv)
        scores = jnp.einsum('bhid,bhjd->bhij', q, k)
        i = jnp.arange(T)
        dist = jnp.clip(i[:, None] - i[None, :], 0, MAX_REL)
        bias = rel[:, dist]
        scores = scores + bias[None]
        causal = i[:, None] >= i[None, :]
        scores = jnp.where(causal[None, None], scores, -jnp.inf)
        attn = jax.nn.softmax(scores, axis=-1)
        y = jnp.einsum('bhij,bhjd->bhid', attn, v)
        y = y.transpose(0, 2, 1, 3).reshape(B, T, D)
        y = y @ Wo.T
        return x0 + y

    def _L0_ffn_ref(x, router_w, wg_r, wu_r, wd_r, wg_s, wu_s, wd_s):
        import jax, jax.numpy as jnp
        import numpy as np
        HIDDEN = 128
        N_ROUTED = 16
        N_SHARED = 2
        TOP_K = 2
        MID_R = HIDDEN // 4
        MID_S = HIDDEN // 2
        orig_shape = x.shape
        flat = x.reshape(-1, orig_shape[-1])
        gs = jnp.einsum('td,ndm->tnm', flat, wg_s)
        us = jnp.einsum('td,ndm->tnm', flat, wu_s)
        out = jnp.einsum('tnm,nmd->td', jax.nn.silu(gs) * us, wd_s)
        logits = (flat @ router_w).astype(jnp.float32)
        probs = jax.nn.softmax(logits, axis=-1)
        weights, indices = jax.lax.top_k(probs, TOP_K)
        weights = weights / (weights.sum(axis=-1, keepdims=True) + 1e-09)
        weights = weights.astype(x.dtype)
        comb = jnp.sum(jax.nn.one_hot(indices, N_ROUTED, dtype=x.dtype) * weights[..., None], axis=1)
        g = jnp.einsum('td,edm->tem', flat, wg_r)
        u = jnp.einsum('td,edm->tem', flat, wu_r)
        h = jax.nn.silu(g) * u
        h = h * comb[:, :, None]
        out = out + jnp.einsum('tem,emd->td', h, wd_r)
        return out.reshape(orig_shape)

    def _L1_attn_a_ref(x, ln_gamma, ln_beta, w_qkv, w_out, qkscale):
        import jax, jax.numpy as jnp
        import numpy as np
        B, S, E, H = (2, 256, 128, 16)
        D = E // H
        LN_EPS = 1e-05
        NORM_EPS = 1e-12
        ROPE_BASE = 10000.0

        def _rope(x, sin, cos):
            x1 = x[..., :-1:2]
            x2 = x[..., 1::2]
            x_rot = jnp.concatenate((-x2, x1), axis=-1)
            return x * cos + x_rot * sin

        def _l2norm(t):
            n = jnp.linalg.norm(t, axis=-1, keepdims=True)
            return t / jnp.maximum(n, NORM_EPS)

        def _forward(x, ln_gamma, ln_beta, w_qkv, w_out, qkscale):
            b, s, e = x.shape
            mu = jnp.mean(x, axis=-1, keepdims=True)
            var = jnp.mean((x - mu) ** 2, axis=-1, keepdims=True)
            h = (x - mu) / jnp.sqrt(var + LN_EPS) * ln_gamma + ln_beta
            qkv = h @ w_qkv
            q, k, v = jnp.split(qkv, 3, axis=-1)
            inv = ROPE_BASE ** (-(jnp.arange(0, e, 2, dtype=jnp.float32) / e))
            emb = jnp.repeat(inv, 2)
            sin, cos = (jnp.sin(s * emb), jnp.cos(s * emb))
            q = _rope(q, sin, cos)
            k = _rope(k, sin, cos)

            def split(t):
                return t.reshape(b, s, H, D).transpose(0, 2, 1, 3)
            q, k, v = (split(q), split(k), split(v))
            qn = _l2norm(q)
            kn = _l2norm(k)
            scores = jnp.einsum('bhqd,bhkd->bhqk', qn, kn) * qkscale
            causal = jnp.tril(jnp.ones((s, s), bool))
            scores = jnp.where(causal, scores, jnp.finfo(scores.dtype).min)
            attn = jax.nn.softmax(scores, axis=-1)
            o = jnp.einsum('bhqk,bhkd->bhqd', attn, v)
            o = o.transpose(0, 2, 1, 3).reshape(b, s, e)
            return o @ w_out
        return _forward(x, ln_gamma, ln_beta, w_qkv, w_out, qkscale)

    def _L1_attn_b_ref(x, W_qkv, W_o):
        import jax, jax.numpy as jnp
        import numpy as np
        D_MODEL = 128
        NUM_HEADS = 16
        HEAD_DIM = D_MODEL // NUM_HEADS
        ROPE_THETA = 10000.0

        def apply_rope(x):
            S, d_k = (x.shape[-2], x.shape[-1])
            inv_freq = ROPE_THETA ** (jnp.arange(0, d_k, 2, dtype=jnp.float32) / d_k)
            ang = jnp.arange(S, dtype=jnp.float32)[:, None] / inv_freq[None, :]
            cos, sin = (jnp.cos(ang), jnp.sin(ang))
            xp = x.reshape(x.shape[:-1] + (d_k // 2, 2))
            x0, x1 = (xp[..., 0], xp[..., 1])
            out = jnp.stack([x0 * cos - x1 * sin, x0 * sin + x1 * cos], axis=-1)
            return out.reshape(x.shape)
        B, S, d_model = x.shape
        H, d_k = (NUM_HEADS, HEAD_DIM)
        qkv = jnp.einsum('bsi,oi->bso', x, W_qkv)
        Q, K, V = jnp.split(qkv, 3, axis=-1)

        def to_heads(t):
            return t.reshape(B, S, H, d_k).transpose(0, 2, 1, 3)
        Q, K, V = (to_heads(Q), to_heads(K), to_heads(V))
        Q, K = (apply_rope(Q), apply_rope(K))
        scores = jnp.einsum('bhqd,bhkd->bhqk', Q, K) / jnp.sqrt(jnp.float32(d_k))
        causal = jnp.tril(jnp.ones((S, S), dtype=bool))
        scores = jnp.where(causal, scores, -jnp.inf)
        attn = jax.nn.softmax(scores, axis=-1)
        out = jnp.einsum('bhqk,bhkd->bhqd', attn, V)
        out = out.transpose(0, 2, 1, 3).reshape(B, S, d_model)
        return jnp.einsum('bsi,oi->bso', out, W_o)

    def _L1_ffn_ref(x, Wqkv, q_scale, k_scale, Wo, ln_g, ln_b, W1, b1, W2, b2):
        import jax, jax.numpy as jnp
        import numpy as np
        DIM = 128
        DEPTH = 6
        HEADS = 16
        DIM_HEAD = 64
        WINDOW = 32
        INNER = HEADS * DIM_HEAD
        DIM_INNER = int(DIM * 4 * 2 / 3)
        QK_SCALE = 8.0

        def shift_tokens(t):
            a, s = jnp.split(t, 2, -1)
            s = jnp.pad(s, ((0, 0), (1, 0), (0, 0)))[:, :-1]
            return jnp.concatenate([a, s], -1)

        def l2norm(t):
            return t / jnp.maximum(jnp.linalg.norm(t, axis=-1, keepdims=True), 1e-12)

        def rotate_half(x):
            x1, x2 = jnp.split(x, 2, -1)
            return jnp.concatenate([-x2, x1], -1)

        def rotary_tables(n):
            half = jnp.arange(0, DIM_HEAD, 2, dtype=jnp.float32)
            inv_freq = 1.0 / 10000.0 ** (half / DIM_HEAD)
            t = jnp.arange(n, dtype=jnp.float32)
            freqs = t[:, None] * inv_freq[None, :]
            freqs = jnp.concatenate([freqs, freqs], -1)
            base_scale = (half + 0.4 * DIM_HEAD) / (1.4 * DIM_HEAD)
            power = (t - n // 2) / (WINDOW // 2)
            scale = base_scale[None, :] ** power[:, None]
            scale = jnp.concatenate([scale, scale], -1)
            return (freqs, scale)

        def local_attention(q, k, v):
            b, h, n, d = q.shape
            w = WINDOW
            nw = n // w
            bq = q.reshape(b, h, nw, w, d)
            bk = k.reshape(b, h, nw, w, d)
            bv = v.reshape(b, h, nw, w, d)

            def look(t):
                p = jnp.pad(t, ((0, 0), (0, 0), (1, 0), (0, 0), (0, 0)))
                return jnp.concatenate([p[:, :, :nw], p[:, :, 1:]], axis=3)
            bk2, bv2 = (look(bk), look(bv))
            seq = jnp.arange(n).reshape(nw, w)
            seq_p = jnp.pad(seq, ((1, 0), (0, 0)), constant_values=-1)
            jt = jnp.concatenate([seq_p[:nw], seq_p[1:]], axis=1)
            it = seq[:, :, None]
            jb = jt[:, None, :]
            mask = (it < jb) | (it > jb + w) | (jb == -1)
            sim = jnp.einsum('bhwie,bhwje->bhwij', bq, bk2) * QK_SCALE
            sim = jnp.where(mask, -jnp.finfo(sim.dtype).max, sim)
            attn = jax.nn.softmax(sim, -1)
            out = jnp.einsum('bhwij,bhwje->bhwie', attn, bv2)
            return out.reshape(b, h, n, d)

        def attn_layer(x, Wqkv, qs, ksc, Wo):
            b, n, _ = x.shape
            qkv = x @ Wqkv
            q, k, v = jnp.split(qkv, 3, -1)
            sh = lambda t: t.reshape(b, n, HEADS, DIM_HEAD).transpose(0, 2, 1, 3)
            q, k, v = (sh(q), sh(k), sh(v))
            q = l2norm(q) * qs
            k = l2norm(k) * ksc
            freqs, scale = rotary_tables(n)
            cos, sin = (jnp.cos(freqs), jnp.sin(freqs))
            q = q * cos * scale + rotate_half(q) * sin * scale
            inv = 1.0 / scale
            k = k * cos * inv + rotate_half(k) * sin * inv
            out = local_attention(q, k, v)
            out = out.transpose(0, 2, 1, 3).reshape(b, n, INNER)
            return out @ Wo

        def ffn_layer(x, g, bln, W1, b1, W2, b2):
            mu = x.mean(-1, keepdims=True)
            var = ((x - mu) ** 2).mean(-1, keepdims=True)
            xn = (x - mu) / jnp.sqrt(var + 1e-05) * g + bln
            hg = xn @ W1 + b1
            a, gate = jnp.split(hg, 2, -1)
            return a * jax.nn.gelu(gate, approximate=False) @ W2 + b2
        for i in range(DEPTH):
            x = attn_layer(shift_tokens(x), Wqkv[i], q_scale[i], k_scale[i], Wo[i]) + x
            x = ffn_layer(shift_tokens(x), ln_g[i], ln_b[i], W1[i], b1[i], W2[i], b2[i]) + x
        return x
    x = L0_attn_a_inputs
    x = x + _L0_attn_a_ref(_layernorm(x, axis=-1), L0_attn_a_ln1_scale, L0_attn_a_ln1_bias, L0_attn_a_wq, L0_attn_a_wk, L0_attn_a_wv, L0_attn_a_wo, L0_attn_a_ln2_scale, L0_attn_a_ln2_bias, L0_attn_a_w1, L0_attn_a_b1, L0_attn_a_w2, L0_attn_a_b2)
    x = x + _L0_ffn_ref(_layernorm(x, axis=-1), L0_ffn_router_w, L0_ffn_wg_r, L0_ffn_wu_r, L0_ffn_wd_r, L0_ffn_wg_s, L0_ffn_wu_s, L0_ffn_wd_s)
    x = x + _L0_attn_b_ref(_layernorm(x, axis=-1), L0_attn_b_Wq, L0_attn_b_Wk, L0_attn_b_Wv, L0_attn_b_Wo, L0_attn_b_rel, L0_attn_b_ln_gamma, L0_attn_b_ln_beta)
    x = x + _L0_ffn_ref(_layernorm(x, axis=-1), L0_ffn_router_w, L0_ffn_wg_r, L0_ffn_wu_r, L0_ffn_wd_r, L0_ffn_wg_s, L0_ffn_wu_s, L0_ffn_wd_s)
    x = x + _L1_attn_a_ref(_layernorm(x, axis=-1), L1_attn_a_ln_gamma, L1_attn_a_ln_beta, L1_attn_a_w_qkv, L1_attn_a_w_out, L1_attn_a_qkscale)
    x = x + _L1_ffn_ref(_layernorm(x, axis=-1), L1_ffn_Wqkv, L1_ffn_q_scale, L1_ffn_k_scale, L1_ffn_Wo, L1_ffn_ln_g, L1_ffn_ln_b, L1_ffn_W1, L1_ffn_b1, L1_ffn_W2, L1_ffn_b2)
    x = x + _L1_attn_b_ref(_layernorm(x, axis=-1), L1_attn_b_W_qkv, L1_attn_b_W_o)
    x = x + _L1_ffn_ref(_layernorm(x, axis=-1), L1_ffn_Wqkv, L1_ffn_q_scale, L1_ffn_k_scale, L1_ffn_Wo, L1_ffn_ln_g, L1_ffn_ln_b, L1_ffn_W1, L1_ffn_b1, L1_ffn_W2, L1_ffn_b2)
    return x

_drawn_inputs = setup_inputs


def setup_inputs(seed=0):
    import zlib

    import numpy as np

    out = dict(_drawn_inputs(seed))
    spreads = {'L0_attn_a_ln1_scale': (1.0, 0.6),
     'L0_attn_a_ln1_bias': (0.0, 0.1),
     'L0_attn_a_ln2_scale': (1.0, 0.2),
     'L0_attn_a_ln2_bias': (0.0, 0.1),
     'L0_attn_a_b1': (0.0, 0.1),
     'L0_attn_a_b2': (0.0, 0.1),
     'L0_attn_b_ln_gamma': (1.0, 0.6),
     'L0_attn_b_ln_beta': (0.0, 0.1),
     'L1_attn_a_ln_gamma': (1.0, 0.6),
     'L1_attn_a_ln_beta': (0.0, 0.8),
     'L1_ffn_q_scale': (1.0, 0.6),
     'L1_ffn_k_scale': (1.0, 0.6),
     'L1_ffn_ln_g': (1.0, 0.6),
     'L1_ffn_ln_b': (0.0, 0.8),
     'L1_ffn_b1': (0.0, 0.8),
     'L1_ffn_b2': (0.0, 0.1)}
    factors = {'L0_attn_b_rel': 3.626,
     'L0_ffn_router_w': 8.0,
     'L0_ffn_wg_r': 8.0,
     'L0_ffn_wu_r': 8.0,
     'L0_ffn_wd_r': 8.0,
     'L0_ffn_wg_s': 8.0,
     'L0_ffn_wu_s': 8.0,
     'L0_ffn_wd_s': 8.0,
     'L1_attn_a_w_qkv': 8.0,
     'L1_attn_a_w_out': 8.0,
     'L1_attn_b_W_qkv': 51.337,
     'L1_attn_b_W_o': 49.242,
     'L1_ffn_W1': 4.211,
     'L1_ffn_W2': 4.126}
    for name, (base, spread) in spreads.items():
        noise = np.random.default_rng([zlib.crc32(name.encode()), seed]).standard_normal(out[name].shape)
        drawn = base * np.exp(spread * noise) if base else spread * noise
        out[name] = jnp.asarray(drawn.astype(out[name].dtype))
    for name, factor in factors.items():
        out[name] = (out[name] * factor).astype(out[name].dtype)
    return out
```

```python
import itertools
from contextlib import ExitStack, contextmanager

import numpy as np

import concourse.bass as bass
from concourse import mybir

F32 = mybir.dt.float32
BF16 = mybir.dt.bfloat16
U32 = mybir.dt.uint32
ALU = mybir.AluOpType
ACT = mybir.ActivationFunctionType
AX = mybir.AxisListType

P = 128
T = 2048
NT = T // P
GW = 512
NG = T // GW
H = 16
DH = P // H
QUADS = H // 4
VW = DH + 1
NEG = -1e30

E = 16
LAYERS = 6
LH = 16
LD = 64
INNER = LH * LD
WIN = 32
HALF = 64
KEYS = HALF + WIN
FF = int(P * 4 * 2 / 3)
FF_ROWS = [P, P, FF - 2 * P]
PAD = WIN + 1

SEM_BASE = 110
USES = itertools.count()


def on_chip(allocate, name, shape, dtype):
    return allocate(f"{name}_{next(USES)}", shape, dtype)


@contextmanager
def phase(nc, *names):
    with ExitStack() as ctx:
        sems = [ctx.enter_context(nc.semaphore(name=n, num=SEM_BASE + i)) for i, n in enumerate(names)]
        with nc.Block() as block:
            yield (block, *sems)
        nc.all_engine_barrier(sems_to_clear=range(SEM_BASE, SEM_BASE + len(names)))


def group(g):
    return slice(g * GW, (g + 1) * GW)


def load_constants(nc, pairs):
    with phase(nc, "loaded") as (block, loaded):
        @block.sync
        def _(sp):
            for dst, src in pairs:
                sp.dma_start(dst, src).then_inc(loaded, 16)
            sp.wait_ge(loaded, 16 * len(pairs))


def layer_norm(nc, c, src, dst, eps, gamma=None, beta=None, shift_from=None):
    with ExitStack() as ctx:
        xc = ctx.enter_context(on_chip(nc.sbuf_tensor, "ln_centered", [P, T], F32))
        sq = ctx.enter_context(on_chip(nc.sbuf_tensor, "ln_squares", [P, 2, GW], F32))
        lv = ctx.enter_context(on_chip(nc.sbuf_tensor, "ln_logvar", [P, 2, GW], F32))
        rs = ctx.enter_context(on_chip(nc.sbuf_tensor, "ln_rstd", [P, 2, GW], F32))
        mean = ctx.enter_context(on_chip(nc.psum_tensor, "ln_mean", [P, 2, GW], F32))
        var = ctx.enter_context(on_chip(nc.psum_tensor, "ln_var", [P, 2, GW], F32))
        with phase(nc, "mean_ready", "centered", "squared", "var_ready", "log_ready", "rstd_ready",
                   "normed", "scaled", "taken") as (
                block, mean_ready, centered, squared, var_ready, log_ready, rstd_ready, normed, scaled,
                taken):
            @block.tensor
            def _(pe):
                def mean_of(g):
                    if shift_from is not None:
                        pe.wait_ge(taken, g + 1)
                    if g >= 2:
                        pe.wait_ge(centered, g - 1)
                    pe.matmul(mean[:, g % 2, :], c.mean_w[:], src[:, group(g)],
                              start=True, stop=True).then_inc(mean_ready, 1)

                mean_of(0)
                for g in range(NG):
                    if g + 1 < NG:
                        mean_of(g + 1)
                    pe.wait_ge(squared, g + 1)
                    if g >= 2:
                        pe.wait_ge(log_ready, g - 1)
                    pe.matmul(var[:, g % 2, :], c.mean_w[:], sq[:, g % 2, :],
                              start=True, stop=True).then_inc(var_ready, 1)

            def rstd(act, g):
                act.wait_ge(var_ready, g + 1)
                act.activation(lv[:, g % 2, :], var[:, g % 2, :], ACT.Ln, bias=eps).then_inc(log_ready, 1)
                act.wait_ge(log_ready, g + 1)
                if g >= 2:
                    act.wait_ge(normed, g - 1)
                act.activation(rs[:, g % 2, :], lv[:, g % 2, :], ACT.Exp, scale=-0.5).then_inc(rstd_ready, 1)

            @block.scalar
            def _(act):
                for g in range(NG):
                    act.wait_ge(centered, g + 1)
                    if g >= 2:
                        act.wait_ge(var_ready, g - 1)
                    act.activation(sq[:, g % 2, :], xc[:, group(g)], ACT.Square).then_inc(squared, 1)
                    if g >= 1:
                        rstd(act, g - 1)
                rstd(act, NG - 1)

            @block.vector
            def _(dve):
                def center(g):
                    dve.wait_ge(mean_ready, g + 1)
                    if shift_from is not None:
                        dve.wait_ge(taken, g + 1)
                    dve.tensor_tensor(xc[:, group(g)], src[:, group(g)], mean[:, g % 2, :],
                                      ALU.subtract).then_inc(centered, 1)

                if shift_from is not None:
                    for g in range(NG):
                        for rows, at in ((slice(0, HALF), PAD), (slice(HALF, P), PAD - 1)):
                            m = dve.tensor_copy(src[rows, group(g)], shift_from[rows, at + g * GW:at + (g + 1) * GW])
                        m.then_inc(taken, 1)
                center(0)
                for g in range(NG):
                    if g + 1 < NG:
                        center(g + 1)
                    dve.wait_ge(rstd_ready, g + 1)
                    dve.wait_ge(centered, g + 1)
                    dve.tensor_tensor(dst[:, group(g)], xc[:, group(g)], rs[:, g % 2, :],
                                      ALU.mult).then_inc(normed, 1)
                    if gamma is not None:
                        dve.wait_ge(normed, g + 1)
                        dve.tensor_scalar(dst[:, group(g)], dst[:, group(g)], gamma, beta,
                                          ALU.mult, ALU.add).then_inc(scaled, 1)


def performer(nc, c, w, xn, ot):
    with ExitStack() as ctx:
        def sb(name, shape, dt=F32):
            return ctx.enter_context(on_chip(nc.sbuf_tensor, name, shape, dt))

        def ps(name, shape):
            return ctx.enter_context(on_chip(nc.psum_tensor, name, shape, F32))

        xt = sb("pf_x", [P, P])
        phi_q = sb("pf_phi_q", [P, P])
        phi_kt = sb("pf_phi_kt", [P, P])
        phi_k = sb("pf_phi_k", [P, P])
        kz = sb("pf_kz", [P, H, P])
        vext = sb("pf_vext", [P, H, 32])
        scores = sb("pf_scores", [P, H, P])
        state = sb("pf_state", [P, H * 32])
        add = sb("pf_add", [P, H * 32])
        proj = ps("pf_proj", [P, GW])
        s_ps = ps("pf_s", [P, 4, GW])
        o_ps = ps("pf_o", [P, GW])
        st_ps = ps("pf_st", [P, GW])
        with phase(nc, "init", "tile_in", "projected", "features", "kz_ready", "scored", "masked",
                   "attended", "stored", "summed", "added", "state_new") as (
                block, init, tile_in, projected, features, kz_ready, scored, masked, attended,
                stored, summed, added, state_new):
            @block.gpsimd
            def _(pool):
                pool.memset(vext[:], 0.0).then_inc(init, 1)
                pool.wait_ge(init, 1)
                pool.memset(vext[:, :, DH:DH + 1], 1.0).then_inc(init, 1)
                pool.memset(state[:], 0.0).then_inc(init, 1)
                def tile(t):
                    pool.wait_ge(projected, t)
                    pool.tensor_copy(xt[:], xn[:, bass.ds(t * P, P)]).then_inc(tile_in, 1)

                tile(0)
                with pool.Fori(1, NT) as t:
                    tile(t)

            @block.tensor
            def _(pe):
                def tile(t):
                    pe.wait_ge(tile_in, t + 1)
                    pe.wait_ge(features, t)
                    pe.matmul(proj[:, 0:P], w.pq[:], xt[:], start=True, stop=True)
                    pe.matmul(proj[:, P:2 * P], w.pkv[:, 0:P], xt[:], start=True, stop=True)
                    pe.matmul(proj[:, 2 * P:], xt[:], w.pkv[:], start=True, stop=True).then_inc(projected, 1)
                    pe.wait_ge(kz_ready, t + 1)
                    for h in range(H):
                        mm = pe.matmul(s_ps[:, h // 4, (h % 4) * P:(h % 4 + 1) * P], kz[:, h, :],
                                       phi_q[:], start=True, stop=True)
                    mm.then_inc(scored, 1)
                    pe.wait_ge(init, 3)
                    pe.wait_ge(state_new, t)
                    pe.wait_ge(masked, t + 1)
                    pe.wait_ge(stored, t)
                    for q in range(QUADS):
                        pe.matmul(o_ps[:, q * P:(q + 1) * P], state[:, q * P:(q + 1) * P], phi_q[:],
                                  start=True, stop=False, skip_group_check=True)
                        for j in range(4):
                            mm = pe.matmul(o_ps[32 * j:32 * j + 32, q * P:(q + 1) * P], vext[:, 4 * q + j, :],
                                           scores[:, 4 * q + j, :], start=False, stop=True,
                                           skip_group_check=True)
                    mm.then_inc(attended, 1)
                    pe.wait_ge(added, t)
                    pe.matmul(st_ps[:], phi_k[:], vext[:].rearrange("p h d -> p (h d)"),
                              start=True, stop=True).then_inc(summed, 1)

                tile(0)
                with pe.Fori(1, NT) as t:
                    tile(t)

            @block.scalar
            def _(act):
                def tile(t):
                    act.wait_ge(attended, t + 1)
                    act.activation(ot[:, :, bass.ds(t * P, P)], o_ps[:].rearrange("p (q n) -> p q n", q=QUADS),
                                   ACT.Copy).then_inc(stored, 1)

                tile(0)
                with act.Fori(1, NT) as t:
                    tile(t)

            @block.vector
            def _(dve):
                dve.wait_ge(init, 3)
                def tile(t):
                    dve.wait_ge(projected, t + 1)
                    dve.wait_ge(summed, t)
                    dve.tensor_scalar(phi_q[:], proj[:, 0:P], 0.0, 1e-3, ALU.max, ALU.add)
                    dve.tensor_scalar(phi_kt[:], proj[:, P:2 * P], 0.0, 1e-3, ALU.max, ALU.add)
                    dve.tensor_scalar(phi_k[:], proj[:, 2 * P:3 * P], 0.0, 1e-3, ALU.max, ALU.add)
                    dve.tensor_copy(vext[:, :, 0:DH],
                                    proj[:, 3 * P:].rearrange("p (h d) -> p h d", h=H)).then_inc(features, 1)
                    dve.wait_ge(features, t + 1)
                    dve.tensor_tensor(kz[:], phi_kt[:, None, :].to_broadcast([P, H, P]),
                                      c.head_mask[:, :, None].to_broadcast([P, H, P]),
                                      ALU.mult).then_inc(kz_ready, 1)
                    dve.wait_ge(scored, t + 1)
                    for b in range(4):
                        m = dve.tensor_tensor(scores[:, 4 * b:4 * b + 4, :],
                                              s_ps[:, b, :].rearrange("p (h n) -> p h n", h=4),
                                              c.causal[:, None, :].to_broadcast([P, 4, P]), ALU.mult)
                    m.then_inc(masked, 1)
                    dve.wait_ge(summed, t + 1)
                    dve.tensor_tensor(add[:], st_ps[:], c.block_mask[:], ALU.mult).then_inc(added, 1)
                    dve.wait_ge(added, t + 1)
                    dve.tensor_tensor(state[:], state[:], add[:], ALU.add).then_inc(state_new, 1)

                tile(0)
                with dve.Fori(1, NT) as t:
                    tile(t)


def normalise_heads(nc, c, ot, at):
    with ExitStack() as ctx:
        rec = ctx.enter_context(on_chip(nc.sbuf_tensor, "nh_rec", [P, 2, H], F32))
        tok = ctx.enter_context(on_chip(nc.sbuf_tensor, "nh_tok", [P, 2, P], F32))
        tps = ctx.enter_context(on_chip(nc.psum_tensor, "nh_tps", [P, 2, GW], F32))
        aps = ctx.enter_context(on_chip(nc.psum_tensor, "nh_aps", [P, 2, GW], F32))
        with phase(nc, "turned", "inverted", "divided", "back", "stored") as (
                block, turned, inverted, divided, back, stored):
            @block.tensor
            def _(pe):
                def turn(t):
                    if t >= 2:
                        pe.wait_ge(divided, t - 1)
                    for q in range(QUADS):
                        m = pe.transpose(tps[:, t % 2, q * P:(q + 1) * P], ot[:, q, t * P:(t + 1) * P], c.ident[:])
                    m.then_inc(turned, 1)

                turn(0)
                for t in range(NT):
                    if t + 1 < NT:
                        turn(t + 1)
                    pe.wait_ge(divided, t + 1)
                    if t >= 8 and t % 4 == 0:
                        pe.wait_ge(stored, t // 4 - 1)
                    pe.transpose(aps[:, t // 4 % 2, (t % 4) * P:(t % 4 + 1) * P], tok[:, t % 2, :],
                                 c.ident[:]).then_inc(back, 1)

            @block.vector
            def _(dve):
                for t in range(NT):
                    heads = tps[:, t % 2, :].rearrange("p (h n) -> p h n", h=H)
                    dve.wait_ge(turned, t + 1)
                    dve.reciprocal(rec[:, t % 2, :, None], heads[:, :, DH:DH + 1]).then_inc(inverted, 1)
                    dve.wait_ge(inverted, t + 1)
                    if t >= 2:
                        dve.wait_ge(back, t - 1)
                    dve.tensor_tensor(tok[:, t % 2, :].rearrange("p (h d) -> p h d", h=H), heads[:, :, 0:DH],
                                      rec[:, t % 2, :, None].to_broadcast([P, H, DH]),
                                      ALU.mult).then_inc(divided, 1)

            @block.scalar
            def _(act):
                for g in range(NG):
                    act.wait_ge(back, 4 * g + 4)
                    act.activation(at[:, group(g)], aps[:, g % 2, :], ACT.Copy).then_inc(stored, 1)


def project_add(nc, w, src, dst, more):
    with ExitStack() as ctx:
        tmp = ctx.enter_context(on_chip(nc.sbuf_tensor, "pa_tmp", [P, T], F32))
        y = ctx.enter_context(on_chip(nc.psum_tensor, "pa_y", [P, NG, GW], F32))
        with phase(nc, "projected", "summed") as (block, projected, summed):
            @block.tensor
            def _(pe):
                for g in range(NG):
                    pe.matmul(y[:, g, :], w[:], src[:, group(g)], start=True, stop=True).then_inc(projected, 1)

            @block.vector
            def _(dve):
                n = 0
                for g in range(NG):
                    dve.wait_ge(projected, g + 1)
                    last = y[:, g, :]
                    for k, m in enumerate(more):
                        to = dst if k == len(more) - 1 else tmp
                        if k:
                            dve.wait_ge(summed, n)
                        dve.tensor_tensor(to[:, group(g)], last, m[:, group(g)], ALU.add).then_inc(summed, 1)
                        n += 1
                        last = to[:, group(g)]


def gelu_mlp(nc, c, w, xn, x1, x):
    with ExitStack() as ctx:
        hid = ctx.enter_context(on_chip(nc.sbuf_tensor, "mlp_h", [P, 2, 4, GW], F32))
        tmp = ctx.enter_context(on_chip(nc.sbuf_tensor, "mlp_t", [P, GW], F32))
        hp = ctx.enter_context(on_chip(nc.psum_tensor, "mlp_hp", [P, 4, GW], F32))
        yp = ctx.enter_context(on_chip(nc.psum_tensor, "mlp_yp", [P, 2, GW], F32))
        with phase(nc, "up", "gelu_done", "down", "biased", "summed") as (
                block, up, gelu_done, down, biased, summed):
            @block.tensor
            def _(pe):
                def first(g):
                    for j in range(4):
                        if g >= 1:
                            pe.wait_ge(gelu_done, 4 * g - 3 + j)
                        pe.matmul(hp[:, j, :], w.w1[:, j * P:(j + 1) * P], xn[:, group(g)],
                                  start=True, stop=True).then_inc(up, 1)

                first(0)
                for g in range(NG):
                    if g + 1 < NG:
                        first(g + 1)
                    if g >= 2:
                        pe.wait_ge(biased, g - 1)
                    for j in range(4):
                        pe.wait_ge(gelu_done, 4 * g + j + 1)
                        m = pe.matmul(yp[:, g % 2, :], w.w2[:, j, :], hid[:, g % 2, j, :],
                                      start=(j == 0), stop=(j == 3))
                    m.then_inc(down, 1)

            @block.scalar
            def _(act):
                for g in range(NG):
                    for j in range(4):
                        act.wait_ge(up, 4 * g + j + 1)
                        if g >= 2:
                            act.wait_ge(down, g - 1)
                        act.activation(hid[:, g % 2, j, :], hp[:, j, :], ACT.Gelu_apprx_tanh,
                                       bias=c.v("a_b1", j)).then_inc(gelu_done, 1)

            @block.vector
            def _(dve):
                for g in range(NG):
                    dve.wait_ge(down, g + 1)
                    if g:
                        dve.wait_ge(summed, 2 * g)
                    dve.scalar_tensor_tensor(out=tmp[:], in0=yp[:, g % 2, :], scalar=c.v("a_b2"),
                                             in1=x1[:, group(g)], op0=ALU.add, op1=ALU.add).then_inc(biased, 1)
                    dve.wait_ge(biased, g + 1)
                    dve.tensor_tensor(x[:, group(g)], x[:, group(g)], tmp[:], ALU.add).then_inc(summed, 2)


def experts(nc, c, w, xn, x):
    with ExitStack() as ctx:
        def sb(name, shape, dt=F32):
            return ctx.enter_context(on_chip(nc.sbuf_tensor, name, shape, dt))

        comb_t = sb("moe_comb_t", [E, T])
        with ExitStack() as ctx2:
            def sb2(name, shape, dt=F32):
                return ctx2.enter_context(on_chip(nc.sbuf_tensor, name, shape, dt))

            pr = sb2("moe_probs", [P, NT, E])
            st = sb2("moe_stat", [P, NT])
            inv = sb2("moe_inv", [P, NT])
            top = sb2("moe_top", [P, NT, 8])
            idx = sb2("moe_idx", [P, NT, 8], U32)
            idf = sb2("moe_idf", [P, NT, 2])
            wt = sb2("moe_wt", [P, NT, 2])
            eq = sb2("moe_eq", [P, 2, NT, E])
            comb = sb2("moe_comb", [P, NT, E])
            lg = ctx2.enter_context(on_chip(nc.psum_tensor, "moe_logits", [P, NT, E], F32))
            ct = ctx2.enter_context(on_chip(nc.psum_tensor, "moe_ct", [P, NG, GW], F32))
            with phase(nc, "routed", "shifted", "exps", "step", "comb_ready", "turned", "stored") as (
                    block, routed, shifted, exps, step, comb_ready, turned, stored):
                @block.tensor
                def _(pe):
                    for t in range(NT):
                        m = pe.matmul(lg[:, t, :], xn[:, t * P:(t + 1) * P], w.router[:], start=True, stop=True)
                    m.then_inc(routed, 1)
                    pe.wait_ge(comb_ready, 1)
                    for t in range(NT):
                        m = pe.transpose(ct[0:E, t // 4, (t % 4) * P:(t % 4 + 1) * P], comb[:, t, :], c.ident[:])
                    m.then_inc(turned, 1)

                @block.scalar
                def _(act):
                    act.wait_ge(shifted, 1)
                    act.activation(pr[:], pr[:], ACT.Exp).then_inc(exps, 1)
                    act.wait_ge(turned, 1)
                    for g in range(NG):
                        act.activation(comb_t[:, group(g)], ct[0:E, g, :], ACT.Copy).then_inc(stored, 1)

                @block.vector
                def _(dve):
                    def spread(a):
                        return a.to_broadcast([P, NT, E])

                    n = 0

                    def then(ins):
                        nonlocal n
                        n += 1
                        ins.then_inc(step, 1)
                        dve.wait_ge(step, n)

                    dve.wait_ge(routed, 1)
                    then(dve.tensor_reduce(st[:], lg[:], AX.X, ALU.max))
                    dve.tensor_tensor(pr[:], lg[:], spread(st[:, :, None]), ALU.subtract).then_inc(shifted, 1)
                    dve.wait_ge(exps, 1)
                    then(dve.tensor_reduce(st[:], pr[:], AX.X, ALU.add))
                    then(dve.reciprocal(inv[:], st[:]))
                    then(dve.tensor_tensor(pr[:], pr[:], spread(inv[:, :, None]), ALU.mult))
                    for t in range(NT):
                        then(dve.max(top[:, t, :], pr[:, t, :]))
                        then(dve.max_index(idx[:, t, :], top[:, t, :], pr[:, t, :]))
                    then(dve.tensor_copy(idf[:], idx[:, :, 0:2]))
                    then(dve.tensor_tensor(st[:], top[:, :, 0], top[:, :, 1], ALU.add))
                    then(dve.tensor_scalar(st[:], st[:], 1e-9, None, ALU.add))
                    then(dve.reciprocal(inv[:], st[:]))
                    then(dve.tensor_tensor(wt[:], top[:, :, 0:2], inv[:, :, None].to_broadcast([P, NT, 2]), ALU.mult))
                    for k in range(2):
                        then(dve.tensor_tensor(eq[:, k], c.iota[:, None, :].to_broadcast([P, NT, E]),
                                               spread(idf[:, :, k:k + 1]), ALU.is_equal))
                        then(dve.tensor_tensor(eq[:, k], eq[:, k], spread(wt[:, :, k:k + 1]), ALU.mult))
                    dve.tensor_tensor(comb[:], eq[:, 0], eq[:, 1], ALU.add).then_inc(comb_ready, 1)
        sg = sb("moe_sg", [P, 2, GW])
        ug = sb("moe_ug", [P, 2, GW])
        hd = sb("moe_h", [P, 2, 5, GW])
        with ExitStack() as ctx3:
            gp = ctx3.enter_context(on_chip(nc.psum_tensor, "moe_g", [P, 2, GW], F32))
            up = ctx3.enter_context(on_chip(nc.psum_tensor, "moe_u", [P, 2, GW], F32))
            cp = ctx3.enter_context(on_chip(nc.psum_tensor, "moe_c", [P, 2, GW], F32))
            yp = ctx3.enter_context(on_chip(nc.psum_tensor, "moe_y", [P, 2, GW], F32))
            with phase(nc, "up_ready", "silu_done", "gated", "h_ready", "down", "summed") as (
                    block, up_ready, silu_done, gated, h_ready, down, summed):
                @block.tensor
                def _(pe):
                    def chunk(g, j):
                        n = 5 * g + j
                        if n >= 2:
                            pe.wait_ge(h_ready, n - 1)
                        wg = w.wg[:, j * P:(j + 1) * P] if j < 4 else w.wgs[:]
                        wu = w.wu[:, j * P:(j + 1) * P] if j < 4 else w.wus[:]
                        pe.matmul(gp[:, n % 2, :], wg, xn[:, group(g)], start=True, stop=True)
                        if j < 4:
                            pe.matmul(cp[:, n % 2, :], c.sel[:, j, :], comb_t[:, group(g)], start=True, stop=True)
                        pe.matmul(up[:, n % 2, :], wu, xn[:, group(g)], start=True, stop=True).then_inc(up_ready, 1)

                    def downs(g):
                        pe.wait_ge(h_ready, 5 * g + 5)
                        if g >= 2:
                            pe.wait_ge(summed, g - 1)
                        for j in range(5):
                            wd = w.wd[:, j, :] if j < 4 else w.wds[:]
                            m = pe.matmul(yp[:, g % 2, :], wd, hd[:, g % 2, j, :], start=(j == 0), stop=(j == 4))
                        m.then_inc(down, 1)

                    for g in range(NG):
                        for j in range(5):
                            chunk(g, j)
                            if j == 1 and g:
                                downs(g - 1)
                    downs(NG - 1)

                @block.scalar
                def _(act):
                    for n in range(5 * NG):
                        act.wait_ge(up_ready, n + 1)
                        if n >= 2:
                            act.wait_ge(h_ready, n - 1)
                        act.activation(sg[:, n % 2, :], gp[:, n % 2, :], ACT.Silu).then_inc(silu_done, 1)

                def add_y(dve, g):
                    dve.wait_ge(down, g + 1)
                    dve.tensor_tensor(x[:, group(g)], yp[:, g % 2, :], x[:, group(g)], ALU.add).then_inc(summed, 1)

                @block.vector
                def _(dve):
                    for g in range(NG):
                        for j in range(5):
                            n = 5 * g + j
                            dve.wait_ge(silu_done, n + 1)
                            if g >= 2:
                                dve.wait_ge(down, g - 1)
                            if j < 4:
                                dve.tensor_tensor(ug[:, n % 2, :], up[:, n % 2, :], sg[:, n % 2, :],
                                                  ALU.mult).then_inc(gated, 1)
                                dve.wait_ge(gated, 4 * g + j + 1)
                                dve.tensor_tensor(hd[:, g % 2, j, :], cp[:, n % 2, :], ug[:, n % 2, :],
                                                  ALU.mult).then_inc(h_ready, 1)
                            else:
                                dve.tensor_tensor(hd[:, g % 2, j, :], up[:, n % 2, :], sg[:, n % 2, :],
                                                  ALU.mult).then_inc(h_ready, 1)
                            if j == 2 and g:
                                add_y(dve, g - 1)
                    add_y(dve, NG - 1)


def split_parts(nc, x, dram):
    with ExitStack() as ctx:
        parts = [ctx.enter_context(on_chip(nc.sbuf_tensor, f"sp_p{i}", [P, T], BF16)) for i in range(3)]
        rest = ctx.enter_context(on_chip(nc.sbuf_tensor, "sp_rest", [P, T], F32))
        with phase(nc, "rounded", "left", "stored") as (block, rounded, left, stored):
            @block.scalar
            def _(act):
                act.activation(parts[0][:], x[:], ACT.Copy).then_inc(rounded, 1)
                act.wait_ge(left, 1)
                act.activation(parts[1][:], rest[:], ACT.Copy).then_inc(rounded, 1)

            @block.vector
            def _(dve):
                dve.wait_ge(rounded, 1)
                dve.tensor_tensor(rest[:], x[:], parts[0][:], ALU.subtract).then_inc(left, 1)
                dve.wait_ge(left, 1)
                dve.wait_ge(rounded, 2)
                dve.tensor_tensor(parts[2][:], rest[:], parts[1][:], ALU.subtract).then_inc(left, 1)

            @block.sync
            def _(sp):
                sp.wait_ge(rounded, 1)
                sp.dma_start(dram[0], parts[0][:]).then_inc(stored, 16)
                sp.wait_ge(rounded, 2)
                sp.dma_start(dram[1], parts[1][:]).then_inc(stored, 16)
                sp.wait_ge(left, 2)
                sp.dma_start(dram[2], parts[2][:]).then_inc(stored, 16)
                sp.wait_ge(stored, 48)


def values(nc, wv, xn, v):
    with ExitStack() as ctx:
        vp = ctx.enter_context(on_chip(nc.psum_tensor, "va_ps", [P, NG, 4, P], F32))
        with phase(nc, "init", "projected", "stored") as (block, init, projected, stored):
            @block.tensor
            def _(pe):
                for t in range(NT):
                    m = pe.matmul(vp[:, t // 4, t % 4, :], xn[:, t * P:(t + 1) * P], wv[:], start=True, stop=True)
                    if t % 4 == 3:
                        m.then_inc(projected, 1)

            @block.gpsimd
            def _(pool):
                pool.memset(v[:], 1.0).then_inc(init, 1)

            @block.vector
            def _(dve):
                dve.wait_ge(init, 1)
                for g in range(NG):
                    dve.wait_ge(projected, g + 1)
                    dve.tensor_copy(v[:, 4 * g:4 * g + 4, 0:H * VW].rearrange("p t (h d) -> p t h d", h=H)[:, :, :, 0:DH],
                                    vp[:, g].rearrange("p t (h d) -> p t h d", h=H)).then_inc(stored, 1)


def near_tables(nc, c, io):
    n = 3 * P
    with ExitStack() as ctx:
        rel = ctx.enter_context(on_chip(nc.sbuf_tensor, "nt_rel", [H, 2, P + 1], F32))
        ext = ctx.enter_context(on_chip(nc.sbuf_tensor, "nt_ext", [H, 2, n], F32))
        rest = ctx.enter_context(on_chip(nc.sbuf_tensor, "nt_rest", [H, 2, n], F32))
        parts = ctx.enter_context(on_chip(nc.sbuf_tensor, "nt_parts", [H, 3, 2, n], BF16))
        with phase(nc, "loaded", "step", "stored") as (block, loaded, step, stored):
            @block.sync
            def _(sp):
                sp.dma_start(rel[:], io["rel"]).then_inc(loaded, 16)
                sp.wait_ge(step, 9)
                sp.dma_start(io["s_ext"].rearrange("a h k n -> h a k n"), parts[:]).then_inc(stored, 16)
                sp.wait_ge(stored, 16)

            @block.vector
            def _(dve):
                k = 0

                def then(ins):
                    nonlocal k
                    k += 1
                    ins.then_inc(step, 1)
                    dve.wait_ge(step, k)

                then(dve.memset(ext[:], 0.0))
                then(dve.memset(ext[:, 0, 0:P - 1], NEG))
                then(dve.memset(ext[:, 1, 2 * P:n], NEG))
                dve.wait_ge(loaded, 16)
                then(dve.tensor_scalar(ext[:, 0, P - 1:2 * P], rel[:, 0, :], rel[:, 0, P:P + 1], None, ALU.subtract))
                then(dve.tensor_scalar(ext[:, 1, P - 1:2 * P], rel[:, 1, :], rel[:, 0, P:P + 1], None, ALU.subtract))
                then(dve.tensor_copy(parts[:, 0], ext[:]))
                then(dve.tensor_tensor(rest[:], ext[:], parts[:, 0], ALU.subtract))
                then(dve.tensor_copy(parts[:, 1], rest[:]))
                then(dve.tensor_tensor(parts[:, 2], rest[:], parts[:, 1], ALU.subtract))


M_ROW = 96
UNITS_A = [(h, i, s) for h in range(4) for i in range(NT) for s in range(1 + (i >= 8))]
STEPS_B = [(g, j) for g in range(NG) for j in range(4 * g + 4)]
START_A = 4


def units_at(step):
    return min(len(UNITS_A), max(0, step + 1 - START_A) * len(UNITS_A) // (len(STEPS_B) - START_A - 2) + 1
               if step >= START_A else 0)


def causal_attention(nc, c, io, v, ot, near):
    n_near = 3 if near else 1
    with ExitStack() as ctx:
        def sb(name, shape, dt=F32):
            return ctx.enter_context(on_chip(nc.sbuf_tensor, name, shape, dt))

        qs = sb("ca_q", [P, 2, 4, T], BF16)
        ks = sb("ca_k", [P, 2, 4, T], BF16)
        pt = sb("ca_p", [P, 3, 4, GW])
        mx = sb("ca_mx", [P, 4, NT, 2])
        negm = sb("ca_negm", [P, 4 * NT])
        rest = sb("ca_rest", [P, 4 * NT])
        mp = sb("ca_mp", [P, 3, 4 * NT], BF16)
        mt = sb("ca_mt", [4 * NT, 3, P], BF16)
        if near:
            near_a = sb("ca_near_a", [P, 2, 4, 3, 2 * P], BF16)
            near_b = sb("ca_near_b", [P, 2, 4, 3, 2 * P], BF16)
        a_ps = ctx.enter_context(on_chip(nc.psum_tensor, "ca_a", [P, 2, 2 * GW], F32))
        s_ps = ctx.enter_context(on_chip(nc.psum_tensor, "ca_s", [P, 2, GW], F32))
        o_ps = ctx.enter_context(on_chip(nc.psum_tensor, "ca_o", [P, 2, GW], F32))
        loads = 18 + 1 + (24 if near else 0)
        with phase(nc, "cleared", "loaded_even", "loaded_odd", "a_scored", "a_reduced", "combined",
                   "m_turned", "mt_ready", "m_placed", "b_scored", "b_exp", "b_out",
                   "o_stored", "mstep", "mx_cleared") as (
                block, cleared, loaded_even, loaded_odd, a_scored, a_reduced, combined, m_turned,
                mt_ready, m_placed, b_scored, b_exp, b_out, o_stored, mstep, mx_cleared):
            loaded = (loaded_even, loaded_odd)
            nb = 4 * len(STEPS_B)

            @block.gpsimd
            def _(pool):
                pool.memset(qs[:].rearrange("p a h t -> p (a h t)").bitcast(F32), 0.0).then_inc(cleared, 1)
                pool.memset(ks[:].rearrange("p a h t -> p (a h t)").bitcast(F32), 0.0).then_inc(cleared, 1)
                pool.wait_ge(cleared, 2)
                pool.memset(ks[M_ROW:M_ROW + 3], 1.0).then_inc(cleared, 1)

            @block.sync
            def _(sp):
                def load(q):
                    for a in range(3):
                        for b in range(3):
                            r = (3 * a + b) * DH
                            for dst, src, part in ((qs, io["s_q"], a), (ks, io["s_k"], b)):
                                heads = src[part, q * 32:q * 32 + 32, :].rearrange("(h d) t -> d h t", h=4)
                                sp.dma_start(dst[r:r + DH, q % 2], heads).then_inc(loaded[q % 2], 16)
                    sp.dma_start(qs[M_ROW:M_ROW + 3, q % 2].rearrange("p h t -> p (h t)"),
                                 io["c_zero"]).then_inc(loaded[q % 2], 16)
                    if near:
                        e = io["s_ext"]
                        for h in range(4):
                            for part in range(3):
                                for k, dst in ((1, near_a), (0, near_b)):
                                    row = e[part, 4 * q + h, k, 0:2 * P]
                                    skew = bass.AP(row.tensor, row.offset, [[1, P], [1, 2 * P]])
                                    sp.dma_start(dst[:, q % 2, h, part, :], skew).then_inc(loaded[q % 2], 16)

                def place(q):
                    sp.wait_ge(mt_ready, q + 1)
                    for part in range(3):
                        sp.dma_start(qs[M_ROW + part:M_ROW + part + 1, q % 2].rearrange("o h (i n) -> o (h i) n", n=P),
                                     mt[:, part, :]).then_inc(m_placed, 16)

                sp.wait_ge(cleared, 3)
                load(0)
                load(1)
                place(0)
                for q in range(1, QUADS):
                    place(q)
                    if q + 1 < QUADS:
                        sp.wait_ge(b_out, q * len(STEPS_B))
                        load(q + 1)

            @block.tensor
            def _(pe):
                def wait_loaded(q):
                    pe.wait_ge(loaded[q % 2], 16 * loads * (q // 2 + 1))

                def near_add(out, side, q, h, cols):
                    for k in range(n_near):
                        if near:
                            rhs = (near_a if side == "a" else near_b)[:, q % 2, h, k, cols]
                        else:
                            rhs = c.mask_a[:] if side == "a" else c.mask_b[:]
                        m = pe.matmul(out, (c.flip_b if near else c.ident_b)[:], rhs, start=False,
                                      stop=True, skip_group_check=True)
                    return m

                def unit_a(q, n):
                    h, i, s = UNITS_A[n]
                    u = q * len(UNITS_A) + n
                    if u >= 2:
                        pe.wait_ge(a_reduced, u - 1)
                    end = min(P * (i + 1), (s + 1) * 2 * GW)
                    for lo in range(s * 2 * GW, end, GW):
                        hi = min(lo + GW, end)
                        at = a_ps[:, u % 2, lo - s * 2 * GW:hi - s * 2 * GW]
                        m = pe.matmul(at, qs[:, q % 2, h, i * P:(i + 1) * P], ks[:, q % 2, h, lo:hi],
                                      start=True, stop=True, skip_group_check=True)
                        first = max(lo, P * (i - 1 if near else i), 0)
                        if first < hi:
                            c0 = first - P * (i - 1)
                            cols = slice(c0, c0 + hi - first)
                            out = a_ps[:, u % 2, first - s * 2 * GW:hi - s * 2 * GW]
                            m = near_add(out, "a", q, h, cols)
                    m.then_inc(a_scored, 1)

                def turn_m(q):
                    u = (q + 1) * len(UNITS_A) - 1
                    pe.wait_ge(combined, q + 1)
                    pe.wait_ge(a_reduced, u + 1)
                    for part in range(3):
                        m = pe.transpose(a_ps[0:4 * NT, 0, :].bitcast(BF16)[:, part * P:(part + 1) * P],
                                         mp[:, part, :], c.ident_b[:])
                    m.then_inc(m_turned, 1)

                def outputs(q, n):
                    g, j = STEPS_B[n]
                    s = q * len(STEPS_B) + n
                    off = max(0, j - 4 * g) * P
                    pe.wait_ge(b_exp, 4 * s + 4)
                    if j == 0 and q * NG + g >= 2:
                        pe.wait_ge(o_stored, q * NG + g - 1)
                    for h in range(4):
                        m = pe.matmul(o_ps[32 * h:32 * h + 32, g % 2, off:GW],
                                      v[:, j, (4 * q + h) * VW:(4 * q + h) * VW + 32],
                                      pt[:, s % 3, h, off:GW], start=(j == 0), stop=(j == 4 * g + 3),
                                      skip_group_check=True)
                    m.then_inc(b_out, 1)

                def step_b(q, n, a_from, a_to):
                    g, j = STEPS_B[n]
                    off = max(0, j - 4 * g) * P
                    for h in range(4):
                        k = q * nb + 4 * n + h
                        if k >= 2:
                            pe.wait_ge(b_exp, k - 1)
                        m = pe.matmul(s_ps[:, k % 2, off:GW], ks[:, q % 2, h, j * P:(j + 1) * P],
                                      qs[:, q % 2, h, g * GW + off:(g + 1) * GW],
                                      start=True, stop=True, skip_group_check=True)
                        lo, hi = max(j, 4 * g), min(j + (2 if near else 1), 4 * g + 4)
                        if lo < hi:
                            m = near_add(s_ps[:, k % 2, lo * P - g * GW:hi * P - g * GW], "b", q, h,
                                         slice((lo - j) * P, (hi - j) * P))
                        m.then_inc(b_scored, 1)
                        for x in range(a_from + (a_to - a_from) * h // 4, a_from + (a_to - a_from) * (h + 1) // 4):
                            unit_a(q + 1, x)
                        if h == 1 and n:
                            outputs(q, n - 1)

                pe.wait_ge(cleared, 3)
                wait_loaded(0)
                for n in range(len(UNITS_A)):
                    unit_a(0, n)
                turn_m(0)
                for q in range(QUADS):
                    pe.wait_ge(m_placed, 48 * (q + 1))
                    done = 0
                    for n in range(len(STEPS_B)):
                        to = units_at(n) if q + 1 < QUADS else 0
                        if to and not done:
                            wait_loaded(q + 1)
                        step_b(q, n, done, to)
                        done = to
                    if q + 1 < QUADS:
                        assert done == len(UNITS_A)
                        turn_m(q + 1)
                    outputs(q, len(STEPS_B) - 1)

            @block.scalar
            def _(act):
                for q in range(QUADS):
                    for n, (g, j) in enumerate(STEPS_B):
                        s = q * len(STEPS_B) + n
                        off = max(0, j - 4 * g) * P
                        if s >= 3:
                            act.wait_ge(b_out, s - 2)
                        for h in range(4):
                            k = 4 * s + h
                            act.wait_ge(b_scored, k + 1)
                            act.activation(pt[:, s % 3, h, off:GW], s_ps[:, k % 2, off:GW],
                                           ACT.Exp).then_inc(b_exp, 1)

            @block.vector
            def _(dve):
                dve.memset(mx[:], -3e38).then_inc(mx_cleared, 1)

                def reduce_a(q, n):
                    h, i, s = UNITS_A[n]
                    u = q * len(UNITS_A) + n
                    width = min(P * (i + 1), (s + 1) * 2 * GW) - s * 2 * GW
                    dve.wait_ge(a_scored, u + 1)
                    if u == 0:
                        dve.wait_ge(mx_cleared, 1)
                    dve.tensor_reduce(mx[:, h, i, s:s + 1], a_ps[:, u % 2, 0:width], AX.X,
                                      ALU.max).then_inc(a_reduced, 1)

                def combine(q):
                    dve.wait_ge(a_reduced, (q + 1) * len(UNITS_A))
                    dve.tensor_reduce(negm[:], mx[:].rearrange("p h i s -> p (h i) s"), AX.X, ALU.max,
                                      negate=True).then_inc(mstep, 1)
                    dve.wait_ge(mstep, 4 * q + 1)
                    dve.tensor_copy(mp[:, 0, :], negm[:]).then_inc(mstep, 1)
                    dve.wait_ge(mstep, 4 * q + 2)
                    dve.tensor_tensor(rest[:], negm[:], mp[:, 0, :], ALU.subtract).then_inc(mstep, 1)
                    dve.wait_ge(mstep, 4 * q + 3)
                    dve.tensor_copy(mp[:, 1, :], rest[:]).then_inc(mstep, 1)
                    dve.wait_ge(mstep, 4 * q + 4)
                    dve.tensor_tensor(mp[:, 2, :], rest[:], mp[:, 1, :], ALU.subtract).then_inc(combined, 1)
                    dve.wait_ge(m_turned, q + 1)
                    if q:
                        dve.wait_ge(m_placed, 48 * q)
                    dve.tensor_copy(mt[:], a_ps[0:4 * NT, 0, :].bitcast(BF16)[:, 0:3 * P]
                                    .rearrange("r (a n) -> r a n", a=3)).then_inc(mt_ready, 1)

                def store_o(q, g):
                    dve.wait_ge(b_out, q * len(STEPS_B) + sum(4 * x + 4 for x in range(g + 1)))
                    dve.tensor_copy(ot[:, q, group(g)], o_ps[:, g % 2, :]).then_inc(o_stored, 1)

                for n in range(len(UNITS_A)):
                    reduce_a(0, n)
                combine(0)
                for q in range(QUADS):
                    done = 0
                    for n, (g, j) in enumerate(STEPS_B):
                        to = units_at(n) if q + 1 < QUADS else 0
                        for x in range(done, to):
                            reduce_a(q + 1, x)
                        done = to
                        if g and j == 1:
                            store_o(q, g - 1)
                    if q + 1 < QUADS:
                        combine(q + 1)
                    store_o(q, NG - 1)


CH = 4
KZ = WIN + P


def slot(k, i):
    return i if isinstance(k, int) and k == 1 else (k - 2) * 11 + (4 + i)


def local_attention(nc, c, lw, xa, xb, prefetch):
    with ExitStack() as ctx:
        def sb(name, shape, dt=F32):
            return ctx.enter_context(on_chip(nc.sbuf_tensor, name, shape, dt))

        xs = sb("la_xs", [P, 2, KZ])
        raw = sb("la_raw", [P, CH, GW])
        sq = sb("la_sq", [P, 2, GW])
        tm = sb("la_tm", [P, 2, GW])
        rp = sb("la_rp", [P, 2, CH, GW])
        ss = sb("la_ss", [P, 2 * LH])
        lg = sb("la_lg", [P, 2 * LH])
        rn = sb("la_rn", [P, 2 * LH])
        qt = sb("la_qt", [P, LH // 2, P])
        kz = sb("la_kz", [P, 2, LH, KZ])
        mx = sb("la_mx", [P, LH])
        pw = sb("la_p", [P, LH, KEYS])
        pts = sb("la_pts", [KEYS, LH, P])
        vx = sb("la_vx", [KEYS, 2, 2, LH, KEYS])
        rec = sb("la_rec", [P, LH])
        otok = sb("la_otok", [P, INNER])
        ots = sb("la_ots", [P, LH // 2, P])
        ysb = sb("la_y", [P, P])
        proj = ctx.enter_context(on_chip(nc.psum_tensor, "la_proj", [P, 2, GW], F32))
        ring = ctx.enter_context(on_chip(nc.psum_tensor, "la_ring", [P, 2, GW], F32))
        so = ctx.enter_context(on_chip(nc.psum_tensor, "la_so", [P, 4, GW], F32))
        so_heads = so[:, :, 0:4 * KEYS].rearrange("p b (j n) -> p b j n", j=4)

        def heads(a):
            return a.rearrange("p (b j) n -> p b j n", b=4)

        with phase(nc, "init", "xs_ready", "projected", "raw_ready", "sq_ready",
                   "scaled_cos", "scaled_sin", "rotated", "squares_summed", "clamped", "logged",
                   "norms_ready", "normed", "slot_full", "slot_free", "k_before", "scored",
                   "max_ready", "shifted", "weights_ready", "values_ready", "weighted", "inverted",
                   "out_ready", "y_added", "scaled_tables", "fetched") as (
                block, init, xs_ready, projected, raw_ready, sq_ready, scaled_cos,
                scaled_sin, rotated, squares_summed, clamped, logged, norms_ready, normed, slot_full,
                slot_free, k_before, scored, max_ready, shifted, weights_ready, values_ready,
                weighted, inverted, out_ready, y_added, scaled_tables, fetched):
            @block.sync
            def _(sp):
                n = prefetch(sp, fetched)
                sp.wait_ge(fetched, 16 * n)

            def pipeline(eng, step):
                step(0, 0, True, False, False)
                step(1, 1, True, True, False)
                step(2, 0, True, True, True)
                step(3, 1, True, True, True)
                with eng.Fori(4, NT - 1, 2) as k:
                    step(k, 0, True, True, True)
                    step(k + 1, 1, True, True, True)
                step(NT, 0, False, True, True)
                step(NT + 1, 1, False, False, True)

            def since(k, n):
                return not isinstance(k, int) or k >= n

            @block.tensor
            def _(pe):
                def take(k, par, i):
                    if not (isinstance(k, int) and slot(k, i) < 2):
                        pe.wait_ge(slot_free, slot(k, i) - 1)
                    return (par + i) % 2 if not (isinstance(k, int) and k == 1) else i % 2

                def project(k, par, i):
                    if 2 <= i < 6:
                        pe.wait_ge(sq_ready, k * 4 + (i - 1))
                    elif i >= 6 or not (isinstance(k, int) and k == 0):
                        pe.wait_ge(values_ready, k * 4 + (i - 5 if i >= 6 else i - 1))
                    if i == 0:
                        pe.wait_ge(xs_ready, k + 1)
                    if i < CH:
                        pe.matmul(proj[:, i % 2, :], xs[:, par, WIN:KZ], lw.qkv[:, i * GW:(i + 1) * GW],
                                  start=True, stop=True).then_inc(projected, 1)
                    else:
                        a = (i - CH) // 2
                        col = 2 * INNER + (i % 2) * GW
                        pe.matmul(proj[0:KEYS, i % 2, :], xs[:, par, a * HALF:a * HALF + KEYS],
                                  lw.qkv[:, col:col + GW], start=True, stop=True).then_inc(projected, 1)

                def step(k, par, a, b, c_):
                    kb, pb, kc, pc = k - 1, 1 - par, k - 2, par
                    if c_:
                        pe.wait_ge(weights_ready, kc + 1)
                        for i in range(4):
                            bank = take(k, par, i)
                            for j in range(4):
                                m = pe.transpose(ring[0:KEYS, bank, j * P:(j + 1) * P], pw[:, 4 * i + j, :], c.ident[:])
                            m.then_inc(slot_full, 1)
                        pe.wait_ge(slot_free, slot(k, 3) + 1)
                        pe.wait_ge(values_ready, kc * 4 + 4)
                        for i in range(4):
                            for j in range(4):
                                h = 4 * i + j
                                for half in range(2):
                                    m = pe.matmul(so[HALF * half:HALF * half + HALF, i, j * KEYS:(j + 1) * KEYS],
                                                  pts[:, h, HALF * half:HALF * half + HALF],
                                                  vx[:, pc, half, h, :], start=True, stop=True,
                                                  skip_group_check=True)
                        m.then_inc(weighted, 1)
                    if a:
                        for i in range(CH):
                            project(k, par, i)
                    if b:
                        first = 4 if c_ else 0
                        for i in range(CH):
                            pe.wait_ge(normed, kb * 4 + (i + 1))
                            bank = take(k, par, first + i)
                            for j in range(4):
                                m = pe.transpose(ring[:, bank, j * P:(j + 1) * P], rp[:, pb, i, j * P:(j + 1) * P],
                                                 c.ident[:])
                            m.then_inc(slot_full, 1)
                        pe.wait_ge(slot_free, slot(k, first + 3) + 1)
                        pe.wait_ge(k_before, kb + 1)
                        if c_:
                            pe.wait_ge(out_ready, kc + 1)
                        mask = c.local_first if isinstance(k, int) and k == 1 else c.local_mask
                        for i in range(4):
                            pe.matmul(so[:, i, 0:4 * KEYS], c.ident_b[:], mask[:], start=True, stop=False,
                                      skip_group_check=True)
                            for j in range(4):
                                h = 4 * i + j
                                for half in range(2):
                                    m = pe.matmul(so[HALF * half:HALF * half + HALF, i, j * KEYS:(j + 1) * KEYS],
                                                  qt[:, h // 2, HALF * half:HALF * half + HALF],
                                                  kz[:, pb, h, HALF * half:HALF * half + KEYS],
                                                  start=False, stop=True, skip_group_check=True)
                        m.then_inc(scored, 1)
                    if a:
                        for i in range(CH, 2 * CH):
                            project(k, par, i)
                    if c_:
                        first = 8 if b else 4
                        pe.wait_ge(out_ready, kc + 1)
                        for i in range(2):
                            bank = take(k, par, first + i)
                            for j in range(4):
                                p = 4 * i + j
                                m = pe.transpose(ring[:, bank, j * P:(j + 1) * P], otok[:, p * P:(p + 1) * P],
                                                 c.ident[:])
                            m.then_inc(slot_full, 1)
                        pe.wait_ge(slot_free, slot(k, first + 1) + 1)
                        bank = take(k, par, first + 2)
                        for p in range(LH // 2):
                            m = pe.matmul(ring[:, bank, 0:P], lw.wo[:, p, :], ots[:, p, :], start=(p == 0),
                                          stop=(p == LH // 2 - 1))
                        m.then_inc(slot_full, 1)

                pe.wait_ge(init, 2)
                pipeline(pe, step)

            @block.scalar
            def _(act):
                def step(k, par, a, b, c_):
                    kb, pb, kc, pc = k - 1, 1 - par, k - 2, par
                    one = isinstance(k, int) and k == 1

                    def bank_of(i):
                        act.wait_ge(slot_full, slot(k, i) + 1)
                        return i % 2 if one else (par + i) % 2

                    if c_:
                        if since(k, 3):
                            act.wait_ge(weighted, kc)
                        for i in range(4):
                            bank = bank_of(i)
                            act.activation(pts[:, 4 * i:4 * i + 4, :],
                                           ring[0:KEYS, bank, :].rearrange("p (j n) -> p j n", j=4),
                                           ACT.Copy).then_inc(slot_free, 1)
                    if a:
                        for i in range(CH):
                            act.wait_ge(projected, k * 8 + (i + 1))
                            if since(k, 1):
                                act.wait_ge(scaled_cos, (k - 1) * 4 + (i + 1))
                                act.wait_ge(scaled_sin, (k - 1) * 4 + (i + 1))
                            act.activation(raw[:, i, :], proj[:, i % 2, :], ACT.Copy).then_inc(raw_ready, 1)
                            if not (isinstance(k, int) and 4 * k + i < 2):
                                act.wait_ge(squares_summed, k * 4 + (i - 1))
                            act.activation(sq[:, i % 2, :], proj[:, i % 2, :], ACT.Square).then_inc(sq_ready, 1)
                    if b:
                        first = 4 if c_ else 0
                        if since(k, 2):
                            act.wait_ge(scored, kb)
                            act.wait_ge(k_before, kb)
                        for i in range(2):
                            bank = bank_of(first + i)
                            act.activation(qt[:, 4 * i:4 * i + 4, :],
                                           ring[:, bank, :].rearrange("p (j n) -> p j n", j=4),
                                           ACT.Copy).then_inc(slot_free, 1)
                        for i in range(2):
                            bank = bank_of(first + 2 + i)
                            for odd in range(2):
                                rows = slice(HALF * odd, HALF * odd + HALF)
                                m = act.activation(kz[rows, pb, 8 * i + odd:8 * i + 8:2, WIN:KZ],
                                                   ring[rows, bank, :].rearrange("p (j n) -> p j n", j=4), ACT.Copy)
                            m.then_inc(slot_free, 1)
                    if a:
                        if since(k, 2):
                            act.wait_ge(weighted, k - 1)
                        for i in range(CH, 2 * CH):
                            act.wait_ge(projected, k * 8 + (i + 1))
                            act.activation(vx[:, par, (i - CH) // 2, 8 * (i % 2):8 * (i % 2) + 8, 0:LD],
                                           proj[0:KEYS, i % 2, :].rearrange("p (h d) -> p h d", h=8),
                                           ACT.Copy).then_inc(values_ready, 1)
                        act.wait_ge(clamped, k + 1)
                        act.activation(lg[:], ss[:], ACT.Ln, scale=float(2 ** 20)).then_inc(logged, 1)
                        act.wait_ge(logged, k + 1)
                        if since(k, 1):
                            act.wait_ge(normed, k * 4)
                        act.activation(rn[:], lg[:], ACT.Exp, scale=-0.5, bias=c.v("ten_ln2")).then_inc(norms_ready, 1)
                    if b:
                        act.wait_ge(shifted, kb + 1)
                        act.activation(pw[:], pw[:], ACT.Exp).then_inc(weights_ready, 1)
                    if c_:
                        first = 8 if b else 4
                        for i in range(2):
                            bank = bank_of(first + i)
                            act.activation(ots[:, 4 * i:4 * i + 4, :],
                                           ring[:, bank, :].rearrange("p (j n) -> p j n", j=4),
                                           ACT.Copy).then_inc(slot_free, 1)
                        bank = bank_of(first + 2)
                        if since(k, 3):
                            act.wait_ge(y_added, kc)
                        act.activation(ysb[:], ring[:, bank, 0:P], ACT.Copy).then_inc(slot_free, 1)

                act.wait_ge(init, 2)
                pipeline(act, step)

            @block.vector
            def _(dve):
                def step(k, par, a, b, c_):
                    kb, pb, kc, pc = k - 1, 1 - par, k - 2, par
                    if c_:
                        dve.wait_ge(weighted, kc + 1)
                        dve.reciprocal(rec[:].rearrange("p (b j o) -> p b j o", b=4, j=4),
                                       so_heads[:, :, :, LD:LD + 1]).then_inc(inverted, 1)
                        dve.wait_ge(inverted, kc + 1)
                        if since(k, 3):
                            dve.wait_ge(slot_full, slot(k, 0))
                        dve.tensor_tensor(heads(otok[:].rearrange("p (h d) -> p h d", h=LH)),
                                          so_heads[:, :, :, 0:LD],
                                          heads(rec[:, :, None].to_broadcast([P, LH, LD])),
                                          ALU.mult).then_inc(out_ready, 1)
                    if a:
                        for i in range(CH):
                            tab = lw.cos_q if i < 2 else lw.cos_k
                            dve.wait_ge(raw_ready, k * 4 + (i + 1))
                            if since(k, 2) and i == 0:
                                dve.wait_ge(slot_full, slot(k, 0))
                            dve.tensor_tensor(rp[:, par, i, :].rearrange("p (h d) -> p h d", h=8),
                                              raw[:, i, :].rearrange("p (h d) -> p h d", h=8),
                                              tab[:, bass.ds(k * LD, LD)][:, None, :].to_broadcast([P, 8, LD]),
                                              ALU.mult).then_inc(scaled_cos, 1)
                            dve.wait_ge(sq_ready, k * 4 + (i + 1))
                            if since(k, 1) and i == 0:
                                dve.wait_ge(logged, k)
                            dve.tensor_reduce(ss[:, 8 * i:8 * i + 8],
                                              sq[:, i % 2, :].rearrange("p (h d) -> p h d", h=8),
                                              AX.X, ALU.add).then_inc(squares_summed, 1)
                        dve.wait_ge(squares_summed, k * 4 + 4)
                        dve.tensor_scalar(ss[:], ss[:], 1e-24, None, ALU.max).then_inc(clamped, 1)
                    if b:
                        dve.wait_ge(scored, kb + 1)
                        dve.tensor_reduce(mx[:].rearrange("p (b j) -> p b j", b=4), so_heads, AX.X,
                                          ALU.max).then_inc(max_ready, 1)
                        dve.wait_ge(max_ready, kb + 1)
                        if c_:
                            dve.wait_ge(slot_full, slot(k, 4))
                        dve.tensor_tensor(heads(pw[:]), so_heads,
                                          heads(mx[:, :, None].to_broadcast([P, LH, KEYS])),
                                          ALU.subtract).then_inc(shifted, 1)
                    if a:
                        dve.wait_ge(norms_ready, k + 1)
                        for i in range(CH):
                            dve.wait_ge(rotated, k * 4 + (i + 1))
                            r = rp[:, par, i, :].rearrange("p (h d) -> p h d", h=8)
                            dve.tensor_tensor(r, r, rn[:, 8 * i:8 * i + 8, None].to_broadcast([P, 8, LD]),
                                              ALU.mult).then_inc(normed, 1)

                dve.memset(vx[:], 1.0).then_inc(init, 1)
                dve.wait_ge(scaled_tables, 4)
                dve.wait_ge(init, 2)
                pipeline(dve, step)

            @block.gpsimd
            def _(pool):
                def take_tokens(k, par):
                    for rows, late in ((slice(0, HALF), 0), (slice(HALF, P), 1)):
                        m = pool.tensor_copy(xs[rows, par, :], xa[rows, bass.ds(k * P + (PAD - WIN - late), KZ)])
                    m.then_inc(xs_ready, 1)

                def step(k, par, a, b, c_):
                    kb, pb, kc, pc = k - 1, 1 - par, k - 2, par
                    if b:
                        if isinstance(k, int) and k == 1:
                            pool.wait_ge(init, 1)
                            pool.memset(kz[:, pb, :, 0:WIN], 0.0).then_inc(k_before, 1)
                        else:
                            pool.wait_ge(slot_free, slot(k, 0))
                            if since(k, 3):
                                pool.wait_ge(scored, kb - 1)
                            pool.tensor_tensor(kz[:, pb, :, 0:WIN], kz[:, par, :, P:KZ],
                                               c.v("k_before")[:, :, None].to_broadcast([P, LH, WIN]),
                                               ALU.mult).then_inc(k_before, 1)
                    if a:
                        def add_chunk(i):
                            pool.wait_ge(scaled_sin, k * 4 + (i + 1))
                            pool.wait_ge(scaled_cos, k * 4 + (i + 1))
                            pool.tensor_tensor(rp[:, par, i, :], rp[:, par, i, :], tm[:, i % 2, :],
                                               ALU.add).then_inc(rotated, 1)

                        for i in range(CH):
                            tab = lw.sin_q if i < 2 else lw.sin_k
                            pool.wait_ge(raw_ready, k * 4 + (i + 1))
                            if i >= 1:
                                add_chunk(i - 1)
                            for half in range(2):
                                t = tm[:, i % 2, :].rearrange("p (h e d) -> p h e d", h=8, e=2)[:, :, half, :]
                                r = raw[:, i, :].rearrange("p (h e d) -> p h e d", h=8, e=2)[:, :, 1 - half, :]
                                w = tab[:, bass.ds(k * LD + half * (LD // 2), LD // 2)][:, None, :]
                                m = pool.tensor_tensor(t, r, w.to_broadcast([P, 8, LD // 2]), ALU.mult)
                            m.then_inc(scaled_sin, 1)
                        add_chunk(CH - 1)
                        if since(k, 1):
                            pool.wait_ge(projected, k * 8)
                        pool.wait_ge(rotated, k * 4 + 4)
                        take_tokens(k + 1, 1 - par)
                        pool.wait_ge(xs_ready, k + 2)
                    if c_:
                        first = 8 if b else 4
                        pool.wait_ge(slot_free, slot(k, first + 2) + 1)
                        at = bass.ds(kc * P + PAD, P)
                        pool.tensor_tensor(xb[:, at], xa[:, at], ysb[:], ALU.add).then_inc(y_added, 1)

                pool.memset(kz[:], 0.0).then_inc(init, 1)
                for tab, scale in ((lw.cos_q, 0), (lw.sin_q, 1), (lw.cos_k, 2), (lw.sin_k, 3)):
                    t = tab[:, 0:NT * LD].rearrange("p (t d) -> p t d", t=NT)
                    pool.tensor_tensor(t, t, lw.qk_scale[:, scale, None, :].to_broadcast([P, NT, LD]),
                                       ALU.mult).then_inc(scaled_tables, 1)
                pool.wait_ge(scaled_tables, 4)
                take_tokens(0, 0)
                pipeline(pool, step)


def local_ffn(nc, c, lw, xn, xb, xa, prefetch):
    with ExitStack() as ctx:
        def sb(name, shape):
            return ctx.enter_context(on_chip(nc.sbuf_tensor, name, shape, F32))

        gl = sb("lf_gl", [P, 2, GW])
        hd = sb("lf_h", [P, 2, 3, GW])
        ap = ctx.enter_context(on_chip(nc.psum_tensor, "lf_a", [P, 2, GW], F32))
        gp = ctx.enter_context(on_chip(nc.psum_tensor, "lf_g", [P, 2, GW], F32))
        yp = ctx.enter_context(on_chip(nc.psum_tensor, "lf_y", [P, 2, GW], F32))
        with phase(nc, "up", "gelu_done", "h_ready", "down", "added", "fetched") as (
                block, up, gelu_done, h_ready, down, added, fetched):
            @block.sync
            def _(sp):
                n = prefetch(sp, fetched)
                sp.wait_ge(fetched, 16 * n)

            @block.tensor
            def _(pe):
                def chunk(g, j):
                    n = 3 * g + j
                    m = FF_ROWS[j]
                    if n >= 2:
                        pe.wait_ge(h_ready, n - 1)
                    pe.matmul(gp[0:m, n % 2, :], lw.w1[:, FF + j * P:FF + j * P + m], xn[:, group(g)],
                              start=True, stop=True)
                    pe.matmul(ap[0:m, n % 2, :], lw.w1[:, j * P:j * P + m], xn[:, group(g)],
                              start=True, stop=True).then_inc(up, 1)

                def downs(g):
                    pe.wait_ge(h_ready, 3 * g + 3)
                    if g >= 2:
                        pe.wait_ge(added, g - 1)
                    for j in range(3):
                        m = pe.matmul(yp[:, g % 2, :], lw.w2[0:FF_ROWS[j], j, :], hd[0:FF_ROWS[j], g % 2, j, :],
                                      start=(j == 0), stop=(j == 2))
                    m.then_inc(down, 1)

                for g in range(NG):
                    for j in range(3):
                        chunk(g, j)
                        if j == 1 and g:
                            downs(g - 1)
                downs(NG - 1)

            @block.scalar
            def _(act):
                for n in range(3 * NG):
                    j, m = n % 3, FF_ROWS[n % 3]
                    act.wait_ge(up, n + 1)
                    if n >= 2:
                        act.wait_ge(h_ready, n - 1)
                    act.activation(gl[0:m, n % 2, :], gp[0:m, n % 2, :], ACT.Gelu,
                                   bias=lw.vec[0:m, 3 + j:4 + j]).then_inc(gelu_done, 1)

            @block.vector
            def _(dve):
                def add_y(g):
                    dve.wait_ge(down, g + 1)
                    dve.scalar_tensor_tensor(out=xa[:, PAD + g * GW:PAD + (g + 1) * GW], in0=yp[:, g % 2, :],
                                             scalar=lw.vec[:, 6:7], in1=xb[:, PAD + g * GW:PAD + (g + 1) * GW],
                                             op0=ALU.add, op1=ALU.add).then_inc(added, 1)

                for g in range(NG):
                    for j in range(3):
                        n, m = 3 * g + j, FF_ROWS[j]
                        dve.wait_ge(gelu_done, n + 1)
                        if g >= 2:
                            dve.wait_ge(down, g - 1)
                        dve.scalar_tensor_tensor(out=hd[0:m, g % 2, j, :], in0=ap[0:m, n % 2, :],
                                                 scalar=lw.vec[0:m, j:j + 1], in1=gl[0:m, n % 2, :],
                                                 op0=ALU.add, op1=ALU.mult).then_inc(h_ready, 1)
                    if g:
                        add_y(g - 1)
                add_y(NG - 1)


def project_qk(nc, c, kind, w, xn, qk):
    n = 2 * NG
    scale = float(1 / np.sqrt(np.float32(DH)))
    with ExitStack() as ctx:
        def sb(name, shape):
            return ctx.enter_context(on_chip(nc.sbuf_tensor, name, shape, F32))

        t1 = sb("qk_t1", [P, 2, GW])
        t2 = sb("qk_t2", [P, 2, GW])
        t3 = sb("qk_t3", [P, 2, GW])
        t4 = sb("qk_t4", [P, 2, GW])
        own = ctx.enter_context(on_chip(nc.psum_tensor, "qk_own", [P, 2, GW], F32))
        other = ctx.enter_context(on_chip(nc.psum_tensor, "qk_other", [P, 2, GW], F32))
        sums = ctx.enter_context(on_chip(nc.psum_tensor, "qk_sums", [P, 2, GW], F32))
        with phase(nc, "projected", "step", "done", "squared", "summed", "clamped", "logged", "norm_ready") as (
                block, projected, step, done, squared, summed, clamped, logged, norm_ready):
            @block.tensor
            def _(pe):
                for u in range(n):
                    x, g = divmod(u, NG)
                    if u >= 2:
                        pe.wait_ge(done, u - 1)
                    m = pe.matmul(own[:, u % 2, :], w[:, x * P:(x + 1) * P], xn[:, group(g)], start=True, stop=True)
                    if kind != "plain":
                        m = pe.matmul(other[:, u % 2, :], w[:, (2 + x) * P:(3 + x) * P], xn[:, group(g)],
                                      start=True, stop=True)
                    m.then_inc(projected, 1)
                    if kind == "channel":
                        pe.wait_ge(squared, u + 1)
                        pe.matmul(sums[:, u % 2, :], c.head_ones[:], t2[:, u % 2, :], start=True,
                                  stop=True).then_inc(summed, 1)

            @block.scalar
            def _(act):
                if kind != "channel":
                    return
                for u in range(n):
                    act.wait_ge(step, 2 * u + 2)
                    act.activation(t2[:, u % 2, :], qk[:, u // NG, group(u % NG)], ACT.Square).then_inc(squared, 1)
                    act.wait_ge(clamped, u + 1)
                    act.activation(t3[:, u % 2, :], t3[:, u % 2, :], ACT.Ln, scale=float(2 ** 20)).then_inc(logged, 1)
                    act.wait_ge(logged, u + 1)
                    act.activation(t4[:, u % 2, :], t3[:, u % 2, :], ACT.Exp, scale=-0.5,
                                   bias=c.v("ten_ln2")).then_inc(norm_ready, 1)

            @block.vector
            def _(dve):
                for u in range(n):
                    x, g = divmod(u, NG)
                    to = qk[:, x, group(g)]
                    dve.wait_ge(projected, u + 1)
                    if kind == "plain":
                        dve.tensor_scalar(to, own[:, u % 2, :], scale if x == 0 else 1.0, None,
                                          ALU.mult).then_inc(done, 1)
                        continue
                    if kind == "channel":
                        dve.tensor_scalar(t1[:, u % 2, :], other[:, u % 2, :], c.v("ch_sin"), None,
                                          ALU.mult).then_inc(step, 1)
                        dve.wait_ge(step, 2 * u + 1)
                        dve.scalar_tensor_tensor(out=to, in0=own[:, u % 2, :], scalar=c.v("ch_cos"),
                                                 in1=t1[:, u % 2, :], op0=ALU.mult, op1=ALU.add).then_inc(step, 1)
                        dve.wait_ge(summed, u + 1)
                        dve.tensor_scalar(t3[:, u % 2, :], sums[:, u % 2, :], 1e-24, None,
                                          ALU.max).then_inc(clamped, 1)
                        dve.wait_ge(norm_ready, u + 1)
                        dve.scalar_tensor_tensor(out=to, in0=to, scalar=c.qkscale[:, 0:1] if x == 0 else 1.0,
                                                 in1=t4[:, u % 2, :], op0=ALU.mult, op1=ALU.mult).then_inc(done, 1)
                        continue
                    dve.tensor_tensor(t1[:, u % 2, :], own[:, u % 2, :], c.rope_cos[:, group(g)], ALU.mult).then_inc(step, 1)
                    dve.tensor_tensor(t2[:, u % 2, :], other[:, u % 2, :], c.rope_sin[:, group(g)], ALU.mult).then_inc(step, 1)
                    dve.wait_ge(step, 3 * u + 2)
                    dve.tensor_tensor(t3[:, u % 2, :], t1[:, u % 2, :], t2[:, u % 2, :], ALU.add).then_inc(step, 1)
                    dve.wait_ge(step, 3 * u + 3)
                    dve.tensor_scalar(to, t3[:, u % 2, :], scale if x == 0 else 1.0, None, ALU.mult).then_inc(done, 1)


def add_into(nc, x, y):
    with phase(nc, "added") as (block, added):
        @block.vector
        def _(dve):
            dve.tensor_tensor(x, x, y, ALU.add).then_inc(added, 1)
            dve.wait_ge(added, 1)


class Names:
    pass


VECTORS = ["a_ln1_s", "a_ln1_b", "a_ln2_s", "a_ln2_b", "a_b1", "a_b1_1", "a_b1_2", "a_b1_3", "a_b2",
           "b_g", "b_b", "c_g", "c_b"]
SHAPE_VECTORS = ["eps5", "eps6", "ten_ln2", "k_before", "ch_sin", "ch_cos"]


def build(nc, io, out, part):
    root = ExitStack()
    with root:
        c = Names()

        def keep(name, shape, dt=F32, ctx=root):
            return ctx.enter_context(on_chip(nc.sbuf_tensor, name, shape, dt))

        x = keep("x", [P, T])
        c.ident = keep("ident", [P, P])
        c.ident_b = keep("ident_b", [P, P], BF16)
        c.flip_b = keep("flip_b", [P, P], BF16)
        c.mean_w = keep("mean_w", [P, P])
        c.vecs = keep("vecs", [P, len(VECTORS)])
        c.svecs = keep("svecs", [P, len(SHAPE_VECTORS)])

        def v(name, j=0):
            if name in VECTORS:
                i = VECTORS.index(name) + j
                return c.vecs[:, i:i + 1]
            i = SHAPE_VECTORS.index(name)
            return c.svecs[:, i:i + 1]

        c.v = v
        load_constants(nc, [(x[:], io["tokens"]), (c.ident[:], io["c_ident"]), (c.ident_b[:], io["c_ident_b"]), (c.flip_b[:], io["c_flip_b"]),
                            (c.mean_w[:], io["c_mean"]), (c.vecs[:], io["vecs"]), (c.svecs[:], io["c_svecs"])])

        def performer_layer():
            with ExitStack() as ctx:
                u = keep("s1_u", [P, T], ctx=ctx)
                layer_norm(nc, c, x, u, v("eps5"))
                n = keep("s1_n", [P, T], ctx=ctx)
                layer_norm(nc, c, u, n, v("eps6"), v("a_ln1_s"), v("a_ln1_b"))
                w = Names()
                at = keep("s1_at", [P, T], ctx=ctx)
                w.wo = keep("s1_wo", [P, P], ctx=ctx)
                with ExitStack() as ctx2:
                    ot = keep("s1_ot", [P, QUADS, T], ctx=ctx2)
                    w.pq = keep("s1_wq", [P, P], ctx=ctx2)
                    w.pkv = keep("s1_wkv", [P, 2 * P], ctx=ctx2)
                    c.causal = keep("causal", [P, P], ctx=ctx2)
                    c.head_mask = keep("head_mask", [P, H], ctx=ctx2)
                    c.block_mask = keep("block_mask", [P, H * 32], ctx=ctx2)
                    load_constants(nc, [(w.pq[:], io["a_wq"]), (w.pkv[:], io["a_wkv"]), (w.wo[:], io["a_wo"]),
                                        (c.causal[:], io["c_causal"]), (c.head_mask[:], io["c_head_mask"]),
                                        (c.block_mask[:], io["c_block_mask"])])
                    performer(nc, c, w, n, ot)
                    normalise_heads(nc, c, ot, at)
                project_add(nc, w.wo, at, u, [u])
                layer_norm(nc, c, u, n, v("eps6"), v("a_ln2_s"), v("a_ln2_b"))
                w.w1 = keep("s1_w1", [P, 4 * P], ctx=ctx)
                w.w2 = keep("s1_w2", [P, 4, P], ctx=ctx)
                load_constants(nc, [(w.w1[:], io["a_w1"]), (w.w2[:], io["a_w2"])])
                gelu_mlp(nc, c, w, n, u, x)

        def mixture():
            with ExitStack() as ctx:
                u = keep("s2_u", [P, T], ctx=ctx)
                w = Names()
                w.router = keep("s2_router", [P, E], ctx=ctx)
                w.wg = keep("s2_wg", [P, 4 * P], ctx=ctx)
                w.wu = keep("s2_wu", [P, 4 * P], ctx=ctx)
                w.wd = keep("s2_wd", [P, 4, P], ctx=ctx)
                w.wgs = keep("s2_wgs", [P, P], ctx=ctx)
                w.wus = keep("s2_wus", [P, P], ctx=ctx)
                w.wds = keep("s2_wds", [P, P], ctx=ctx)
                c.sel = keep("s2_sel", [E, 4, P], ctx=ctx)
                c.iota = keep("s2_iota", [P, E], ctx=ctx)
                load_constants(nc, [(w.router[:], io["m_router"]), (w.wg[:], io["m_wg"]), (w.wu[:], io["m_wu"]),
                                    (w.wd[:], io["m_wd"]), (w.wgs[:], io["m_wgs"]), (w.wus[:], io["m_wus"]),
                                    (w.wds[:], io["m_wds"]), (c.sel[:], io["c_sel"]), (c.iota[:], io["c_iota"])])
                layer_norm(nc, c, x, u, v("eps5"))
                experts(nc, c, w, u, x)

        def attention(kind, gamma, beta, w_qk, w_v, w_o, residual):
            with ExitStack() as ctx:
                u = keep("s3_u", [P, T], ctx=ctx)
                layer_norm(nc, c, x, u, v("eps5"))
                wv = keep("s3_wv", [P, P], ctx=ctx)
                wo = keep("s3_wo", [P, P], ctx=ctx)
                vv = keep("s3_v", [P, NT, 176], ctx=ctx)
                with ExitStack() as ctx2:
                    xn = u
                    if gamma is not None:
                        xn = keep("s3_n", [P, T], ctx=ctx2)
                        layer_norm(nc, c, u, xn, v("eps5"), gamma, beta)
                    qk = keep("s3_qk", [P, 2, T], ctx=ctx2)
                    cols = io[w_qk].shape[1]
                    wqk = keep("s3_wqk", [P, cols], ctx=ctx2)
                    loads = [(wqk[:], io[w_qk]), (wv[:], io[w_v]), (wo[:], io[w_o])]
                    if kind == "channel":
                        c.head_ones = keep("head_ones", [P, P], ctx=ctx2)
                        c.qkscale = keep("qkscale", [P, 1], ctx=ctx2)
                        loads += [(c.head_ones[:], io["c_head_ones"]),
                                  (c.qkscale[:], io["c_scale"])]
                    if kind == "position":
                        c.rope_cos = keep("rope_cos", [P, T], ctx=ctx2)
                        c.rope_sin = keep("rope_sin", [P, T], ctx=ctx2)
                        loads += [(c.rope_cos[:], io["c_rope_cos"]), (c.rope_sin[:], io["c_rope_sin"])]
                    load_constants(nc, loads)
                    project_qk(nc, c, kind, wqk, xn, qk)
                    values(nc, wv, xn, vv)
                    split_parts(nc, qk[:, 0, :], io["s_q"])
                    split_parts(nc, qk[:, 1, :], io["s_k"])
                if kind == "plain":
                    near_tables(nc, c, io)
                with ExitStack() as ctx2:
                    ot = keep("s3_ot", [P, QUADS, T], ctx=ctx2)
                    with ExitStack() as ctx3:
                        if kind != "plain":
                            c.mask_a = keep("mask_a", [P, P], BF16, ctx=ctx3)
                            c.mask_b = keep("mask_b", [P, P], BF16, ctx=ctx3)
                            load_constants(nc, [(c.mask_a[:], io["c_mask_a"]), (c.mask_b[:], io["c_mask_b"])])
                        causal_attention(nc, c, io, vv, ot, kind == "plain")
                    at = keep("s3_at", [P, T], ctx=ctx2)
                    normalise_heads(nc, c, ot, at)
                    project_add(nc, wo, at, x, [x, u] if residual else [x])

        def local_layers():
            with ExitStack() as ctx:
                wide = PAD + T + P
                xa = keep("l_xa", [P, wide], ctx=ctx)
                xb = keep("l_xb", [P, wide], ctx=ctx)
                layer_norm(nc, c, x, xb[:, PAD:PAD + T], v("eps5"))
                lw = Names()
                lw.qkv = keep("l_qkv", [P, 3 * INNER], ctx=ctx)
                lw.wo = keep("l_wo", [P, LH // 2, P], ctx=ctx)
                lw.w1 = keep("l_w1", [P, 2 * FF], ctx=ctx)
                lw.w2 = keep("l_w2", [P, 3, P], ctx=ctx)
                lw.vec = keep("l_vec", [P, 9], ctx=ctx)
                lw.tables = keep("l_tables", [P, 4, NT * LD], ctx=ctx)
                lw.cos_q, lw.sin_q, lw.cos_k, lw.sin_k = (lw.tables[:, i, :] for i in range(4))
                lw.qk_scale = keep("l_qk_scale", [P, 4, LD], ctx=ctx)
                c.local_mask = keep("local_mask", [P, 4 * KEYS], BF16, ctx=ctx)
                c.local_first = keep("local_first", [P, 4 * KEYS], BF16, ctx=ctx)

                def fetch(pairs):
                    def start(sp, sem):
                        for dst, src in pairs:
                            sp.dma_start(dst, src).then_inc(sem, 16)
                        return len(pairs)
                    return start

                load_constants(nc, [(c.local_mask[:], io["c_local_mask"]), (c.local_first[:], io["c_local_first"])]
                               + attention_weights_at(io, lw, 0))
                with phase(nc, "copied", "cleared") as (block, copied, cleared):
                    @block.gpsimd
                    def _(pool):
                        for b in (xa, xb):
                            pool.memset(b[:, 0:PAD], 0.0).then_inc(cleared, 1)
                            pool.memset(b[:, PAD + T:], 0.0).then_inc(cleared, 1)

                    @block.vector
                    def _(dve):
                        dve.tensor_copy(xa[:, PAD:PAD + T], xb[:, PAD:PAD + T]).then_inc(copied, 1)
                with nc.Fori(0, LAYERS) as layer:
                    local_attention(nc, c, lw, xa, xb, fetch(ffn_weights_at(io, lw, layer)))
                    with ExitStack() as ctx2:
                        xs = keep("l_xs", [P, T], ctx=ctx2)
                        xn = keep("l_xn", [P, T], ctx=ctx2)
                        layer_norm(nc, c, xs, xn, v("eps5"), lw.vec[:, 7:8], lw.vec[:, 8:9], shift_from=xb)
                        local_ffn(nc, c, lw, xn, xb, xa, fetch(attention_weights_at(io, lw, layer + 1)))
                add_into(nc, x[:], xa[:, PAD:PAD + T])

        stages = [
            performer_layer,
            mixture,
            lambda: attention("plain", v("b_g"), v("b_b"), "b_wqk", "b_wv", "b_wo", True),
            mixture,
            lambda: attention("channel", v("c_g"), v("c_b"), "c_wqk", "c_wv", "c_wo", False),
            local_layers,
            lambda: attention("position", None, None, "d_wqk", "d_wv", "d_wo", False),
            local_layers,
        ]
        for stage in stages[part]:
            stage()

        with phase(nc, "stored") as (block, stored):
            @block.sync
            def _(sp):
                sp.dma_start(out, x[:]).then_inc(stored, 16)
                sp.wait_ge(stored, 16)


def layer_of(a, layer):
    return a[bass.ds(layer, 1)].rearrange("o p n -> (o p) n")


def attention_weights_at(io, lw, layer):
    return [(lw.qkv[:], layer_of(io["l_qkv"], layer)),
            (lw.wo[:].rearrange("p a d -> p (a d)"), layer_of(io["l_wo"], layer)),
            (lw.tables[:].rearrange("p a d -> p (a d)"), io["c_tables"]),
            (lw.qk_scale[:].rearrange("p a d -> p (a d)"), layer_of(io["l_qk_scale"], layer))]


def ffn_weights_at(io, lw, layer):
    return [(lw.w1[:], layer_of(io["l_w1"], layer)),
            (lw.w2[:].rearrange("p a d -> p (a d)"), layer_of(io["l_w2"], layer)),
            (lw.vec[:], layer_of(io["l_vec"], layer))]


def shape_constants():
    bf = mybir.dt.np(BF16)
    f = np.float32
    i = np.arange(P)
    k = {}
    k["c_ident"] = np.eye(P, dtype=f)
    k["c_ident_b"] = np.eye(P).astype(bf)
    k["c_flip_b"] = np.eye(P)[::-1].astype(bf)
    k["c_mean"] = np.full((P, P), 1 / P, f)
    k["c_causal"] = (i[:, None] <= i[None, :]).astype(f)
    k["c_head_mask"] = (i[:, None] // DH == np.arange(H)[None, :]).astype(f)
    k["c_block_mask"] = (i[:, None] // DH == np.arange(H * 32)[None, :] // 32).astype(f)
    k["c_head_ones"] = (i[:, None] // DH == i[None, :] // DH).astype(f)
    k["c_mask_a"] = np.where(i[None, :] > i[:, None], NEG, 0).astype(bf)
    k["c_mask_b"] = np.where(i[:, None] > i[None, :], NEG, 0).astype(bf)
    k["c_zero"] = np.zeros((3, 4 * T), bf)
    k["c_sel"] = (np.arange(E)[:, None] == np.arange(4 * P)[None, :] // (P // 4)).astype(f)
    k["c_iota"] = np.tile(np.arange(E, dtype=f), (P, 1))
    q, key = np.arange(P) % HALF, np.arange(KEYS)
    seen = (q[:, None] <= key[None, :]) & (key[None, :] <= q[:, None] + WIN)
    first = seen & ((key[None, :] >= WIN) | (i[:, None] >= HALF))
    k["c_local_mask"] = np.tile(np.where(seen, 0, NEG), (1, 4)).astype(bf)
    k["c_local_first"] = np.tile(np.where(first, 0, NEG), (1, 4)).astype(bf)
    inv = f(10000.0) ** (np.arange(0, DH, 2, dtype=f) / f(DH))
    ang = (np.arange(T, dtype=f)[:, None] / inv[None, :]).astype(f)
    cos, sin = np.cos(ang).astype(f), np.sin(ang).astype(f)
    pair = (i % DH) // 2
    k["c_rope_cos"] = np.ascontiguousarray(cos[:, pair].T)
    k["c_rope_sin"] = np.ascontiguousarray((sin[:, pair] * np.where(i % 2 == 0, -1, 1)[None, :]).T.astype(f))
    freq = np.repeat(f(10000.0) ** (-(np.arange(0, P, 2, dtype=f) / f(P))), 2).astype(f)
    ch = (f(T) * freq).astype(f)
    half = np.arange(0, LD, 2, dtype=f)
    freqs = (np.arange(T, dtype=f)[:, None] * (f(1) / f(10000.0) ** (half / f(LD)))[None, :]).astype(f)
    base = ((half.astype(np.float64) + 0.4 * LD) / (1.4 * LD))
    grow = base[None, :] ** ((np.arange(T) % P)[:, None] / (WIN // 2))
    cos, sin = np.cos(freqs).astype(np.float64), np.sin(freqs).astype(np.float64)
    tables = []
    for g in (8.0 * grow, 1 / grow):
        tables += [np.concatenate([cos * g, cos * g], -1), np.concatenate([-sin * g, sin * g], -1)]
    k["c_tables"] = np.ascontiguousarray(
        np.stack(tables).reshape(4, NT, P, LD).transpose(2, 0, 1, 3).reshape(P, 4 * NT * LD).astype(f))
    cols = {
        "eps5": np.full(P, 1e-5), "eps6": np.full(P, 1e-6), "ten_ln2": np.full(P, 10 * np.log(2)),
        "k_before": np.tile(base ** (P // (WIN // 2)), 4),
        "ch_sin": np.sin(ch) * np.where(i < P // 2, -1, 1), "ch_cos": np.cos(ch),
    }
    k["c_svecs"] = np.stack([cols[n] for n in SHAPE_VECTORS], 1).astype(f)
    return k


def lay_out(a):
    r = {n: np.asarray(x) for n, x in a.items()}
    m = {}
    m["tokens"] = r["L0_attn_a_inputs"][0].T
    b1 = r["L0_attn_a_b1"].reshape(4, P)
    m["vecs"] = np.stack([r["L0_attn_a_ln1_scale"], r["L0_attn_a_ln1_bias"], r["L0_attn_a_ln2_scale"],
                          r["L0_attn_a_ln2_bias"], *b1, r["L0_attn_a_b2"], r["L0_attn_b_ln_gamma"],
                          r["L0_attn_b_ln_beta"], r["L1_attn_a_ln_gamma"], r["L1_attn_a_ln_beta"]], 1)
    m["a_wq"] = r["L0_attn_a_wq"].reshape(P, P)
    m["a_wkv"] = np.concatenate([r["L0_attn_a_wk"].reshape(P, P), r["L0_attn_a_wv"].reshape(P, P)], 1)
    m["a_wo"] = r["L0_attn_a_wo"].reshape(P, P)
    m["a_w1"] = r["L0_attn_a_w1"]
    m["a_w2"] = r["L0_attn_a_w2"].reshape(4, P, P).transpose(1, 0, 2)
    m["m_router"] = r["L0_ffn_router_w"]
    m["m_wg"] = r["L0_ffn_wg_r"].transpose(1, 0, 2).reshape(P, 4 * P)
    m["m_wu"] = r["L0_ffn_wu_r"].transpose(1, 0, 2).reshape(P, 4 * P)
    m["m_wd"] = r["L0_ffn_wd_r"].reshape(4, P, P).transpose(1, 0, 2)
    m["m_wgs"] = r["L0_ffn_wg_s"].transpose(1, 0, 2).reshape(P, P)
    m["m_wus"] = r["L0_ffn_wu_s"].transpose(1, 0, 2).reshape(P, P)
    m["m_wds"] = r["L0_ffn_wd_s"].reshape(P, P)
    m["b_wqk"] = np.concatenate([r["L0_attn_b_Wq"].T, r["L0_attn_b_Wk"].T], 1)
    m["b_wv"] = r["L0_attn_b_Wv"].T
    m["b_wo"] = r["L0_attn_b_Wo"].T
    m["rel"] = np.stack([r["L0_attn_b_rel"], r["L0_attn_b_rel"][:, ::-1]], 1)
    w = r["L1_attn_a_w_qkv"]
    partner = np.concatenate([np.arange(1, P, 2), np.arange(0, P, 2)])
    m["c_wqk"] = np.concatenate([w[:, 0:P], w[:, P:2 * P], w[:, 0:P][:, partner], w[:, P:2 * P][:, partner]], 1)
    m["c_wv"] = w[:, 2 * P:]
    m["c_wo"] = r["L1_attn_a_w_out"]
    m["c_scale"] = np.broadcast_to(r["L1_attn_a_qkscale"].reshape(1, 1), (P, 1))
    w = r["L1_attn_b_W_qkv"].T
    partner = np.arange(P) ^ 1
    m["d_wqk"] = np.concatenate([w[:, 0:P], w[:, P:2 * P], w[:, 0:P][:, partner], w[:, P:2 * P][:, partner]], 1)
    m["d_wv"] = w[:, 2 * P:]
    m["d_wo"] = r["L1_attn_b_W_o"].T

    def again(x):
        return np.concatenate([x, x[:1]])

    m["l_qkv"] = again(r["L1_ffn_Wqkv"])
    m["l_wo"] = again(r["L1_ffn_Wo"].reshape(LAYERS, LH // 2, P, P).transpose(0, 2, 1, 3).reshape(LAYERS, P, INNER))
    qs, ks = r["L1_ffn_q_scale"], r["L1_ffn_k_scale"]

    def swap(s):
        return np.concatenate([s[:, LD // 2:], s[:, :LD // 2]], 1)

    scales = np.stack([qs, swap(qs), ks, swap(ks)], 1).reshape(LAYERS, 1, 4 * LD)
    m["l_qk_scale"] = again(np.broadcast_to(scales, (LAYERS, P, 4 * LD)))
    m["l_w1"] = again(r["L1_ffn_W1"])
    w2 = np.zeros((LAYERS, 3 * P, P), np.float32)
    w2[:, :FF] = r["L1_ffn_W2"]
    m["l_w2"] = again(w2.reshape(LAYERS, 3, P, P).transpose(0, 2, 1, 3).reshape(LAYERS, P, 3 * P))
    b = np.zeros((LAYERS, 6, P), np.float32)
    for half in range(2):
        part = np.zeros((LAYERS, 3 * P), np.float32)
        part[:, :FF] = r["L1_ffn_b1"][:, half * FF:(half + 1) * FF]
        b[:, 3 * half:3 * half + 3] = part.reshape(LAYERS, 3, P)
    vec = np.concatenate([b, r["L1_ffn_b2"][:, None], r["L1_ffn_ln_g"][:, None], r["L1_ffn_ln_b"][:, None]], 1)
    m["l_vec"] = again(vec.transpose(0, 2, 1))
    return {n: np.ascontiguousarray(x) for n, x in m.items()}


def program(nc, arrays, part=slice(None)):
    io = {}
    for name, a in arrays.items():
        io[name] = nc.dram_tensor(name, a.shape, mybir.dt.from_np(a.dtype), kind="ExternalInput").ap()
    io["s_q"] = nc.dram_tensor("s_q", (3, P, T), BF16, kind="Internal").ap()
    io["s_k"] = nc.dram_tensor("s_k", (3, P, T), BF16, kind="Internal").ap()
    io["s_ext"] = nc.dram_tensor("s_ext", (3, H, 2, 3 * P), BF16, kind="Internal").ap()
    out = nc.dram_tensor("out", (P, T), F32, kind="ExternalOutput").ap()
    build(nc, io, out, part)


def kernel(**inputs):
    import concourse.bacc as bacc
    from concourse.bass_utils import run_bass_kernel_spmd

    nc = bacc.Bacc("TRN2", target_bir_lowering=False, num_devices=1)
    arrays = {**lay_out(inputs), **shape_constants()}
    program(nc, arrays)
    r = run_bass_kernel_spmd(nc, [arrays], core_ids=[0])
    return np.ascontiguousarray(r.results[0]["out"].T)[None]
```

```python
import itertools
from contextlib import ExitStack, contextmanager

import numpy as np

import concourse.bass as bass
from concourse import mybir

F32 = mybir.dt.float32
BF16 = mybir.dt.bfloat16
U32 = mybir.dt.uint32
ALU = mybir.AluOpType
ACT = mybir.ActivationFunctionType
AX = mybir.AxisListType

P = 128
T = 2048
NT = T // P
GW = 512
NG = T // GW
H = 16
DH = P // H
QUADS = H // 4
VW = DH + 1
NEG = -1e30

E = 16
LAYERS = 6
LH = 16
LD = 64
INNER = LH * LD
WIN = 32
HALF = 64
KEYS = HALF + WIN
FF = int(P * 4 * 2 / 3)
FF_ROWS = [P, P, FF - 2 * P]
PAD = WIN + 1

SEM_BASE = 110
USES = itertools.count()


def on_chip(allocate, name, shape, dtype):
    return allocate(f"{name}_{next(USES)}", shape, dtype)


@contextmanager
def phase(nc, *names):
    with ExitStack() as ctx:
        sems = [ctx.enter_context(nc.semaphore(name=n, num=SEM_BASE + i)) for i, n in enumerate(names)]
        with nc.Block() as block:
            yield (block, *sems)
        nc.all_engine_barrier(sems_to_clear=range(SEM_BASE, SEM_BASE + len(names)))


def group(g):
    return slice(g * GW, (g + 1) * GW)


def load_constants(nc, pairs):
    with phase(nc, "loaded") as (block, loaded):
        @block.sync
        def _(sp):
            for dst, src in pairs:
                sp.dma_start(dst, src).then_inc(loaded, 16)
            sp.wait_ge(loaded, 16 * len(pairs))


def layer_norm(nc, c, src, dst, eps, gamma=None, beta=None, shift_from=None):
    with ExitStack() as ctx:
        xc = ctx.enter_context(on_chip(nc.sbuf_tensor, "ln_centered", [P, T], F32))
        sq = ctx.enter_context(on_chip(nc.sbuf_tensor, "ln_squares", [P, 2, GW], F32))
        lv = ctx.enter_context(on_chip(nc.sbuf_tensor, "ln_logvar", [P, 2, GW], F32))
        rs = ctx.enter_context(on_chip(nc.sbuf_tensor, "ln_rstd", [P, 2, GW], F32))
        mean = ctx.enter_context(on_chip(nc.psum_tensor, "ln_mean", [P, 2, GW], F32))
        var = ctx.enter_context(on_chip(nc.psum_tensor, "ln_var", [P, 2, GW], F32))
        with phase(nc, "mean_ready", "centered", "squared", "var_ready", "log_ready", "rstd_ready",
                   "normed", "scaled", "taken") as (
                block, mean_ready, centered, squared, var_ready, log_ready, rstd_ready, normed, scaled,
                taken):
            @block.tensor
            def _(pe):
                def mean_of(g):
                    if shift_from is not None:
                        pe.wait_ge(taken, g + 1)
                    if g >= 2:
                        pe.wait_ge(centered, g - 1)
                    pe.matmul(mean[:, g % 2, :], c.mean_w[:], src[:, group(g)],
                              start=True, stop=True).then_inc(mean_ready, 1)

                mean_of(0)
                for g in range(NG):
                    if g + 1 < NG:
                        mean_of(g + 1)
                    pe.wait_ge(squared, g + 1)
                    if g >= 2:
                        pe.wait_ge(log_ready, g - 1)
                    pe.matmul(var[:, g % 2, :], c.mean_w[:], sq[:, g % 2, :],
                              start=True, stop=True).then_inc(var_ready, 1)

            def rstd(act, g):
                act.wait_ge(var_ready, g + 1)
                act.activation(lv[:, g % 2, :], var[:, g % 2, :], ACT.Ln, bias=eps).then_inc(log_ready, 1)
                act.wait_ge(log_ready, g + 1)
                if g >= 2:
                    act.wait_ge(normed, g - 1)
                act.activation(rs[:, g % 2, :], lv[:, g % 2, :], ACT.Exp, scale=-0.5).then_inc(rstd_ready, 1)

            @block.scalar
            def _(act):
                act.preload_act_table_set("natural_log_exp_and_others")
                for g in range(NG):
                    act.wait_ge(centered, g + 1)
                    if g >= 2:
                        act.wait_ge(var_ready, g - 1)
                    act.activation(sq[:, g % 2, :], xc[:, group(g)], ACT.Square).then_inc(squared, 1)
                    if g >= 1:
                        rstd(act, g - 1)
                rstd(act, NG - 1)

            @block.vector
            def _(dve):
                def center(g):
                    dve.wait_ge(mean_ready, g + 1)
                    if shift_from is not None:
                        dve.wait_ge(taken, g + 1)
                    dve.tensor_tensor(xc[:, group(g)], src[:, group(g)], mean[:, g % 2, :],
                                      ALU.subtract).then_inc(centered, 1)

                if shift_from is not None:
                    for g in range(NG):
                        for rows, at in ((slice(0, HALF), PAD), (slice(HALF, P), PAD - 1)):
                            m = dve.tensor_copy(src[rows, group(g)], shift_from[rows, at + g * GW:at + (g + 1) * GW])
                        m.then_inc(taken, 1)
                center(0)
                for g in range(NG):
                    if g + 1 < NG:
                        center(g + 1)
                    dve.wait_ge(rstd_ready, g + 1)
                    dve.wait_ge(centered, g + 1)
                    dve.tensor_tensor(dst[:, group(g)], xc[:, group(g)], rs[:, g % 2, :],
                                      ALU.mult).then_inc(normed, 1)
                    if gamma is not None:
                        dve.wait_ge(normed, g + 1)
                        dve.tensor_scalar(dst[:, group(g)], dst[:, group(g)], gamma, beta,
                                          ALU.mult, ALU.add).then_inc(scaled, 1)


def performer(nc, c, w, xn, ot):
    with ExitStack() as ctx:
        def sb(name, shape, dt=F32):
            return ctx.enter_context(on_chip(nc.sbuf_tensor, name, shape, dt))

        def ps(name, shape):
            return ctx.enter_context(on_chip(nc.psum_tensor, name, shape, F32))

        xt = sb("pf_x", [P, P])
        phi_q = sb("pf_phi_q", [P, P])
        phi_kt = sb("pf_phi_kt", [P, P])
        phi_k = sb("pf_phi_k", [P, P])
        kz = sb("pf_kz", [P, H, P])
        vext = sb("pf_vext", [P, H, 32])
        scores = sb("pf_scores", [P, H, P])
        state = sb("pf_state", [P, H * 32])
        add = sb("pf_add", [P, H * 32])
        proj = ps("pf_proj", [P, GW])
        s_ps = ps("pf_s", [P, 4, GW])
        o_ps = ps("pf_o", [P, GW])
        st_ps = ps("pf_st", [P, GW])
        with phase(nc, "init", "tile_in", "projected", "features", "kz_ready", "scored", "masked",
                   "attended", "stored", "summed", "added", "state_new") as (
                block, init, tile_in, projected, features, kz_ready, scored, masked, attended,
                stored, summed, added, state_new):
            @block.gpsimd
            def _(pool):
                pool.memset(vext[:], 0.0).then_inc(init, 1)
                pool.wait_ge(init, 1)
                pool.memset(vext[:, :, DH:DH + 1], 1.0).then_inc(init, 1)
                pool.memset(state[:], 0.0).then_inc(init, 1)
                def tile(t):
                    pool.wait_ge(projected, t)
                    pool.tensor_copy(xt[:], xn[:, bass.ds(t * P, P)]).then_inc(tile_in, 1)

                tile(0)
                with pool.Fori(1, NT) as t:
                    tile(t)

            @block.tensor
            def _(pe):
                def tile(t):
                    pe.wait_ge(tile_in, t + 1)
                    pe.wait_ge(features, t)
                    pe.matmul(proj[:, 0:P], w.pq[:], xt[:], start=True, stop=True)
                    pe.matmul(proj[:, P:2 * P], w.pkv[:, 0:P], xt[:], start=True, stop=True)
                    pe.matmul(proj[:, 2 * P:], xt[:], w.pkv[:], start=True, stop=True).then_inc(projected, 1)
                    pe.wait_ge(kz_ready, t + 1)
                    for h in range(H):
                        mm = pe.matmul(s_ps[:, h // 4, (h % 4) * P:(h % 4 + 1) * P], kz[:, h, :],
                                       phi_q[:], start=True, stop=True)
                    mm.then_inc(scored, 1)
                    pe.wait_ge(init, 3)
                    pe.wait_ge(state_new, t)
                    pe.wait_ge(masked, t + 1)
                    pe.wait_ge(stored, t)
                    for q in range(QUADS):
                        pe.matmul(o_ps[:, q * P:(q + 1) * P], state[:, q * P:(q + 1) * P], phi_q[:],
                                  start=True, stop=False, skip_group_check=True)
                        for j in range(4):
                            mm = pe.matmul(o_ps[32 * j:32 * j + 32, q * P:(q + 1) * P], vext[:, 4 * q + j, :],
                                           scores[:, 4 * q + j, :], start=False, stop=True,
                                           skip_group_check=True)
                    mm.then_inc(attended, 1)
                    pe.wait_ge(added, t)
                    pe.matmul(st_ps[:], phi_k[:], vext[:].rearrange("p h d -> p (h d)"),
                              start=True, stop=True).then_inc(summed, 1)

                tile(0)
                with pe.Fori(1, NT) as t:
                    tile(t)

            @block.scalar
            def _(act):
                def tile(t):
                    act.wait_ge(attended, t + 1)
                    act.activation(ot[:, :, bass.ds(t * P, P)], o_ps[:].rearrange("p (q n) -> p q n", q=QUADS),
                                   ACT.Copy).then_inc(stored, 1)

                tile(0)
                with act.Fori(1, NT) as t:
                    tile(t)

            @block.vector
            def _(dve):
                dve.wait_ge(init, 3)
                def tile(t):
                    dve.wait_ge(projected, t + 1)
                    dve.wait_ge(summed, t)
                    dve.tensor_scalar(phi_q[:], proj[:, 0:P], 0.0, 1e-3, ALU.max, ALU.add)
                    dve.tensor_scalar(phi_kt[:], proj[:, P:2 * P], 0.0, 1e-3, ALU.max, ALU.add)
                    dve.tensor_scalar(phi_k[:], proj[:, 2 * P:3 * P], 0.0, 1e-3, ALU.max, ALU.add)
                    dve.tensor_copy(vext[:, :, 0:DH],
                                    proj[:, 3 * P:].rearrange("p (h d) -> p h d", h=H)).then_inc(features, 1)
                    dve.wait_ge(features, t + 1)
                    dve.tensor_tensor(kz[:], phi_kt[:, None, :].to_broadcast([P, H, P]),
                                      c.head_mask[:, :, None].to_broadcast([P, H, P]),
                                      ALU.mult).then_inc(kz_ready, 1)
                    dve.wait_ge(scored, t + 1)
                    for b in range(4):
                        m = dve.tensor_tensor(scores[:, 4 * b:4 * b + 4, :],
                                              s_ps[:, b, :].rearrange("p (h n) -> p h n", h=4),
                                              c.causal[:, None, :].to_broadcast([P, 4, P]), ALU.mult)
                    m.then_inc(masked, 1)
                    dve.wait_ge(summed, t + 1)
                    dve.tensor_tensor(add[:], st_ps[:], c.block_mask[:], ALU.mult).then_inc(added, 1)
                    dve.wait_ge(added, t + 1)
                    dve.tensor_tensor(state[:], state[:], add[:], ALU.add).then_inc(state_new, 1)

                tile(0)
                with dve.Fori(1, NT) as t:
                    tile(t)


def normalise_heads(nc, c, ot, at):
    with ExitStack() as ctx:
        rec = ctx.enter_context(on_chip(nc.sbuf_tensor, "nh_rec", [P, 2, H], F32))
        tok = ctx.enter_context(on_chip(nc.sbuf_tensor, "nh_tok", [P, 2, P], F32))
        tps = ctx.enter_context(on_chip(nc.psum_tensor, "nh_tps", [P, 2, GW], F32))
        aps = ctx.enter_context(on_chip(nc.psum_tensor, "nh_aps", [P, 2, GW], F32))
        with phase(nc, "turned", "inverted", "divided", "back", "stored") as (
                block, turned, inverted, divided, back, stored):
            @block.tensor
            def _(pe):
                def turn(t):
                    if t >= 2:
                        pe.wait_ge(divided, t - 1)
                    for q in range(QUADS):
                        m = pe.transpose(tps[:, t % 2, q * P:(q + 1) * P], ot[:, q, t * P:(t + 1) * P], c.ident[:])
                    m.then_inc(turned, 1)

                turn(0)
                for t in range(NT):
                    if t + 1 < NT:
                        turn(t + 1)
                    pe.wait_ge(divided, t + 1)
                    if t >= 8 and t % 4 == 0:
                        pe.wait_ge(stored, t // 4 - 1)
                    pe.transpose(aps[:, t // 4 % 2, (t % 4) * P:(t % 4 + 1) * P], tok[:, t % 2, :],
                                 c.ident[:]).then_inc(back, 1)

            @block.vector
            def _(dve):
                for t in range(NT):
                    heads = tps[:, t % 2, :].rearrange("p (h n) -> p h n", h=H)
                    dve.wait_ge(turned, t + 1)
                    dve.reciprocal(rec[:, t % 2, :, None], heads[:, :, DH:DH + 1]).then_inc(inverted, 1)
                    dve.wait_ge(inverted, t + 1)
                    if t >= 2:
                        dve.wait_ge(back, t - 1)
                    dve.tensor_tensor(tok[:, t % 2, :].rearrange("p (h d) -> p h d", h=H), heads[:, :, 0:DH],
                                      rec[:, t % 2, :, None].to_broadcast([P, H, DH]),
                                      ALU.mult).then_inc(divided, 1)

            @block.scalar
            def _(act):
                for g in range(NG):
                    act.wait_ge(back, 4 * g + 4)
                    act.activation(at[:, group(g)], aps[:, g % 2, :], ACT.Copy).then_inc(stored, 1)


def project_add(nc, w, src, dst, more):
    with ExitStack() as ctx:
        tmp = ctx.enter_context(on_chip(nc.sbuf_tensor, "pa_tmp", [P, T], F32))
        y = ctx.enter_context(on_chip(nc.psum_tensor, "pa_y", [P, NG, GW], F32))
        with phase(nc, "projected", "summed") as (block, projected, summed):
            @block.tensor
            def _(pe):
                for g in range(NG):
                    pe.matmul(y[:, g, :], w[:], src[:, group(g)], start=True, stop=True).then_inc(projected, 1)

            @block.vector
            def _(dve):
                n = 0
                for g in range(NG):
                    dve.wait_ge(projected, g + 1)
                    last = y[:, g, :]
                    for k, m in enumerate(more):
                        to = dst if k == len(more) - 1 else tmp
                        if k:
                            dve.wait_ge(summed, n)
                        dve.tensor_tensor(to[:, group(g)], last, m[:, group(g)], ALU.add).then_inc(summed, 1)
                        n += 1
                        last = to[:, group(g)]


def gelu_mlp(nc, c, w, xn, x1, x):
    with ExitStack() as ctx:
        hid = ctx.enter_context(on_chip(nc.sbuf_tensor, "mlp_h", [P, 2, 4, GW], F32))
        tmp = ctx.enter_context(on_chip(nc.sbuf_tensor, "mlp_t", [P, GW], F32))
        hp = ctx.enter_context(on_chip(nc.psum_tensor, "mlp_hp", [P, 4, GW], F32))
        yp = ctx.enter_context(on_chip(nc.psum_tensor, "mlp_yp", [P, 2, GW], F32))
        with phase(nc, "up", "gelu_done", "down", "biased", "summed") as (
                block, up, gelu_done, down, biased, summed):
            @block.tensor
            def _(pe):
                def first(g):
                    for j in range(4):
                        if g >= 1:
                            pe.wait_ge(gelu_done, 4 * g - 3 + j)
                        pe.matmul(hp[:, j, :], w.w1[:, j * P:(j + 1) * P], xn[:, group(g)],
                                  start=True, stop=True).then_inc(up, 1)

                first(0)
                for g in range(NG):
                    if g + 1 < NG:
                        first(g + 1)
                    if g >= 2:
                        pe.wait_ge(biased, g - 1)
                    for j in range(4):
                        pe.wait_ge(gelu_done, 4 * g + j + 1)
                        m = pe.matmul(yp[:, g % 2, :], w.w2[:, j, :], hid[:, g % 2, j, :],
                                      start=(j == 0), stop=(j == 3))
                    m.then_inc(down, 1)

            @block.scalar
            def _(act):
                for g in range(NG):
                    for j in range(4):
                        act.wait_ge(up, 4 * g + j + 1)
                        if g >= 2:
                            act.wait_ge(down, g - 1)
                        act.activation(hid[:, g % 2, j, :], hp[:, j, :], ACT.Gelu_apprx_tanh,
                                       bias=c.v("a_b1", j)).then_inc(gelu_done, 1)

            @block.vector
            def _(dve):
                for g in range(NG):
                    dve.wait_ge(down, g + 1)
                    if g:
                        dve.wait_ge(summed, 2 * g)
                    dve.scalar_tensor_tensor(out=tmp[:], in0=yp[:, g % 2, :], scalar=c.v("a_b2"),
                                             in1=x1[:, group(g)], op0=ALU.add, op1=ALU.add).then_inc(biased, 1)
                    dve.wait_ge(biased, g + 1)
                    dve.tensor_tensor(x[:, group(g)], x[:, group(g)], tmp[:], ALU.add).then_inc(summed, 2)


def experts(nc, c, w, xn, x):
    with ExitStack() as ctx:
        def sb(name, shape, dt=F32):
            return ctx.enter_context(on_chip(nc.sbuf_tensor, name, shape, dt))

        comb_t = sb("moe_comb_t", [E, T])
        with ExitStack() as ctx2:
            def sb2(name, shape, dt=F32):
                return ctx2.enter_context(on_chip(nc.sbuf_tensor, name, shape, dt))

            pr = sb2("moe_probs", [P, NT, E])
            st = sb2("moe_stat", [P, NT])
            inv = sb2("moe_inv", [P, NT])
            top = sb2("moe_top", [P, NT, 8])
            idx = sb2("moe_idx", [P, NT, 8], U32)
            idf = sb2("moe_idf", [P, NT, 2])
            wt = sb2("moe_wt", [P, NT, 2])
            eq = sb2("moe_eq", [P, 2, NT, E])
            comb = sb2("moe_comb", [P, NT, E])
            lg = ctx2.enter_context(on_chip(nc.psum_tensor, "moe_logits", [P, NT, E], F32))
            ct = ctx2.enter_context(on_chip(nc.psum_tensor, "moe_ct", [P, NG, GW], F32))
            with phase(nc, "routed", "shifted", "exps", "step", "comb_ready", "turned", "stored") as (
                    block, routed, shifted, exps, step, comb_ready, turned, stored):
                @block.tensor
                def _(pe):
                    for t in range(NT):
                        m = pe.matmul(lg[:, t, :], xn[:, t * P:(t + 1) * P], w.router[:], start=True, stop=True)
                    m.then_inc(routed, 1)
                    pe.wait_ge(comb_ready, 1)
                    for t in range(NT):
                        m = pe.transpose(ct[0:E, t // 4, (t % 4) * P:(t % 4 + 1) * P], comb[:, t, :], c.ident[:])
                    m.then_inc(turned, 1)

                @block.scalar
                def _(act):
                    act.wait_ge(shifted, 1)
                    act.activation(pr[:], pr[:], ACT.Exp).then_inc(exps, 1)
                    act.wait_ge(turned, 1)
                    for g in range(NG):
                        act.activation(comb_t[:, group(g)], ct[0:E, g, :], ACT.Copy).then_inc(stored, 1)

                @block.vector
                def _(dve):
                    def spread(a):
                        return a.to_broadcast([P, NT, E])

                    n = 0

                    def then(ins):
                        nonlocal n
                        n += 1
                        ins.then_inc(step, 1)
                        dve.wait_ge(step, n)

                    dve.wait_ge(routed, 1)
                    then(dve.tensor_reduce(st[:], lg[:], AX.X, ALU.max))
                    dve.tensor_tensor(pr[:], lg[:], spread(st[:, :, None]), ALU.subtract).then_inc(shifted, 1)
                    dve.wait_ge(exps, 1)
                    then(dve.tensor_reduce(st[:], pr[:], AX.X, ALU.add))
                    then(dve.reciprocal(inv[:], st[:]))
                    then(dve.tensor_tensor(pr[:], pr[:], spread(inv[:, :, None]), ALU.mult))
                    for t in range(NT):
                        then(dve.max(top[:, t, :], pr[:, t, :]))
                        then(dve.max_index(idx[:, t, :], top[:, t, :], pr[:, t, :]))
                    then(dve.tensor_copy(idf[:], idx[:, :, 0:2]))
                    then(dve.tensor_tensor(st[:], top[:, :, 0], top[:, :, 1], ALU.add))
                    then(dve.tensor_scalar(st[:], st[:], 1e-9, None, ALU.add))
                    then(dve.reciprocal(inv[:], st[:]))
                    then(dve.tensor_tensor(wt[:], top[:, :, 0:2], inv[:, :, None].to_broadcast([P, NT, 2]), ALU.mult))
                    for k in range(2):
                        then(dve.tensor_tensor(eq[:, k], c.iota[:, None, :].to_broadcast([P, NT, E]),
                                               spread(idf[:, :, k:k + 1]), ALU.is_equal))
                        then(dve.tensor_tensor(eq[:, k], eq[:, k], spread(wt[:, :, k:k + 1]), ALU.mult))
                    dve.tensor_tensor(comb[:], eq[:, 0], eq[:, 1], ALU.add).then_inc(comb_ready, 1)
        sg = sb("moe_sg", [P, 2, GW])
        ug = sb("moe_ug", [P, 2, GW])
        hd = sb("moe_h", [P, 2, 5, GW])
        with ExitStack() as ctx3:
            gp = ctx3.enter_context(on_chip(nc.psum_tensor, "moe_g", [P, 2, GW], F32))
            up = ctx3.enter_context(on_chip(nc.psum_tensor, "moe_u", [P, 2, GW], F32))
            cp = ctx3.enter_context(on_chip(nc.psum_tensor, "moe_c", [P, 2, GW], F32))
            yp = ctx3.enter_context(on_chip(nc.psum_tensor, "moe_y", [P, 2, GW], F32))
            with phase(nc, "up_ready", "silu_done", "gated", "h_ready", "down", "summed") as (
                    block, up_ready, silu_done, gated, h_ready, down, summed):
                @block.tensor
                def _(pe):
                    def chunk(g, j):
                        n = 5 * g + j
                        if n >= 2:
                            pe.wait_ge(h_ready, n - 1)
                        wg = w.wg[:, j * P:(j + 1) * P] if j < 4 else w.wgs[:]
                        wu = w.wu[:, j * P:(j + 1) * P] if j < 4 else w.wus[:]
                        pe.matmul(gp[:, n % 2, :], wg, xn[:, group(g)], start=True, stop=True)
                        if j < 4:
                            pe.matmul(cp[:, n % 2, :], c.sel[:, j, :], comb_t[:, group(g)], start=True, stop=True)
                        pe.matmul(up[:, n % 2, :], wu, xn[:, group(g)], start=True, stop=True).then_inc(up_ready, 1)

                    def downs(g):
                        pe.wait_ge(h_ready, 5 * g + 5)
                        if g >= 2:
                            pe.wait_ge(summed, g - 1)
                        for j in range(5):
                            wd = w.wd[:, j, :] if j < 4 else w.wds[:]
                            m = pe.matmul(yp[:, g % 2, :], wd, hd[:, g % 2, j, :], start=(j == 0), stop=(j == 4))
                        m.then_inc(down, 1)

                    for g in range(NG):
                        for j in range(5):
                            chunk(g, j)
                            if j == 1 and g:
                                downs(g - 1)
                    downs(NG - 1)

                @block.scalar
                def _(act):
                    for n in range(5 * NG):
                        act.wait_ge(up_ready, n + 1)
                        if n >= 2:
                            act.wait_ge(h_ready, n - 1)
                        act.activation(sg[:, n % 2, :], gp[:, n % 2, :], ACT.Silu).then_inc(silu_done, 1)

                def add_y(dve, g):
                    dve.wait_ge(down, g + 1)
                    dve.tensor_tensor(x[:, group(g)], yp[:, g % 2, :], x[:, group(g)], ALU.add).then_inc(summed, 1)

                @block.vector
                def _(dve):
                    for g in range(NG):
                        for j in range(5):
                            n = 5 * g + j
                            dve.wait_ge(silu_done, n + 1)
                            if g >= 2:
                                dve.wait_ge(down, g - 1)
                            if j < 4:
                                dve.tensor_tensor(ug[:, n % 2, :], up[:, n % 2, :], sg[:, n % 2, :],
                                                  ALU.mult).then_inc(gated, 1)
                                dve.wait_ge(gated, 4 * g + j + 1)
                                dve.tensor_tensor(hd[:, g % 2, j, :], cp[:, n % 2, :], ug[:, n % 2, :],
                                                  ALU.mult).then_inc(h_ready, 1)
                            else:
                                dve.tensor_tensor(hd[:, g % 2, j, :], up[:, n % 2, :], sg[:, n % 2, :],
                                                  ALU.mult).then_inc(h_ready, 1)
                            if j == 2 and g:
                                add_y(dve, g - 1)
                    add_y(dve, NG - 1)


def split_parts(nc, x, dram):
    with ExitStack() as ctx:
        parts = [ctx.enter_context(on_chip(nc.sbuf_tensor, f"sp_p{i}", [P, T], BF16)) for i in range(3)]
        rest = ctx.enter_context(on_chip(nc.sbuf_tensor, "sp_rest", [P, T], F32))
        with phase(nc, "rounded", "left", "stored") as (block, rounded, left, stored):
            @block.scalar
            def _(act):
                act.activation(parts[0][:], x[:], ACT.Copy).then_inc(rounded, 1)
                act.wait_ge(left, 1)
                act.activation(parts[1][:], rest[:], ACT.Copy).then_inc(rounded, 1)

            @block.vector
            def _(dve):
                dve.wait_ge(rounded, 1)
                dve.tensor_tensor(rest[:], x[:], parts[0][:], ALU.subtract).then_inc(left, 1)
                dve.wait_ge(left, 1)
                dve.wait_ge(rounded, 2)
                dve.tensor_tensor(parts[2][:], rest[:], parts[1][:], ALU.subtract).then_inc(left, 1)

            @block.sync
            def _(sp):
                sp.wait_ge(rounded, 1)
                sp.dma_start(dram[0], parts[0][:]).then_inc(stored, 16)
                sp.wait_ge(rounded, 2)
                sp.dma_start(dram[1], parts[1][:]).then_inc(stored, 16)
                sp.wait_ge(left, 2)
                sp.dma_start(dram[2], parts[2][:]).then_inc(stored, 16)
                sp.wait_ge(stored, 48)


def values(nc, wv, xn, v):
    with ExitStack() as ctx:
        vp = ctx.enter_context(on_chip(nc.psum_tensor, "va_ps", [P, NG, 4, P], F32))
        with phase(nc, "init", "projected", "stored") as (block, init, projected, stored):
            @block.tensor
            def _(pe):
                for t in range(NT):
                    m = pe.matmul(vp[:, t // 4, t % 4, :], xn[:, t * P:(t + 1) * P], wv[:], start=True, stop=True)
                    if t % 4 == 3:
                        m.then_inc(projected, 1)

            @block.gpsimd
            def _(pool):
                pool.memset(v[:], 1.0).then_inc(init, 1)

            @block.vector
            def _(dve):
                dve.wait_ge(init, 1)
                for g in range(NG):
                    dve.wait_ge(projected, g + 1)
                    dve.tensor_copy(v[:, 4 * g:4 * g + 4, 0:H * VW].rearrange("p t (h d) -> p t h d", h=H)[:, :, :, 0:DH],
                                    vp[:, g].rearrange("p t (h d) -> p t h d", h=H)).then_inc(stored, 1)


def near_tables(nc, c, io):
    n = 3 * P
    with ExitStack() as ctx:
        rel = ctx.enter_context(on_chip(nc.sbuf_tensor, "nt_rel", [H, 2, P + 1], F32))
        ext = ctx.enter_context(on_chip(nc.sbuf_tensor, "nt_ext", [H, 2, n], F32))
        rest = ctx.enter_context(on_chip(nc.sbuf_tensor, "nt_rest", [H, 2, n], F32))
        parts = ctx.enter_context(on_chip(nc.sbuf_tensor, "nt_parts", [H, 3, 2, n], BF16))
        with phase(nc, "loaded", "step", "stored") as (block, loaded, step, stored):
            @block.sync
            def _(sp):
                sp.dma_start(rel[:], io["rel"]).then_inc(loaded, 16)
                sp.wait_ge(step, 9)
                sp.dma_start(io["s_ext"].rearrange("a h k n -> h a k n"), parts[:]).then_inc(stored, 16)
                sp.wait_ge(stored, 16)

            @block.vector
            def _(dve):
                k = 0

                def then(ins):
                    nonlocal k
                    k += 1
                    ins.then_inc(step, 1)
                    dve.wait_ge(step, k)

                then(dve.memset(ext[:], 0.0))
                then(dve.memset(ext[:, 0, 0:P - 1], NEG))
                then(dve.memset(ext[:, 1, 2 * P:n], NEG))
                dve.wait_ge(loaded, 16)
                then(dve.tensor_scalar(ext[:, 0, P - 1:2 * P], rel[:, 0, :], rel[:, 0, P:P + 1], None, ALU.subtract))
                then(dve.tensor_scalar(ext[:, 1, P - 1:2 * P], rel[:, 1, :], rel[:, 0, P:P + 1], None, ALU.subtract))
                then(dve.tensor_copy(parts[:, 0], ext[:]))
                then(dve.tensor_tensor(rest[:], ext[:], parts[:, 0], ALU.subtract))
                then(dve.tensor_copy(parts[:, 1], rest[:]))
                then(dve.tensor_tensor(parts[:, 2], rest[:], parts[:, 1], ALU.subtract))


M_ROW = 96
STEPS_B = [(g, j) for g in range(NG) for j in range(4 * g + 4)]


def scan_events():
    events = []
    for q in range(QUADS):
        for g in range(NG):
            blocks = [("block", q, g, h, i, s) for i in range(4 * g, 4 * g + 4) for h in range(4)
                      for s in range(1 + (i >= 8))]
            if events:
                blocks.insert(2, ("turn",) + turn)
            events += blocks
            turn = (q, g)
    return events + [("turn",) + turn]


EVENTS = scan_events()


def scan_schedule(lead=4, most=2800):
    steps = QUADS * len(STEPS_B)
    price = []
    for kind, q, g, *block in EVENTS:
        price.append(150 + (min(P * (block[1] + 1), (block[2] + 1) * 2 * GW) - block[2] * 2 * GW if block else 3 * GW))
    done = []
    for n in range(steps):
        q, m = divmod(min(n + lead, steps - 1), len(STEPS_B))
        done.append(EVENTS.index(("turn", q, STEPS_B[m][0])) + 1)
    for n in range(steps - 2, -1, -1):
        while sum(price[done[n]:done[n + 1]]) > most:
            done[n] += 1
    return done


EVENTS_BY = scan_schedule()
EVENTS_FIRST = EVENTS_BY[0]


def causal_attention(nc, c, io, v, ot, near):
    n_near = 3 if near else 1
    with ExitStack() as ctx:
        def sb(name, shape, dt=F32):
            return ctx.enter_context(on_chip(nc.sbuf_tensor, name, shape, dt))

        qs = sb("ca_q", [P, 2, 4, T], BF16)
        ks = sb("ca_k", [P, 2, 4, T], BF16)
        pt = sb("ca_p", [P, 3, 4, GW])
        mx = sb("ca_mx", [P, 4, NT, 2])
        negm = sb("ca_negm", [P, 4, 4])
        rest = sb("ca_rest", [P, 4, 4])
        mp = sb("ca_mp", [P, 3, 4, 4], BF16)
        mt = sb("ca_mt", [4, 2, 3, GW], BF16)
        if near:
            near_a = sb("ca_near_a", [P, 2, 4, 3, 2 * P], BF16)
            near_b = sb("ca_near_b", [P, 2, 4, 3, 2 * P], BF16)
        a_ps = ctx.enter_context(on_chip(nc.psum_tensor, "ca_a", [P, 2, 2 * GW], F32))
        s_ps = ctx.enter_context(on_chip(nc.psum_tensor, "ca_s", [P, 3, GW], F32))
        o_ps = ctx.enter_context(on_chip(nc.psum_tensor, "ca_o", [P, GW], F32))
        loads = 18 + 1 + (24 if near else 0)
        with phase(nc, "q_cleared", "k_cleared", "loaded_even", "loaded_odd", "event_ready", "event_done", "combined",
                   "m_placed_even", "m_placed_odd", "b_scored", "b_exp", "b_out",
                   "o_stored", "mstep", "mx_cleared") as (
                block, q_cleared, k_cleared, loaded_even, loaded_odd, event_ready, event_done, combined, m_placed_even, m_placed_odd, b_scored, b_exp, b_out, o_stored, mstep, mx_cleared):
            loaded = (loaded_even, loaded_odd)
            m_placed = (m_placed_even, m_placed_odd)
            nb = 4 * len(STEPS_B)

            def clear(eng, b, a):
                return eng.memset(b[:, a].rearrange("p h t -> p (h t)").bitcast(F32), 0.0)

            def load_parts(eng, q, dst, src, of):
                for a in range(3):
                    for b in range(3):
                        r = (3 * a + b) * DH
                        heads = src[of(a, b), q * 32:q * 32 + 32, :].rearrange("(h d) t -> d h t", h=4)
                        eng.dma_start(dst[r:r + DH, q % 2], heads).then_inc(loaded[q % 2], 16)

            def load_k(eng, q):
                load_parts(eng, q, ks, io["s_k"], lambda a, b: b)

            @block.gpsimd
            def _(pool):
                for a in range(2):
                    clear(pool, ks, a).then_inc(k_cleared, 1)
                    pool.wait_ge(k_cleared, 2 * a + 1)
                    pool.memset(ks[M_ROW:M_ROW + 3, a], 1.0).then_inc(k_cleared, 1)
                    pool.wait_ge(k_cleared, 2 * a + 2)

            @block.sync
            def _(sp):
                def load(q):
                    load_parts(sp, q, qs, io["s_q"], lambda a, b: a)
                    if q:
                        load_k(sp, q)
                    sp.dma_start(qs[M_ROW:M_ROW + 3, q % 2].rearrange("p h t -> p (h t)"),
                                 io["c_zero"]).then_inc(loaded[q % 2], 16)
                    if near:
                        e = io["s_ext"]
                        for h in range(4):
                            for part in range(3):
                                for k, dst in ((1, near_a), (0, near_b)):
                                    row = e[part, 4 * q + h, k, 0:2 * P]
                                    skew = bass.AP(row.tensor, row.offset, [[1, P], [1, 2 * P]])
                                    sp.dma_start(dst[:, q % 2, h, part, :], skew).then_inc(loaded[q % 2], 16)

                def place(q, g):
                    n = q * NG + g
                    sp.wait_ge(event_done, EVENTS.index(("turn", q, g)) + 1)
                    sp.wait_ge(loaded[q % 2], 16 * loads * (q // 2 + 1))
                    for part in range(3):
                        sp.dma_start(qs[M_ROW + part:M_ROW + part + 1, q % 2, :, group(g)],
                                     mt[:, n % 2, part, :]).then_inc(m_placed[n % 2], 16)

                sp.wait_ge(q_cleared, 1)
                load(0)
                for q in range(QUADS):
                    for g in range(NG):
                        if g == 2 and q + 1 < QUADS:
                            if q:
                                sp.wait_ge(b_out, q * len(STEPS_B))
                            sp.wait_ge(q_cleared, 2)
                            sp.wait_ge(k_cleared, 4)
                            load(q + 1)
                        place(q, g)

            @block.tensor
            def _(pe):
                def wait_loaded(q):
                    pe.wait_ge(loaded[q % 2], 16 * loads * (q // 2 + 1))

                def near_add(out, side, q, h, cols):
                    for k in range(n_near):
                        if near:
                            rhs = (near_a if side == "a" else near_b)[:, q % 2, h, k, cols]
                        else:
                            rhs = c.mask_a[:] if side == "a" else c.mask_b[:]
                        m = pe.matmul(out, (c.flip_b if near else c.ident_b)[:], rhs, start=False,
                                      stop=True, skip_group_check=True)
                    return m

                def event(u):
                    if u >= 2:
                        pe.wait_ge(event_done, u - 1)
                    kind, q, g, *block_of = EVENTS[u]
                    if kind == "turn":
                        pe.wait_ge(combined, q * NG + g + 1)
                        for part in range(3):
                            for i in range(4):
                                at = part * GW + i * P
                                m = pe.transpose(a_ps[0:4, u % 2, :].bitcast(BF16)[:, at:at + P],
                                                 mp[:, part, :, i], c.ident_b[:])
                        m.then_inc(event_ready, 1)
                        return
                    h, i, s = block_of
                    if g == 0 and h == 0 and i == 0:
                        wait_loaded(q)
                    end = min(P * (i + 1), (s + 1) * 2 * GW)
                    for lo in range(s * 2 * GW, end, GW):
                        hi = min(lo + GW, end)
                        at = a_ps[:, u % 2, lo - s * 2 * GW:hi - s * 2 * GW]
                        m = pe.matmul(at, qs[:, q % 2, h, i * P:(i + 1) * P], ks[:, q % 2, h, lo:hi],
                                      start=True, stop=True, skip_group_check=True)
                        first = max(lo, P * (i - 1 if near else i), 0)
                        if first < hi:
                            c0 = first - P * (i - 1)
                            cols = slice(c0, c0 + hi - first)
                            out = a_ps[:, u % 2, first - s * 2 * GW:hi - s * 2 * GW]
                            m = near_add(out, "a", q, h, cols)
                    m.then_inc(event_ready, 1)

                def outputs(q, n):
                    g, j = STEPS_B[n]
                    s = q * len(STEPS_B) + n
                    off = max(0, j - 4 * g) * P
                    pe.wait_ge(b_exp, 4 * s + 4)
                    if j == 0 and q + g:
                        pe.wait_ge(o_stored, q * NG + g)
                    for h in range(4):
                        m = pe.matmul(o_ps[32 * h:32 * h + 32, off:GW],
                                      v[:, j, (4 * q + h) * VW:(4 * q + h) * VW + 32],
                                      pt[:, s % 3, h, off:GW], start=(j == 0), stop=(j == 4 * g + 3),
                                      skip_group_check=True)
                    m.then_inc(b_out, 1)

                def step_b(q, n, a_from, a_to):
                    g, j = STEPS_B[n]
                    off = max(0, j - 4 * g) * P
                    for h in range(4):
                        k = q * nb + 4 * n + h
                        if k >= 3:
                            pe.wait_ge(b_exp, k - 2)
                        m = pe.matmul(s_ps[:, k % 3, off:GW], ks[:, q % 2, h, j * P:(j + 1) * P],
                                      qs[:, q % 2, h, g * GW + off:(g + 1) * GW],
                                      start=True, stop=True, skip_group_check=True)
                        lo, hi = max(j, 4 * g), min(j + (2 if near else 1), 4 * g + 4)
                        if lo < hi:
                            m = near_add(s_ps[:, k % 3, lo * P - g * GW:hi * P - g * GW], "b", q, h,
                                         slice((lo - j) * P, (hi - j) * P))
                        m.then_inc(b_scored, 1)
                        for x in range(a_from + (a_to - a_from) * h // 4, a_from + (a_to - a_from) * (h + 1) // 4):
                            event(x)
                        if h == 1 and n:
                            outputs(q, n - 1)

                pe.wait_ge(k_cleared, 2)
                for u in range(EVENTS_FIRST):
                    event(u)
                done = EVENTS_FIRST
                for q in range(QUADS):
                    for n, (g, j) in enumerate(STEPS_B):
                        to = EVENTS_BY[q * len(STEPS_B) + n]
                        if j == 0:
                            pe.wait_ge(m_placed[g % 2], 48 * ((q * NG + g) // 2 + 1))
                        step_b(q, n, done, to)
                        done = to
                    outputs(q, len(STEPS_B) - 1)

            @block.scalar
            def _(act):
                act.wait_ge(k_cleared, 1)
                load_k(act, 0)
                for q in range(QUADS):
                    for n, (g, j) in enumerate(STEPS_B):
                        s = q * len(STEPS_B) + n
                        off = max(0, j - 4 * g) * P
                        if s >= 3:
                            act.wait_ge(b_out, s - 2)
                        for h in range(4):
                            k = 4 * s + h
                            act.wait_ge(b_scored, k + 1)
                            act.activation(pt[:, s % 3, h, off:GW], s_ps[:, k % 3, off:GW],
                                           ACT.Exp).then_inc(b_exp, 1)

            @block.vector
            def _(dve):
                for a in range(2):
                    clear(dve, qs, a).then_inc(q_cleared, 1)
                dve.memset(mx[:], -3e38).then_inc(mx_cleared, 1)

                def event(u):
                    kind, q, g, *block_of = EVENTS[u]
                    dve.wait_ge(event_ready, u + 1)
                    if kind == "turn":
                        n = q * NG + g
                        if n >= 2:
                            dve.wait_ge(m_placed[n % 2], 48 * (n // 2))
                        dve.tensor_copy(mt[:, n % 2], a_ps[0:4, u % 2, :].bitcast(BF16)[:, 0:3 * GW]
                                        .rearrange("r (a n) -> r a n", a=3)).then_inc(event_done, 1)
                        return
                    h, i, s = block_of
                    width = min(P * (i + 1), (s + 1) * 2 * GW) - s * 2 * GW
                    if u == 0:
                        dve.wait_ge(mx_cleared, 1)
                    dve.tensor_reduce(mx[:, h, i, s:s + 1], a_ps[:, u % 2, 0:width], AX.X,
                                      ALU.max).then_inc(event_done, 1)
                    if i % 4 == 3 and h == 3 and s == int(i >= 8):
                        combine(u, q, g)

                def combine(u, q, g):
                    n = q * NG + g
                    dve.wait_ge(event_done, u + 1)
                    dve.tensor_reduce(negm[:], mx[:, :, 4 * g:4 * g + 4, :], AX.X, ALU.max,
                                      negate=True).then_inc(mstep, 1)
                    dve.wait_ge(mstep, 4 * n + 1)
                    dve.tensor_copy(mp[:, 0], negm[:]).then_inc(mstep, 1)
                    dve.wait_ge(mstep, 4 * n + 2)
                    dve.tensor_tensor(rest[:], negm[:], mp[:, 0], ALU.subtract).then_inc(mstep, 1)
                    dve.wait_ge(mstep, 4 * n + 3)
                    dve.tensor_copy(mp[:, 1], rest[:]).then_inc(mstep, 1)
                    dve.wait_ge(mstep, 4 * n + 4)
                    dve.tensor_tensor(mp[:, 2], rest[:], mp[:, 1], ALU.subtract).then_inc(combined, 1)

                def store_o(q, g):
                    dve.wait_ge(b_out, q * len(STEPS_B) + sum(4 * x + 4 for x in range(g + 1)))
                    dve.tensor_copy(ot[:, q, group(g)], o_ps[:]).then_inc(o_stored, 1)

                for u in range(EVENTS_FIRST):
                    event(u)
                done = EVENTS_FIRST
                for q in range(QUADS):
                    for n, (g, j) in enumerate(STEPS_B):
                        to = EVENTS_BY[q * len(STEPS_B) + n]
                        for x in range(done, to):
                            event(x)
                        done = to
                        if g and j == 0:
                            store_o(q, g - 1)
                    store_o(q, NG - 1)


CH = 4
KZ = WIN + P


def turns_before(k):
    return 0 if isinstance(k, int) and k < 2 else (k - 2) * 10 + 4


def scale_tables(pool, lw, scaled_tables):
    for tab, scale in ((lw.cos_q, 0), (lw.sin_q, 1), (lw.cos_k, 2), (lw.sin_k, 3)):
        t = tab[:, 0:NT * LD].rearrange("p (t d) -> p t d", t=NT)
        pool.tensor_tensor(t, t, lw.qk_scale[:, scale, None, :].to_broadcast([P, NT, LD]),
                           ALU.mult).then_inc(scaled_tables, 1)


def local_attention(nc, c, lw, xa, xb, kz, vx, prefetch):
    with ExitStack() as ctx:
        def sb(name, shape, dt=F32):
            return ctx.enter_context(on_chip(nc.sbuf_tensor, name, shape, dt))

        xs = sb("la_xs", [P, 2, KZ])
        raw = sb("la_raw", [P, CH, GW])
        sq = sb("la_sq", [P, 2, GW])
        tm = sb("la_tm", [P, 2, GW])
        rp = sb("la_rp", [P, 2, CH, GW])
        ss = sb("la_ss", [P, 2 * LH])
        lg = sb("la_lg", [P, 2 * LH])
        rn = sb("la_rn", [P, 2 * LH])
        qt = sb("la_qt", [P, LH // 2, P])
        mx = sb("la_mx", [P, LH])
        pw = sb("la_p", [P, LH, KEYS])
        pts = sb("la_pts", [KEYS, LH, P])
        rec = sb("la_rec", [P, LH])
        otok = sb("la_otok", [P, INNER])
        ots = sb("la_ots", [P, LH // 2, P])
        proj = ctx.enter_context(on_chip(nc.psum_tensor, "la_proj", [P, 2, GW], F32))
        ring = ctx.enter_context(on_chip(nc.psum_tensor, "la_ring", [P, 2, GW], F32))
        so = ctx.enter_context(on_chip(nc.psum_tensor, "la_so", [P, 4, GW], F32))
        so_heads = so[:, :, 0:4 * KEYS].rearrange("p b (j n) -> p b j n", j=4)

        y_ps = so[:, 1, 4 * KEYS:GW]

        def heads(a):
            return a.rearrange("p (b j) n -> p b j n", b=2)

        with phase(nc, "xs_ready", "projected", "raw_ready", "sq_ready",
                   "scaled_cos", "scaled_sin", "rotated", "squares_summed", "clamped", "logged",
                   "norms_ready", "normed", "turned", "q0_stored", "q1_stored", "k_even_stored",
                   "k_odd_stored", "w_stored", "o_stored",
                   "k_before", "scored", "max_ready", "shifted", "weights_ready", "values_ready",
                   "weighted", "inverted", "out_ready", "y_ready", "y_added",
                   "fetched") as (
                block, xs_ready, projected, raw_ready, sq_ready, scaled_cos,
                scaled_sin, rotated, squares_summed, clamped, logged, norms_ready, normed, turned,
                q0_stored, q1_stored, k_even_stored, k_odd_stored, w_stored, o_stored, k_before, scored, max_ready, shifted,
                weights_ready, values_ready, weighted, inverted, out_ready, y_ready, y_added,
                fetched):
            @block.sync
            def _(sp):
                n = prefetch(sp, fetched)
                sp.wait_ge(fetched, 16 * n)

            def pipeline(eng, step):
                step(0, 0, True, False, False)
                step(1, 1, True, True, False)
                step(2, 0, True, True, True)
                step(3, 1, True, True, True)
                with eng.Fori(4, NT - 1, 2) as k:
                    step(k, 0, True, True, True)
                    step(k + 1, 1, True, True, True)
                step(NT, 0, False, True, True)
                step(NT + 1, 1, False, False, True)

            def since(k, n):
                return not isinstance(k, int) or k >= n

            @block.tensor
            def _(pe):
                def step(k, par, a, b, c_):
                    kb, pb, kc, pc = k - 1, 1 - par, k - 2, par

                    tail = isinstance(k, int) and k == NT

                    def project(i):
                        if not (a or tail and i >= CH):
                            return
                        if i >= 2 and not tail:
                            pe.wait_ge(sq_ready, k * 4 + (i - 1))
                        elif since(k, 1):
                            pe.wait_ge(values_ready, k * 2 + (i % 2 - 1))
                        if i == 0 or tail:
                            pe.wait_ge(xs_ready, k + 1)
                        if i < CH:
                            pe.matmul(proj[:, i % 2, :], xs[:, par, WIN:KZ], lw.qkv[:, i * GW:(i + 1) * GW],
                                      start=True, stop=True).then_inc(projected, 1)
                        else:
                            col = 2 * INNER + (i - CH) * GW
                            pe.matmul(proj[:, i % 2, :], xs[:, par, 0:P], lw.qkv[:, col:col + GW],
                                      start=True, stop=True).then_inc(projected, 1)

                    def turn_weights(i):
                        if not c_:
                            return
                        pe.wait_ge(weights_ready, kc * 2 + (i // 2 + 1))
                        if i >= 2:
                            pe.wait_ge(w_stored, kc * 4 + (i - 1))
                        elif b:
                            pe.wait_ge((q0_stored, q1_stored)[i], kb + 1)
                        for j in range(4):
                            m = pe.transpose(ring[0:KEYS, i % 2, j * P:(j + 1) * P], pw[:, 4 * i + j, :], c.ident[:])
                        m.then_inc(turned, 1)

                    def weigh(half_heads):
                        if not c_:
                            return
                        pe.wait_ge(values_ready, kc * 2 + 4)
                        if half_heads == 0 and since(k, 3):
                            pe.wait_ge(y_added, kc)
                        for i in (2 * half_heads, 2 * half_heads + 1):
                            pe.wait_ge(w_stored, kc * 4 + (i + 1))
                            for j in range(4):
                                h = 4 * i + j
                                for half in range(2):
                                    m = pe.matmul(so[HALF * half:HALF * half + HALF, i, j * KEYS:(j + 1) * KEYS],
                                                  pts[:, h, HALF * half:HALF * half + HALF],
                                                  vx[:, pc, half, h, :], start=True, stop=True,
                                                  skip_group_check=True)
                        m.then_inc(weighted, 1)

                    def score(half_heads):
                        if not b:
                            return
                        if c_:
                            pe.wait_ge(out_ready, kc * 2 + (half_heads + 1))
                        mask = c.local_first if isinstance(k, int) and k == 1 else c.local_mask
                        for i in (2 * half_heads, 2 * half_heads + 1):
                            pe.matmul(so[:, i, 0:4 * KEYS], c.ident_b[:], mask[:], start=True, stop=False,
                                      skip_group_check=True)
                            for j in range(4):
                                h = 4 * i + j
                                for half in range(2):
                                    m = pe.matmul(so[HALF * half:HALF * half + HALF, i, j * KEYS:(j + 1) * KEYS],
                                                  qt[:, h // 2, HALF * half:HALF * half + HALF],
                                                  kz[:, pb, h, HALF * half:HALF * half + KEYS],
                                                  start=False, stop=True, skip_group_check=True)
                        m.then_inc(scored, 1)

                    if b:
                        for i in range(CH):
                            x = (i + 2) % 4
                            pe.wait_ge(normed, kb * 4 + (i + 1))
                            if i >= 2:
                                pe.wait_ge(k_even_stored, kb * 2 + (i - 1))
                                pe.wait_ge(k_odd_stored, kb * 2 + (i - 1))
                            for j in range(4):
                                m = pe.transpose(ring[:, i % 2, j * P:(j + 1) * P], rp[:, pb, x, j * P:(j + 1) * P],
                                                 c.ident[:])
                            m.then_inc(turned, 1)
                            if i == 1:
                                project(0)
                    else:
                        project(0)
                    project(1)
                    turn_weights(0)
                    turn_weights(1)
                    project(2)
                    turn_weights(2)
                    turn_weights(3)
                    weigh(0)
                    weigh(1)
                    project(3)
                    if b:
                        pe.wait_ge(q0_stored, kb + 1)
                        pe.wait_ge(q1_stored, kb + 1)
                        pe.wait_ge(k_before, kb + 1)
                    score(0)
                    if c_:
                        pe.wait_ge(out_ready, kc * 2 + 2)
                        for i in range(2):
                            for j in range(4):
                                p = 4 * i + j
                                m = pe.transpose(ring[:, i % 2, j * P:(j + 1) * P], otok[:, p * P:(p + 1) * P],
                                                 c.ident[:])
                            m.then_inc(turned, 1)
                    score(1)
                    project(4)
                    project(5)
                    if c_:
                        if b:
                            pe.wait_ge(shifted, kb * 2 + 1)
                        pe.wait_ge(o_stored, kc * 2 + 2)
                        for p in range(LH // 2):
                            m = pe.matmul(y_ps, lw.wo[:, p, :], ots[:, p, :], start=(p == 0),
                                          stop=(p == LH // 2 - 1))
                        m.then_inc(y_ready, 1)

                pipeline(pe, step)

            @block.scalar
            def _(act):
                def step(k, par, a, b, c_):
                    kb, pb, kc, pc = k - 1, 1 - par, k - 2, par
                    t0 = turns_before(k)
                    tw = 4 if b else 0

                    def keep_chunk(i):
                        if not a:
                            return
                        act.wait_ge(projected, k * 6 + (i + 1))
                        if since(k, 1):
                            act.wait_ge(scaled_cos, (k - 1) * 4 + (i + 1))
                            act.wait_ge(scaled_sin, (k - 1) * 4 + (i + 1))
                        act.activation(raw[:, i, :], proj[:, i % 2, :], ACT.Copy).then_inc(raw_ready, 1)
                        if not (isinstance(k, int) and 4 * k + i < 2):
                            act.wait_ge(squares_summed, k * 4 + (i - 1))
                        act.activation(sq[:, i % 2, :], proj[:, i % 2, :], ACT.Square).then_inc(sq_ready, 1)

                    def store_weights(i):
                        if not c_:
                            return
                        act.wait_ge(turned, t0 + (tw + i + 1))
                        if i % 2 == 0 and since(k, 3):
                            act.wait_ge(weighted, kc * 2 + (i // 2 - 1))
                        act.activation(pts[:, 4 * i:4 * i + 4, :],
                                       ring[0:KEYS, i % 2, :].rearrange("p (j n) -> p j n", j=4),
                                       ACT.Copy).then_inc(w_stored, 1)

                    tail = isinstance(k, int) and k == NT

                    def store_values(i):
                        if not (a or tail):
                            return
                        if since(k, 2) and i == 0:
                            act.wait_ge(weighted, kc * 2 + 2)
                        act.wait_ge(projected, k * 6 + (i + (1 if tail else 5)))
                        eight = slice(8 * i, 8 * i + 8)
                        copies = [(vx[0:KEYS, par, 0], slice(0, KEYS)), (vx[0:HALF, par, 1], slice(HALF, P)),
                                  (vx[HALF:KEYS, 1 - par, 1], slice(0, WIN))]
                        first, last = (2 if tail else 0), (3 if since(k, 1) else 2)
                        for to, rows in copies[first:last]:
                            m = act.activation(to[:, eight, 0:LD], proj[rows, i, :].rearrange("p (h d) -> p h d", h=8),
                                               ACT.Copy)
                        m.then_inc(values_ready, 1)

                    def exponentials(half_heads):
                        if not b:
                            return
                        act.wait_ge(shifted, kb * 2 + (half_heads + 1))
                        part = pw[:, 8 * half_heads:8 * half_heads + 8, :]
                        act.activation(part, part, ACT.Exp).then_inc(weights_ready, 1)

                    if b:
                        if since(k, 2):
                            act.wait_ge(scored, kb * 2)
                            act.wait_ge(k_before, kb)
                        for i in range(2):
                            act.wait_ge(turned, t0 + (i + 1))
                            rows = slice(0, HALF)
                            act.activation(kz[rows, pb, 8 * i:8 * i + 8:2, WIN:KZ],
                                           ring[rows, i, :].rearrange("p (j n) -> p j n", j=4),
                                           ACT.Copy).then_inc(k_even_stored, 1)
                    keep_chunk(0)
                    if b:
                        act.wait_ge(turned, t0 + 3)
                        act.activation(qt[:, 0:4, :], ring[:, 0, :].rearrange("p (j n) -> p j n", j=4),
                                       ACT.Copy).then_inc(q0_stored, 1)
                    keep_chunk(1)
                    store_weights(0)
                    store_weights(1)
                    keep_chunk(2)
                    store_weights(2)
                    store_weights(3)
                    keep_chunk(3)
                    if c_:
                        for i in range(2):
                            act.wait_ge(turned, t0 + (tw + 5 + i))
                            if since(k, 3) and i == 0:
                                act.wait_ge(y_ready, kc)
                            act.activation(ots[:, 4 * i:4 * i + 4, :],
                                           ring[:, i, :].rearrange("p (j n) -> p j n", j=4),
                                           ACT.Copy).then_inc(o_stored, 1)
                    if a:
                        act.wait_ge(clamped, k + 1)
                        act.activation(lg[:], ss[:], ACT.Ln, scale=float(2 ** 20)).then_inc(logged, 1)
                        act.wait_ge(logged, k + 1)
                        if since(k, 1):
                            act.wait_ge(normed, k * 4)
                        act.activation(rn[:], lg[:], ACT.Exp, scale=-0.5, bias=c.v("ten_ln2")).then_inc(norms_ready, 1)
                    exponentials(0)
                    store_values(0)
                    store_values(1)
                    exponentials(1)

                act.preload_act_table_set("natural_log_exp_and_others")
                pipeline(act, step)

            @block.vector
            def _(dve):
                def add_y(kc):
                    dve.wait_ge(y_ready, kc + 1)
                    at = bass.ds(kc * P + PAD, P)
                    dve.tensor_tensor(xb[:, at], y_ps, xa[:, at], ALU.add).then_inc(y_added, 1)

                def step(k, par, a, b, c_):
                    kb, pb, kc, pc = k - 1, 1 - par, k - 2, par
                    t0 = turns_before(k)

                    def rotate(i):
                        if not a:
                            return
                        tab = lw.cos_q if i < 2 else lw.cos_k
                        dve.wait_ge(raw_ready, k * 4 + (i + 1))
                        if since(k, 2) and i == 0:
                            dve.wait_ge(turned, t0)
                        dve.tensor_tensor(rp[:, par, i, :].rearrange("p (h d) -> p h d", h=8),
                                          raw[:, i, :].rearrange("p (h d) -> p h d", h=8),
                                          tab[:, bass.ds(k * LD, LD)][:, None, :].to_broadcast([P, 8, LD]),
                                          ALU.mult).then_inc(scaled_cos, 1)
                        dve.wait_ge(sq_ready, k * 4 + (i + 1))
                        if since(k, 1) and i == 0:
                            dve.wait_ge(logged, k)
                        dve.tensor_reduce(ss[:, 8 * i:8 * i + 8],
                                          sq[:, i % 2, :].rearrange("p (h d) -> p h d", h=8),
                                          AX.X, ALU.add).then_inc(squares_summed, 1)

                    def divide(half_heads):
                        if not c_:
                            return
                        n = kc * 2 + (half_heads + 1)
                        banks = slice(2 * half_heads, 2 * half_heads + 2)
                        eight = slice(8 * half_heads, 8 * half_heads + 8)
                        dve.wait_ge(weighted, n)
                        dve.reciprocal(rec[:, eight].rearrange("p (b j o) -> p b j o", b=2, j=4),
                                       so_heads[:, banks, :, LD:LD + 1]).then_inc(inverted, 1)
                        dve.wait_ge(inverted, n)
                        if since(k, 3) and half_heads == 0:
                            dve.wait_ge(turned, t0)
                        dve.tensor_tensor(heads(otok[:].rearrange("p (h d) -> p h d", h=LH)[:, eight]),
                                          so_heads[:, banks, :, 0:LD],
                                          heads(rec[:, eight, None].to_broadcast([P, 8, LD])),
                                          ALU.mult).then_inc(out_ready, 1)

                    def shift(half_heads):
                        if not b:
                            return
                        n = kb * 2 + (half_heads + 1)
                        banks = slice(2 * half_heads, 2 * half_heads + 2)
                        eight = slice(8 * half_heads, 8 * half_heads + 8)
                        dve.wait_ge(scored, n)
                        dve.tensor_reduce(mx[:, eight].rearrange("p (b j) -> p b j", b=2), so_heads[:, banks], AX.X,
                                          ALU.max).then_inc(max_ready, 1)
                        dve.wait_ge(max_ready, n)
                        dve.tensor_tensor(heads(pw[:, eight]), so_heads[:, banks],
                                          heads(mx[:, eight, None].to_broadcast([P, 8, KEYS])),
                                          ALU.subtract).then_inc(shifted, 1)

                    if since(k, 3):
                        add_y(k - 3)
                    if b:
                        if since(k, 2):
                            dve.wait_ge(scored, kb * 2)
                            dve.wait_ge(k_before, kb)
                        for i in range(2):
                            dve.wait_ge(turned, t0 + (i + 1))
                            rows = slice(HALF, P)
                            dve.tensor_copy(kz[rows, pb, 8 * i + 1:8 * i + 8:2, WIN:KZ],
                                            ring[rows, i, :].rearrange("p (j n) -> p j n", j=4)
                                            ).then_inc(k_odd_stored, 1)
                        dve.wait_ge(turned, t0 + 4)
                        dve.tensor_copy(qt[:, 4:8, :], ring[:, 1, :].rearrange("p (j n) -> p j n", j=4)
                                        ).then_inc(q1_stored, 1)
                    rotate(0)
                    rotate(1)
                    rotate(2)
                    divide(0)
                    divide(1)
                    rotate(3)
                    if a:
                        dve.wait_ge(squares_summed, k * 4 + 4)
                        dve.tensor_scalar(ss[:], ss[:], 1e-24, None, ALU.max).then_inc(clamped, 1)
                    shift(0)
                    shift(1)
                    if a:
                        dve.wait_ge(norms_ready, k + 1)
                        dve.wait_ge(rotated, k * 4 + 4)
                        for i in (2, 3, 0, 1):
                            r = rp[:, par, i, :].rearrange("p (h d) -> p h d", h=8)
                            dve.tensor_tensor(r, r, rn[:, 8 * i:8 * i + 8, None].to_broadcast([P, 8, LD]),
                                              ALU.mult).then_inc(normed, 1)

                pipeline(dve, step)
                add_y(NT - 1)

            @block.gpsimd
            def _(pool):
                def take_tokens(k, par):
                    for rows, late in ((slice(0, HALF), 0), (slice(HALF, P), 1)):
                        m = pool.tensor_copy(xs[rows, par, :], xa[rows, bass.ds(k * P + (PAD - WIN - late), KZ)])
                    m.then_inc(xs_ready, 1)

                def step(k, par, a, b, c_):
                    kb, pb, kc, pc = k - 1, 1 - par, k - 2, par
                    if b:
                        if isinstance(k, int) and k == 1:
                            pool.memset(kz[:, pb, :, 0:WIN], 0.0).then_inc(k_before, 1)
                        else:
                            pool.wait_ge(k_even_stored, kb * 2)
                            pool.wait_ge(k_odd_stored, kb * 2)
                            if since(k, 3):
                                pool.wait_ge(scored, kb * 2 - 2)
                            pool.tensor_tensor(kz[:, pb, :, 0:WIN], kz[:, par, :, P:KZ],
                                               c.v("k_before")[:, :, None].to_broadcast([P, LH, WIN]),
                                               ALU.mult).then_inc(k_before, 1)
                    if a:
                        def add_chunk(i):
                            pool.wait_ge(scaled_sin, k * 4 + (i + 1))
                            pool.wait_ge(scaled_cos, k * 4 + (i + 1))
                            pool.tensor_tensor(rp[:, par, i, :], rp[:, par, i, :], tm[:, i % 2, :],
                                               ALU.add).then_inc(rotated, 1)

                        for i in range(CH):
                            tab = lw.sin_q if i < 2 else lw.sin_k
                            pool.wait_ge(raw_ready, k * 4 + (i + 1))
                            if i >= 1:
                                add_chunk(i - 1)
                            for half in range(2):
                                t = tm[:, i % 2, :].rearrange("p (h e d) -> p h e d", h=8, e=2)[:, :, half, :]
                                r = raw[:, i, :].rearrange("p (h e d) -> p h e d", h=8, e=2)[:, :, 1 - half, :]
                                w = tab[:, bass.ds(k * LD + half * (LD // 2), LD // 2)][:, None, :]
                                m = pool.tensor_tensor(t, r, w.to_broadcast([P, 8, LD // 2]), ALU.mult)
                            m.then_inc(scaled_sin, 1)
                        add_chunk(CH - 1)
                        if since(k, 1):
                            pool.wait_ge(projected, k * 6)
                        pool.wait_ge(rotated, k * 4 + 4)
                        take_tokens(k + 1, 1 - par)
                        pool.wait_ge(xs_ready, k + 2)

                take_tokens(0, 0)
                pipeline(pool, step)


def local_ffn(nc, c, lw, xn, xb, xa, prefetch):
    with ExitStack() as ctx:
        def sb(name, shape):
            return ctx.enter_context(on_chip(nc.sbuf_tensor, name, shape, F32))

        gl = sb("lf_gl", [P, 2, GW])
        hd = sb("lf_h", [P, 2, 3, GW])
        ap = ctx.enter_context(on_chip(nc.psum_tensor, "lf_a", [P, 2, GW], F32))
        gp = ctx.enter_context(on_chip(nc.psum_tensor, "lf_g", [P, 2, GW], F32))
        yp = ctx.enter_context(on_chip(nc.psum_tensor, "lf_y", [P, 2, GW], F32))
        with phase(nc, "up", "gelu_done", "h_ready", "down", "added", "fetched",
                   "scaled_tables") as (
                block, up, gelu_done, h_ready, down, added, fetched, scaled_tables):
            @block.sync
            def _(sp):
                n = prefetch(sp, fetched)
                sp.wait_ge(fetched, 16 * n)

            @block.gpsimd
            def _(pool):
                pool.wait_ge(fetched, 16 * ATTENTION_LOADS)
                scale_tables(pool, lw, scaled_tables)

            @block.tensor
            def _(pe):
                def chunk(g, j):
                    n = 3 * g + j
                    m = FF_ROWS[j]
                    if n >= 2:
                        pe.wait_ge(h_ready, n - 1)
                    pe.matmul(gp[0:m, n % 2, :], lw.w1[:, FF + j * P:FF + j * P + m], xn[:, group(g)],
                              start=True, stop=True)
                    pe.matmul(ap[0:m, n % 2, :], lw.w1[:, j * P:j * P + m], xn[:, group(g)],
                              start=True, stop=True).then_inc(up, 1)

                def downs(g):
                    pe.wait_ge(h_ready, 3 * g + 3)
                    if g >= 2:
                        pe.wait_ge(added, g - 1)
                    for j in range(3):
                        m = pe.matmul(yp[:, g % 2, :], lw.w2[0:FF_ROWS[j], j, :], hd[0:FF_ROWS[j], g % 2, j, :],
                                      start=(j == 0), stop=(j == 2))
                    m.then_inc(down, 1)

                for g in range(NG):
                    for j in range(3):
                        chunk(g, j)
                        if j == 1 and g:
                            downs(g - 1)
                downs(NG - 1)

            @block.scalar
            def _(act):
                for n in range(3 * NG):
                    j, m = n % 3, FF_ROWS[n % 3]
                    act.wait_ge(up, n + 1)
                    if n >= 2:
                        act.wait_ge(h_ready, n - 1)
                    act.activation(gl[0:m, n % 2, :], gp[0:m, n % 2, :], ACT.Gelu,
                                   bias=lw.vec[0:m, 3 + j:4 + j]).then_inc(gelu_done, 1)

            @block.vector
            def _(dve):
                def add_y(g):
                    dve.wait_ge(down, g + 1)
                    dve.scalar_tensor_tensor(out=xa[:, PAD + g * GW:PAD + (g + 1) * GW], in0=yp[:, g % 2, :],
                                             scalar=lw.vec[:, 6:7], in1=xb[:, PAD + g * GW:PAD + (g + 1) * GW],
                                             op0=ALU.add, op1=ALU.add).then_inc(added, 1)

                for g in range(NG):
                    for j in range(3):
                        n, m = 3 * g + j, FF_ROWS[j]
                        dve.wait_ge(gelu_done, n + 1)
                        if g >= 2:
                            dve.wait_ge(down, g - 1)
                        dve.scalar_tensor_tensor(out=hd[0:m, g % 2, j, :], in0=ap[0:m, n % 2, :],
                                                 scalar=lw.vec[0:m, j:j + 1], in1=gl[0:m, n % 2, :],
                                                 op0=ALU.add, op1=ALU.mult).then_inc(h_ready, 1)
                    if g:
                        add_y(g - 1)
                add_y(NG - 1)


def project_qk(nc, c, kind, w, xn, qk):
    n = 2 * NG
    scale = float(1 / np.sqrt(np.float32(DH)))
    with ExitStack() as ctx:
        def sb(name, shape):
            return ctx.enter_context(on_chip(nc.sbuf_tensor, name, shape, F32))

        t1 = sb("qk_t1", [P, 2, GW])
        t2 = sb("qk_t2", [P, 2, GW])
        t3 = sb("qk_t3", [P, 2, GW])
        t4 = sb("qk_t4", [P, 2, GW])
        own = ctx.enter_context(on_chip(nc.psum_tensor, "qk_own", [P, 2, GW], F32))
        other = ctx.enter_context(on_chip(nc.psum_tensor, "qk_other", [P, 2, GW], F32))
        sums = ctx.enter_context(on_chip(nc.psum_tensor, "qk_sums", [P, 2, GW], F32))
        with phase(nc, "projected", "step", "done", "squared", "summed", "clamped", "logged", "norm_ready") as (
                block, projected, step, done, squared, summed, clamped, logged, norm_ready):
            @block.tensor
            def _(pe):
                for u in range(n):
                    x, g = divmod(u, NG)
                    if u >= 2:
                        pe.wait_ge(done, u - 1)
                    m = pe.matmul(own[:, u % 2, :], w[:, x * P:(x + 1) * P], xn[:, group(g)], start=True, stop=True)
                    if kind != "plain":
                        m = pe.matmul(other[:, u % 2, :], w[:, (2 + x) * P:(3 + x) * P], xn[:, group(g)],
                                      start=True, stop=True)
                    m.then_inc(projected, 1)
                    if kind == "channel":
                        pe.wait_ge(squared, u + 1)
                        pe.matmul(sums[:, u % 2, :], c.head_ones[:], t2[:, u % 2, :], start=True,
                                  stop=True).then_inc(summed, 1)

            @block.scalar
            def _(act):
                if kind != "channel":
                    return
                act.preload_act_table_set("natural_log_exp_and_others")
                for u in range(n):
                    act.wait_ge(step, 2 * u + 2)
                    act.activation(t2[:, u % 2, :], qk[:, u // NG, group(u % NG)], ACT.Square).then_inc(squared, 1)
                    act.wait_ge(clamped, u + 1)
                    act.activation(t3[:, u % 2, :], t3[:, u % 2, :], ACT.Ln, scale=float(2 ** 20)).then_inc(logged, 1)
                    act.wait_ge(logged, u + 1)
                    act.activation(t4[:, u % 2, :], t3[:, u % 2, :], ACT.Exp, scale=-0.5,
                                   bias=c.v("ten_ln2")).then_inc(norm_ready, 1)

            @block.vector
            def _(dve):
                for u in range(n):
                    x, g = divmod(u, NG)
                    to = qk[:, x, group(g)]
                    dve.wait_ge(projected, u + 1)
                    if kind == "plain":
                        dve.tensor_scalar(to, own[:, u % 2, :], scale if x == 0 else 1.0, None,
                                          ALU.mult).then_inc(done, 1)
                        continue
                    if kind == "channel":
                        dve.tensor_scalar(t1[:, u % 2, :], other[:, u % 2, :], c.v("ch_sin"), None,
                                          ALU.mult).then_inc(step, 1)
                        dve.wait_ge(step, 2 * u + 1)
                        dve.scalar_tensor_tensor(out=to, in0=own[:, u % 2, :], scalar=c.v("ch_cos"),
                                                 in1=t1[:, u % 2, :], op0=ALU.mult, op1=ALU.add).then_inc(step, 1)
                        dve.wait_ge(summed, u + 1)
                        dve.tensor_scalar(t3[:, u % 2, :], sums[:, u % 2, :], 1e-24, None,
                                          ALU.max).then_inc(clamped, 1)
                        dve.wait_ge(norm_ready, u + 1)
                        dve.scalar_tensor_tensor(out=to, in0=to, scalar=c.qkscale[:, 0:1] if x == 0 else 1.0,
                                                 in1=t4[:, u % 2, :], op0=ALU.mult, op1=ALU.mult).then_inc(done, 1)
                        continue
                    dve.tensor_tensor(t1[:, u % 2, :], own[:, u % 2, :], c.rope_cos[:, group(g)], ALU.mult).then_inc(step, 1)
                    dve.tensor_tensor(t2[:, u % 2, :], other[:, u % 2, :], c.rope_sin[:, group(g)], ALU.mult).then_inc(step, 1)
                    dve.wait_ge(step, 3 * u + 2)
                    dve.tensor_tensor(t3[:, u % 2, :], t1[:, u % 2, :], t2[:, u % 2, :], ALU.add).then_inc(step, 1)
                    dve.wait_ge(step, 3 * u + 3)
                    dve.tensor_scalar(to, t3[:, u % 2, :], scale if x == 0 else 1.0, None, ALU.mult).then_inc(done, 1)


def add_into(nc, x, y):
    with phase(nc, "added") as (block, added):
        @block.vector
        def _(dve):
            dve.tensor_tensor(x, x, y, ALU.add).then_inc(added, 1)
            dve.wait_ge(added, 1)


class Names:
    pass


VECTORS = ["a_ln1_s", "a_ln1_b", "a_ln2_s", "a_ln2_b", "a_b1", "a_b1_1", "a_b1_2", "a_b1_3", "a_b2",
           "b_g", "b_b", "c_g", "c_b"]
SHAPE_VECTORS = ["eps5", "eps6", "ten_ln2", "k_before", "ch_sin", "ch_cos"]


def build(nc, io, out, part):
    root = ExitStack()
    with root:
        c = Names()

        def keep(name, shape, dt=F32, ctx=root):
            return ctx.enter_context(on_chip(nc.sbuf_tensor, name, shape, dt))

        x = keep("x", [P, T])
        c.ident = keep("ident", [P, P])
        c.ident_b = keep("ident_b", [P, P], BF16)
        c.flip_b = keep("flip_b", [P, P], BF16)
        c.mean_w = keep("mean_w", [P, P])
        c.vecs = keep("vecs", [P, len(VECTORS)])
        c.svecs = keep("svecs", [P, len(SHAPE_VECTORS)])

        def v(name, j=0):
            if name in VECTORS:
                i = VECTORS.index(name) + j
                return c.vecs[:, i:i + 1]
            i = SHAPE_VECTORS.index(name)
            return c.svecs[:, i:i + 1]

        c.v = v
        load_constants(nc, [(x[:], io["tokens"]), (c.ident[:], io["c_ident"]), (c.ident_b[:], io["c_ident_b"]), (c.flip_b[:], io["c_flip_b"]),
                            (c.mean_w[:], io["c_mean"]), (c.vecs[:], io["vecs"]), (c.svecs[:], io["c_svecs"])])

        def performer_layer():
            with ExitStack() as ctx:
                u = keep("s1_u", [P, T], ctx=ctx)
                layer_norm(nc, c, x, u, v("eps5"))
                n = keep("s1_n", [P, T], ctx=ctx)
                layer_norm(nc, c, u, n, v("eps6"), v("a_ln1_s"), v("a_ln1_b"))
                w = Names()
                at = keep("s1_at", [P, T], ctx=ctx)
                w.wo = keep("s1_wo", [P, P], ctx=ctx)
                with ExitStack() as ctx2:
                    ot = keep("s1_ot", [P, QUADS, T], ctx=ctx2)
                    w.pq = keep("s1_wq", [P, P], ctx=ctx2)
                    w.pkv = keep("s1_wkv", [P, 2 * P], ctx=ctx2)
                    c.causal = keep("causal", [P, P], ctx=ctx2)
                    c.head_mask = keep("head_mask", [P, H], ctx=ctx2)
                    c.block_mask = keep("block_mask", [P, H * 32], ctx=ctx2)
                    load_constants(nc, [(w.pq[:], io["a_wq"]), (w.pkv[:], io["a_wkv"]), (w.wo[:], io["a_wo"]),
                                        (c.causal[:], io["c_causal"]), (c.head_mask[:], io["c_head_mask"]),
                                        (c.block_mask[:], io["c_block_mask"])])
                    performer(nc, c, w, n, ot)
                    normalise_heads(nc, c, ot, at)
                project_add(nc, w.wo, at, u, [u])
                layer_norm(nc, c, u, n, v("eps6"), v("a_ln2_s"), v("a_ln2_b"))
                w.w1 = keep("s1_w1", [P, 4 * P], ctx=ctx)
                w.w2 = keep("s1_w2", [P, 4, P], ctx=ctx)
                load_constants(nc, [(w.w1[:], io["a_w1"]), (w.w2[:], io["a_w2"])])
                gelu_mlp(nc, c, w, n, u, x)

        def mixture():
            with ExitStack() as ctx:
                u = keep("s2_u", [P, T], ctx=ctx)
                w = Names()
                w.router = keep("s2_router", [P, E], ctx=ctx)
                w.wg = keep("s2_wg", [P, 4 * P], ctx=ctx)
                w.wu = keep("s2_wu", [P, 4 * P], ctx=ctx)
                w.wd = keep("s2_wd", [P, 4, P], ctx=ctx)
                w.wgs = keep("s2_wgs", [P, P], ctx=ctx)
                w.wus = keep("s2_wus", [P, P], ctx=ctx)
                w.wds = keep("s2_wds", [P, P], ctx=ctx)
                c.sel = keep("s2_sel", [E, 4, P], ctx=ctx)
                c.iota = keep("s2_iota", [P, E], ctx=ctx)
                load_constants(nc, [(w.router[:], io["m_router"]), (w.wg[:], io["m_wg"]), (w.wu[:], io["m_wu"]),
                                    (w.wd[:], io["m_wd"]), (w.wgs[:], io["m_wgs"]), (w.wus[:], io["m_wus"]),
                                    (w.wds[:], io["m_wds"]), (c.sel[:], io["c_sel"]), (c.iota[:], io["c_iota"])])
                layer_norm(nc, c, x, u, v("eps5"))
                experts(nc, c, w, u, x)

        def attention(kind, gamma, beta, w_qk, w_v, w_o, residual):
            with ExitStack() as ctx:
                u = keep("s3_u", [P, T], ctx=ctx)
                layer_norm(nc, c, x, u, v("eps5"))
                wv = keep("s3_wv", [P, P], ctx=ctx)
                wo = keep("s3_wo", [P, P], ctx=ctx)
                vv = keep("s3_v", [P, NT, 176], ctx=ctx)
                with ExitStack() as ctx2:
                    xn = u
                    if gamma is not None:
                        xn = keep("s3_n", [P, T], ctx=ctx2)
                        layer_norm(nc, c, u, xn, v("eps5"), gamma, beta)
                    qk = keep("s3_qk", [P, 2, T], ctx=ctx2)
                    cols = io[w_qk].shape[1]
                    wqk = keep("s3_wqk", [P, cols], ctx=ctx2)
                    loads = [(wqk[:], io[w_qk]), (wv[:], io[w_v]), (wo[:], io[w_o])]
                    if kind == "channel":
                        c.head_ones = keep("head_ones", [P, P], ctx=ctx2)
                        c.qkscale = keep("qkscale", [P, 1], ctx=ctx2)
                        loads += [(c.head_ones[:], io["c_head_ones"]),
                                  (c.qkscale[:], io["c_scale"])]
                    if kind == "position":
                        c.rope_cos = keep("rope_cos", [P, T], ctx=ctx2)
                        c.rope_sin = keep("rope_sin", [P, T], ctx=ctx2)
                        loads += [(c.rope_cos[:], io["c_rope_cos"]), (c.rope_sin[:], io["c_rope_sin"])]
                    load_constants(nc, loads)
                    project_qk(nc, c, kind, wqk, xn, qk)
                    values(nc, wv, xn, vv)
                    split_parts(nc, qk[:, 0, :], io["s_q"])
                    split_parts(nc, qk[:, 1, :], io["s_k"])
                if kind == "plain":
                    near_tables(nc, c, io)
                with ExitStack() as ctx2:
                    ot = keep("s3_ot", [P, QUADS, T], ctx=ctx2)
                    with ExitStack() as ctx3:
                        if kind != "plain":
                            c.mask_a = keep("mask_a", [P, P], BF16, ctx=ctx3)
                            c.mask_b = keep("mask_b", [P, P], BF16, ctx=ctx3)
                            load_constants(nc, [(c.mask_a[:], io["c_mask_a"]), (c.mask_b[:], io["c_mask_b"])])
                        causal_attention(nc, c, io, vv, ot, kind == "plain")
                    at = keep("s3_at", [P, T], ctx=ctx2)
                    normalise_heads(nc, c, ot, at)
                    project_add(nc, wo, at, x, [x, u] if residual else [x])

        def local_layers():
            with ExitStack() as ctx:
                wide = PAD + T + P
                xa = keep("l_xa", [P, wide], ctx=ctx)
                xb = keep("l_xb", [P, wide], ctx=ctx)
                layer_norm(nc, c, x, xb[:, PAD:PAD + T], v("eps5"))
                lw = Names()
                lw.qkv = keep("l_qkv", [P, 3 * INNER], ctx=ctx)
                lw.wo = keep("l_wo", [P, LH // 2, P], ctx=ctx)
                lw.w1 = keep("l_w1", [P, 2 * FF], ctx=ctx)
                lw.w2 = keep("l_w2", [P, 3, P], ctx=ctx)
                lw.vec = keep("l_vec", [P, 9], ctx=ctx)
                lw.tables = keep("l_tables", [P, 4, NT * LD], ctx=ctx)
                lw.cos_q, lw.sin_q, lw.cos_k, lw.sin_k = (lw.tables[:, i, :] for i in range(4))
                lw.qk_scale = keep("l_qk_scale", [P, 4, LD], ctx=ctx)
                c.local_mask = keep("local_mask", [P, 4 * KEYS], BF16, ctx=ctx)
                c.local_first = keep("local_first", [P, 4 * KEYS], BF16, ctx=ctx)

                def fetch(pairs):
                    def start(sp, sem):
                        for dst, src in pairs:
                            sp.dma_start(dst, src).then_inc(sem, 16)
                        return len(pairs)
                    return start

                load_constants(nc, [(c.local_mask[:], io["c_local_mask"]), (c.local_first[:], io["c_local_first"])]
                               + attention_weights_at(io, lw, 0))
                kz = keep("l_kz", [P, 2, LH, KZ], ctx=ctx)
                vx = keep("l_vx", [KEYS, 2, 2, LH, KEYS], ctx=ctx)
                with phase(nc, "copied", "cleared", "scaled_tables") as (block, copied, cleared, scaled_tables):
                    @block.gpsimd
                    def _(pool):
                        scale_tables(pool, lw, scaled_tables)
                        pool.memset(kz[:], 0.0).then_inc(cleared, 1)
                        for b in (xa, xb):
                            pool.memset(b[:, 0:PAD], 0.0).then_inc(cleared, 1)
                            pool.memset(b[:, PAD + T:], 0.0).then_inc(cleared, 1)

                    @block.vector
                    def _(dve):
                        dve.tensor_copy(xa[:, PAD:PAD + T], xb[:, PAD:PAD + T]).then_inc(copied, 1)
                        dve.memset(vx[:], 1.0).then_inc(copied, 1)
                with nc.Fori(0, LAYERS) as layer:
                    local_attention(nc, c, lw, xa, xb, kz, vx, fetch(ffn_weights_at(io, lw, layer)))
                    with ExitStack() as ctx2:
                        xs = keep("l_xs", [P, T], ctx=ctx2)
                        xn = keep("l_xn", [P, T], ctx=ctx2)
                        layer_norm(nc, c, xs, xn, v("eps5"), lw.vec[:, 7:8], lw.vec[:, 8:9], shift_from=xb)
                        local_ffn(nc, c, lw, xn, xb, xa, fetch(attention_weights_at(io, lw, layer + 1)))
                add_into(nc, x[:], xa[:, PAD:PAD + T])

        stages = [
            performer_layer,
            mixture,
            lambda: attention("plain", v("b_g"), v("b_b"), "b_wqk", "b_wv", "b_wo", True),
            mixture,
            lambda: attention("channel", v("c_g"), v("c_b"), "c_wqk", "c_wv", "c_wo", False),
            local_layers,
            lambda: attention("position", None, None, "d_wqk", "d_wv", "d_wo", False),
            local_layers,
        ]
        for stage in stages[part]:
            stage()

        with phase(nc, "stored") as (block, stored):
            @block.sync
            def _(sp):
                sp.dma_start(out, x[:]).then_inc(stored, 16)
                sp.wait_ge(stored, 16)


def layer_of(a, layer):
    return a[bass.ds(layer, 1)].rearrange("o p n -> (o p) n")


ATTENTION_LOADS = 4


def attention_weights_at(io, lw, layer):
    return [(lw.qkv[:], layer_of(io["l_qkv"], layer)),
            (lw.wo[:].rearrange("p a d -> p (a d)"), layer_of(io["l_wo"], layer)),
            (lw.tables[:].rearrange("p a d -> p (a d)"), io["c_tables"]),
            (lw.qk_scale[:].rearrange("p a d -> p (a d)"), layer_of(io["l_qk_scale"], layer))]


def ffn_weights_at(io, lw, layer):
    return [(lw.w1[:], layer_of(io["l_w1"], layer)),
            (lw.w2[:].rearrange("p a d -> p (a d)"), layer_of(io["l_w2"], layer)),
            (lw.vec[:], layer_of(io["l_vec"], layer))]


def shape_constants():
    bf = mybir.dt.np(BF16)
    f = np.float32
    i = np.arange(P)
    k = {}
    k["c_ident"] = np.eye(P, dtype=f)
    k["c_ident_b"] = np.eye(P).astype(bf)
    k["c_flip_b"] = np.eye(P)[::-1].astype(bf)
    k["c_mean"] = np.full((P, P), 1 / P, f)
    k["c_causal"] = (i[:, None] <= i[None, :]).astype(f)
    k["c_head_mask"] = (i[:, None] // DH == np.arange(H)[None, :]).astype(f)
    k["c_block_mask"] = (i[:, None] // DH == np.arange(H * 32)[None, :] // 32).astype(f)
    k["c_head_ones"] = (i[:, None] // DH == i[None, :] // DH).astype(f)
    k["c_mask_a"] = np.where(i[None, :] > i[:, None], NEG, 0).astype(bf)
    k["c_mask_b"] = np.where(i[:, None] > i[None, :], NEG, 0).astype(bf)
    k["c_zero"] = np.zeros((3, 4 * T), bf)
    k["c_sel"] = (np.arange(E)[:, None] == np.arange(4 * P)[None, :] // (P // 4)).astype(f)
    k["c_iota"] = np.tile(np.arange(E, dtype=f), (P, 1))
    q, key = np.arange(P) % HALF, np.arange(KEYS)
    seen = (q[:, None] <= key[None, :]) & (key[None, :] <= q[:, None] + WIN)
    first = seen & ((key[None, :] >= WIN) | (i[:, None] >= HALF))
    k["c_local_mask"] = np.tile(np.where(seen, 0, NEG), (1, 4)).astype(bf)
    k["c_local_first"] = np.tile(np.where(first, 0, NEG), (1, 4)).astype(bf)
    inv = f(10000.0) ** (np.arange(0, DH, 2, dtype=f) / f(DH))
    ang = (np.arange(T, dtype=f)[:, None] / inv[None, :]).astype(f)
    cos, sin = np.cos(ang).astype(f), np.sin(ang).astype(f)
    pair = (i % DH) // 2
    k["c_rope_cos"] = np.ascontiguousarray(cos[:, pair].T)
    k["c_rope_sin"] = np.ascontiguousarray((sin[:, pair] * np.where(i % 2 == 0, -1, 1)[None, :]).T.astype(f))
    freq = np.repeat(f(10000.0) ** (-(np.arange(0, P, 2, dtype=f) / f(P))), 2).astype(f)
    ch = (f(T) * freq).astype(f)
    half = np.arange(0, LD, 2, dtype=f)
    freqs = (np.arange(T, dtype=f)[:, None] * (f(1) / f(10000.0) ** (half / f(LD)))[None, :]).astype(f)
    base = ((half.astype(np.float64) + 0.4 * LD) / (1.4 * LD))
    grow = base[None, :] ** ((np.arange(T) % P)[:, None] / (WIN // 2))
    cos, sin = np.cos(freqs).astype(np.float64), np.sin(freqs).astype(np.float64)
    tables = []
    for g in (8.0 * grow, 1 / grow):
        tables += [np.concatenate([cos * g, cos * g], -1), np.concatenate([-sin * g, sin * g], -1)]
    k["c_tables"] = np.ascontiguousarray(
        np.stack(tables).reshape(4, NT, P, LD).transpose(2, 0, 1, 3).reshape(P, 4 * NT * LD).astype(f))
    cols = {
        "eps5": np.full(P, 1e-5), "eps6": np.full(P, 1e-6), "ten_ln2": np.full(P, 10 * np.log(2)),
        "k_before": np.tile(base ** (P // (WIN // 2)), 4),
        "ch_sin": np.sin(ch) * np.where(i < P // 2, -1, 1), "ch_cos": np.cos(ch),
    }
    k["c_svecs"] = np.stack([cols[n] for n in SHAPE_VECTORS], 1).astype(f)
    return k


def lay_out(a):
    r = {n: np.asarray(x) for n, x in a.items()}
    m = {}
    m["tokens"] = r["L0_attn_a_inputs"][0].T
    b1 = r["L0_attn_a_b1"].reshape(4, P)
    m["vecs"] = np.stack([r["L0_attn_a_ln1_scale"], r["L0_attn_a_ln1_bias"], r["L0_attn_a_ln2_scale"],
                          r["L0_attn_a_ln2_bias"], *b1, r["L0_attn_a_b2"], r["L0_attn_b_ln_gamma"],
                          r["L0_attn_b_ln_beta"], r["L1_attn_a_ln_gamma"], r["L1_attn_a_ln_beta"]], 1)
    m["a_wq"] = r["L0_attn_a_wq"].reshape(P, P)
    m["a_wkv"] = np.concatenate([r["L0_attn_a_wk"].reshape(P, P), r["L0_attn_a_wv"].reshape(P, P)], 1)
    m["a_wo"] = r["L0_attn_a_wo"].reshape(P, P)
    m["a_w1"] = r["L0_attn_a_w1"]
    m["a_w2"] = r["L0_attn_a_w2"].reshape(4, P, P).transpose(1, 0, 2)
    m["m_router"] = r["L0_ffn_router_w"]
    m["m_wg"] = r["L0_ffn_wg_r"].transpose(1, 0, 2).reshape(P, 4 * P)
    m["m_wu"] = r["L0_ffn_wu_r"].transpose(1, 0, 2).reshape(P, 4 * P)
    m["m_wd"] = r["L0_ffn_wd_r"].reshape(4, P, P).transpose(1, 0, 2)
    m["m_wgs"] = r["L0_ffn_wg_s"].transpose(1, 0, 2).reshape(P, P)
    m["m_wus"] = r["L0_ffn_wu_s"].transpose(1, 0, 2).reshape(P, P)
    m["m_wds"] = r["L0_ffn_wd_s"].reshape(P, P)
    m["b_wqk"] = np.concatenate([r["L0_attn_b_Wq"].T, r["L0_attn_b_Wk"].T], 1)
    m["b_wv"] = r["L0_attn_b_Wv"].T
    m["b_wo"] = r["L0_attn_b_Wo"].T
    m["rel"] = np.stack([r["L0_attn_b_rel"], r["L0_attn_b_rel"][:, ::-1]], 1)
    w = r["L1_attn_a_w_qkv"]
    partner = np.concatenate([np.arange(1, P, 2), np.arange(0, P, 2)])
    m["c_wqk"] = np.concatenate([w[:, 0:P], w[:, P:2 * P], w[:, 0:P][:, partner], w[:, P:2 * P][:, partner]], 1)
    m["c_wv"] = w[:, 2 * P:]
    m["c_wo"] = r["L1_attn_a_w_out"]
    m["c_scale"] = np.broadcast_to(r["L1_attn_a_qkscale"].reshape(1, 1), (P, 1))
    w = r["L1_attn_b_W_qkv"].T
    partner = np.arange(P) ^ 1
    m["d_wqk"] = np.concatenate([w[:, 0:P], w[:, P:2 * P], w[:, 0:P][:, partner], w[:, P:2 * P][:, partner]], 1)
    m["d_wv"] = w[:, 2 * P:]
    m["d_wo"] = r["L1_attn_b_W_o"].T

    def again(x):
        return np.concatenate([x, x[:1]])

    m["l_qkv"] = again(r["L1_ffn_Wqkv"])
    m["l_wo"] = again(r["L1_ffn_Wo"].reshape(LAYERS, LH // 2, P, P).transpose(0, 2, 1, 3).reshape(LAYERS, P, INNER))
    qs, ks = r["L1_ffn_q_scale"], r["L1_ffn_k_scale"]

    def swap(s):
        return np.concatenate([s[:, LD // 2:], s[:, :LD // 2]], 1)

    scales = np.stack([qs, swap(qs), ks, swap(ks)], 1).reshape(LAYERS, 1, 4 * LD)
    m["l_qk_scale"] = again(np.broadcast_to(scales, (LAYERS, P, 4 * LD)))
    m["l_w1"] = again(r["L1_ffn_W1"])
    w2 = np.zeros((LAYERS, 3 * P, P), np.float32)
    w2[:, :FF] = r["L1_ffn_W2"]
    m["l_w2"] = again(w2.reshape(LAYERS, 3, P, P).transpose(0, 2, 1, 3).reshape(LAYERS, P, 3 * P))
    b = np.zeros((LAYERS, 6, P), np.float32)
    for half in range(2):
        part = np.zeros((LAYERS, 3 * P), np.float32)
        part[:, :FF] = r["L1_ffn_b1"][:, half * FF:(half + 1) * FF]
        b[:, 3 * half:3 * half + 3] = part.reshape(LAYERS, 3, P)
    vec = np.concatenate([b, r["L1_ffn_b2"][:, None], r["L1_ffn_ln_g"][:, None], r["L1_ffn_ln_b"][:, None]], 1)
    m["l_vec"] = again(vec.transpose(0, 2, 1))
    return {n: np.ascontiguousarray(x) for n, x in m.items()}


def program(nc, arrays, part=slice(None)):
    io = {}
    for name, a in arrays.items():
        io[name] = nc.dram_tensor(name, a.shape, mybir.dt.from_np(a.dtype), kind="ExternalInput").ap()
    io["s_q"] = nc.dram_tensor("s_q", (3, P, T), BF16, kind="Internal").ap()
    io["s_k"] = nc.dram_tensor("s_k", (3, P, T), BF16, kind="Internal").ap()
    io["s_ext"] = nc.dram_tensor("s_ext", (3, H, 2, 3 * P), BF16, kind="Internal").ap()
    out = nc.dram_tensor("out", (P, T), F32, kind="ExternalOutput").ap()
    build(nc, io, out, part)


def kernel(**inputs):
    import concourse.bacc as bacc
    from concourse.bass_utils import run_bass_kernel_spmd

    nc = bacc.Bacc("TRN2", target_bir_lowering=False, num_devices=1)
    arrays = {**lay_out(inputs), **shape_constants()}
    program(nc, arrays)
    r = run_bass_kernel_spmd(nc, [arrays], core_ids=[0])
    return np.ascontiguousarray(r.results[0]["out"].T)[None]
```
